# Optimizing a Trainium2 kernel written in Bass

```python
import numpy as np
import jax
import jax.numpy as jnp

def _softmax(x, axis=-1):
    return jax.nn.softmax(x, axis=axis)

def _gelu(x):
    return jax.nn.gelu(x, approximate=True)

def _silu(x):
    return jax.nn.silu(x)

def _sigmoid(x):
    return jax.nn.sigmoid(x)

def _layernorm(x, axis=-1, eps=1e-05):
    m = jnp.mean(x, axis=axis, keepdims=True)
    v = jnp.var(x, axis=axis, keepdims=True)
    return (x - m) / jnp.sqrt(v + eps)

def _scatter_add(tgt, idx, src, axis=0):
    return tgt.at[idx].add(src)

def _segment_sum(src, seg, n):
    return jax.ops.segment_sum(src, seg, n)
kernel_name = 'mk_xattn_ffn_d4_seqx_r4_af0913'

def setup_inputs(seed: int=0):
    np.random.seed(seed)
    _w = jnp.asarray

    def _rec_inputs():
        import jax
        import jax.numpy as jnp
        _rk = jax.random.key(seed)
        x = 4.136e-05 + 0.9999 * jax.random.normal(jax.random.fold_in(_rk, 1), (4, 512, 512), jnp.float32)
        _lenS = 512 - jax.random.randint(jax.random.fold_in(_rk, 7), (4,), 0, max(1, 512 // 4) + 1, jnp.int32)
        _lenS2 = 512 - jax.random.randint(jax.random.fold_in(_rk, 8), (4,), 0, max(1, 512 // 4) + 1, jnp.int32)
        _ctx_1024P = jax.random.normal(jax.random.fold_in(_rk, 11), (4, 16, 256), jnp.float32)
        _ctx_1024c = jax.random.dirichlet(jax.random.fold_in(_rk, 511), 0.3 * jnp.ones((16,), jnp.float32), (4, 512))
        _ctx_1024t = jnp.einsum('bsk,bkd->bsd', _ctx_1024c, _ctx_1024P)
        _ctx_1024t = _ctx_1024t * jax.lax.rsqrt(jnp.mean(jnp.square(_ctx_1024t)) + 1e-12) * 0.953939
        ctx_1024 = -0.000292821 + 1.00034 * (_ctx_1024t + 0.3 * jax.random.normal(jax.random.fold_in(_rk, 611), (4, 512, 256), jnp.float32))
        return (x, ctx_1024)
    x, ctx_1024 = _rec_inputs()

    def _L0_xattn_setup():
        import jax, jax.numpy as jnp
        import numpy as np
        import math
        B, L, DM = (2, 512, 256)
        DS, DC, EXP = (16, 4, 2)
        DI = EXP * DM
        DR = math.ceil(DM / 16)
        DT_MIN, DT_MAX, DT_FLOOR = (0.001, 0.1, 0.0001)

        def _ssm_forward(hidden_states, z, in_proj_w, conv_w, conv_b, x_proj_w, dt_proj_w, dt_proj_b, A_log, D):
            b = hidden_states.shape[0]
            x = jnp.einsum('ed,bld->bel', in_proj_w, hidden_states)
            xp = jnp.pad(x, ((0, 0), (0, 0), (DC - 1, 0)))
            xc = jax.lax.conv_general_dilated(xp, conv_w[:, None, :], window_strides=(1,), padding='VALID', dimension_numbers=('NCH', 'OIH', 'NCH'), feature_group_count=DI)
            u = jax.nn.silu(xc + conv_b[None, :, None])
            x_dbl = jnp.einsum('ke,bel->bkl', x_proj_w, u)
            dt_lo = x_dbl[:, :DR]
            Bm = x_dbl[:, DR:DR + DS]
            Cm = x_dbl[:, DR + DS:]
            delta = jax.nn.softplus(jnp.einsum('er,brl->bel', dt_proj_w, dt_lo) + dt_proj_b[None, :, None])
            A = -jnp.exp(A_log)

            def step(state, xs):
                d_t, B_t, C_t, u_t = xs
                dA = jnp.exp(d_t[..., None] * A)
                state = state * dA + (d_t * u_t)[..., None] * B_t[:, None, :]
                y_t = jnp.einsum('ben,bn->be', state, C_t)
                return (state, y_t)
            xs = (jnp.moveaxis(delta, -1, 0), jnp.moveaxis(Bm, -1, 0), jnp.moveaxis(Cm, -1, 0), jnp.moveaxis(u, -1, 0))
            state0 = jnp.zeros((b, DI, DS), delta.dtype)
            _, ys = jax.lax.scan(step, state0, xs)
            y = jnp.moveaxis(ys, 0, -1)
            y = y + D[None, :, None] * u
            y = y * jax.nn.silu(z)
            return jnp.swapaxes(y, 1, 2)
        key = jax.random.key(seed)
        ks = jax.random.split(key, 8)
        hidden_states = jax.random.normal(ks[0], (B, L, DM), jnp.float32)
        z = jax.random.normal(ks[1], (B, DI, L), jnp.float32)
        in_proj_w = jax.random.normal(ks[2], (DI, DM), jnp.float32) * DM ** (-0.5)
        conv_w = jax.random.normal(ks[3], (DI, DC), jnp.float32) * DC ** (-0.5)
        conv_b = jnp.zeros((DI,), jnp.float32)
        x_proj_w = jax.random.normal(ks[4], (DR + 2 * DS, DI), jnp.float32) * DI ** (-0.5)
        dt_std = DR ** (-0.5)
        dt_proj_w = jax.random.uniform(ks[5], (DI, DR), jnp.float32, -dt_std, dt_std)
        dt = jnp.exp(jax.random.uniform(ks[6], (DI,), jnp.float32) * (math.log(DT_MAX) - math.log(DT_MIN)) + math.log(DT_MIN))
        dt = jnp.clip(dt, DT_FLOOR)
        dt_proj_b = dt + jnp.log(-jnp.expm1(-dt))
        A_log = jnp.log(jnp.broadcast_to(jnp.arange(1, DS + 1, dtype=jnp.float32), (DI, DS)))
        D = jnp.ones((DI,), jnp.float32)
        return dict(hidden_states=hidden_states, z=z, in_proj_w=in_proj_w, conv_w=conv_w, conv_b=conv_b, x_proj_w=x_proj_w, dt_proj_w=dt_proj_w, dt_proj_b=dt_proj_b, A_log=A_log, D=D)
    _L0_xattn_all = _L0_xattn_setup()
    _L0_xattn_in = {k: v for k, v in _L0_xattn_all.items() if k in ('in_proj_w', 'conv_w', 'conv_b', 'x_proj_w', 'dt_proj_w', 'dt_proj_b', 'A_log', 'D')}
    del _L0_xattn_all

    def _L0_ffn_setup():
        import jax, jax.numpy as jnp
        import numpy as np
        H = 512
        I = 256
        E = 32
        K = 4
        N_SHARED = 1
        EPS = 1e-06

        def _rmsnorm(x, w, eps=EPS):
            var = jnp.mean(jnp.square(x), axis=-1, keepdims=True)
            return x * jax.lax.rsqrt(var + eps) * w

        def _moe_core(x, gate_w, w13, w2):
            T = x.shape[0]
            N = T * K
            C = 2 * N // E
            logits = jnp.einsum('th,eh->te', x.astype(jnp.float32), gate_w.astype(jnp.float32))
            scores = jax.nn.softmax(logits, axis=-1)
            topk_w, topk_ids = jax.lax.top_k(scores, K)
            topk_w = topk_w / jnp.sum(topk_w, axis=-1, keepdims=True)
            flat_ids = topk_ids.reshape(-1)
            flat_w = topk_w.reshape(-1)
            order = jnp.argsort(flat_ids)
            sorted_eid = flat_ids[order]
            tok = order // K
            counts = jnp.zeros((E,), jnp.int32).at[flat_ids].add(1)
            starts = jnp.cumsum(counts) - counts
            pos = jnp.arange(N) - starts[sorted_eid]
            buf = jnp.zeros((E, C, x.shape[1]), x.dtype).at[sorted_eid, pos].set(x[tok], mode='drop')
            gu = jnp.einsum('ech,ehf->ecf', buf, w13)
            g, u = jnp.split(gu, 2, axis=-1)
            act = jax.nn.silu(g) * u
            eo = jnp.einsum('eci,eih->ech', act, w2)
            out_slots = eo[sorted_eid, pos]
            routed = jnp.zeros_like(x).at[tok].add(out_slots * flat_w[order][:, None])
            return routed
        key = jax.random.key(seed)
        ks = jax.random.split(key, 8)
        s = 1.0 / np.sqrt(H)
        si = 1.0 / np.sqrt(I)
        return {'hidden_states': jax.random.normal(ks[0], (1, 1024, H), jnp.float32), 'norm_w': jnp.ones((H,), jnp.float32), 'gate_w': jax.random.normal(ks[1], (E, H), jnp.float32) * s, 'w13': jax.random.normal(ks[2], (E, H, 2 * I), jnp.float32) * s, 'w2': jax.random.normal(ks[3], (E, I, H), jnp.float32) * si, 'shared_gate_w': jax.random.normal(ks[4], (H, I * N_SHARED), jnp.float32) * s, 'shared_up_w': jax.random.normal(ks[5], (H, I * N_SHARED), jnp.float32) * s, 'shared_down_w': jax.random.normal(ks[6], (I * N_SHARED, H), jnp.float32) * si}
    _L0_ffn_all = _L0_ffn_setup()
    _L0_ffn_in = {k: v for k, v in _L0_ffn_all.items() if k in ('norm_w', 'gate_w', 'w13', 'w2', 'shared_gate_w', 'shared_up_w', 'shared_down_w')}
    del _L0_ffn_all

    def _L1_xattn_setup():
        import jax, jax.numpy as jnp
        import numpy as np
        B_, L_, D_MODEL = (4, 512, 256)
        D_STATE, D_CONV, EXPAND = (16, 4, 2)
        D_INNER = EXPAND * D_MODEL
        DT_RANK = (D_MODEL + 15) // 16

        def silu(x):
            return x * jax.nn.sigmoid(x)
        key = jax.random.key(seed)
        ks = jax.random.split(key, 10)
        f32 = jnp.float32
        hidden_states = jax.random.normal(ks[0], (B_, L_, D_MODEL), dtype=f32)
        z = jax.random.normal(ks[1], (B_, D_INNER, L_), dtype=f32)
        in_proj_w = jax.random.normal(ks[2], (D_INNER, D_MODEL), dtype=f32) * 0.02
        conv_w = jax.random.normal(ks[3], (D_INNER, 1, D_CONV), dtype=f32) * 0.1
        conv_b = jax.random.normal(ks[4], (D_INNER,), dtype=f32) * 0.02
        x_proj_w = jax.random.normal(ks[5], (DT_RANK + 2 * D_STATE, D_INNER), dtype=f32) * 0.02
        dt_proj_w = jax.random.uniform(ks[6], (D_INNER, DT_RANK), dtype=f32, minval=-DT_RANK ** (-0.5), maxval=DT_RANK ** (-0.5))
        dt = jnp.exp(jax.random.uniform(ks[7], (D_INNER,), dtype=f32, minval=np.log(0.001), maxval=np.log(0.1)))
        dt_proj_b = jnp.log(jnp.expm1(dt))
        A_log = jnp.log(jnp.broadcast_to(jnp.arange(1, D_STATE + 1, dtype=f32), (D_INNER, D_STATE)))
        D = jnp.ones((D_INNER,), f32)
        return {'hidden_states': hidden_states, 'z': z, 'in_proj_w': in_proj_w, 'conv_w': conv_w, 'conv_b': conv_b, 'x_proj_w': x_proj_w, 'dt_proj_w': dt_proj_w, 'dt_proj_b': dt_proj_b, 'A_log': A_log, 'D': D}
    _L1_xattn_all = _L1_xattn_setup()
    _L1_xattn_in = {k: v for k, v in _L1_xattn_all.items() if k in ('in_proj_w', 'conv_w', 'conv_b', 'x_proj_w', 'dt_proj_w', 'dt_proj_b', 'A_log', 'D')}
    del _L1_xattn_all

    def _L1_ffn_setup():
        import jax, jax.numpy as jnp
        import numpy as np
        B, S, D = (4, 512, 512)
        E = 8
        N_SHARE = 2
        N_ROUTED = E - N_SHARE
        H = 2048 // E
        key = jax.random.key(seed)
        ks = jax.random.split(key, 12)
        s = 0.02
        return {'x': jax.random.normal(ks[0], (B, S, D), jnp.float32), 'Wg': jax.random.normal(ks[1], (D, E), jnp.float32) * s, 'bg': jnp.zeros((E,), jnp.float32), 'Wgate': jax.random.normal(ks[2], (N_ROUTED, D, H), jnp.float32) * s, 'bgate': jnp.zeros((N_ROUTED, H), jnp.float32), 'Wup': jax.random.normal(ks[3], (N_ROUTED, D, H), jnp.float32) * s, 'bup': jnp.zeros((N_ROUTED, H), jnp.float32), 'Wdown': jax.random.normal(ks[4], (N_ROUTED, H, D), jnp.float32) * s, 'bdown': jnp.zeros((N_ROUTED, D), jnp.float32), 'Ws_up': jax.random.normal(ks[5], (D, N_SHARE * H), jnp.float32) * s, 'bs_up': jnp.zeros((N_SHARE * H,), jnp.float32), 'Ws_down': jax.random.normal(ks[6], (N_SHARE * H, D), jnp.float32) * s, 'bs_down': jnp.zeros((D,), jnp.float32)}
    _L1_ffn_all = _L1_ffn_setup()
    _L1_ffn_in = {k: v for k, v in _L1_ffn_all.items() if k in ('Wg', 'bg', 'Wgate', 'bgate', 'Wup', 'bup', 'Wdown', 'bdown', 'Ws_up', 'bs_up', 'Ws_down', 'bs_down')}
    del _L1_ffn_all

    def _L2_xattn_setup():
        import jax, jax.numpy as jnp
        import numpy as np
        key = jax.random.key(seed)
        ks = jax.random.split(key, 6)
        B, L, N, C, D = (8, 128, 512, 256, 128)
        return {'teacher_logits': jax.random.normal(ks[0], (B, L, N), dtype=jnp.float32), 'teacher_features': jax.random.normal(ks[1], (B, N, C), dtype=jnp.float32), 'Wq': jax.random.normal(ks[2], (D, C), dtype=jnp.float32) * (1.0 / np.sqrt(C)), 'bq': jnp.zeros((D,), dtype=jnp.float32), 'Wk': jax.random.normal(ks[3], (D, C), dtype=jnp.float32) * (1.0 / np.sqrt(C)), 'bk': jnp.zeros((D,), dtype=jnp.float32)}
    _L2_xattn_all = _L2_xattn_setup()
    _L2_xattn_in = {k: v for k, v in _L2_xattn_all.items() if k in ('Wq', 'bq', 'Wk', 'bk')}
    del _L2_xattn_all

    def _L2_ffn_setup():
        import jax, jax.numpy as jnp
        import numpy as np
        B, S, H = (2, 256, 512)
        E, K, F = (64, 8, 192)
        CAP = 128
        key = jax.random.key(seed)
        k1, k2, k3, k4, k5 = jax.random.split(key, 5)
        scale_h = 1.0 / np.sqrt(H)
        scale_f = 1.0 / np.sqrt(F)
        return {'hidden_states': jax.random.normal(k1, (B, S, H), jnp.float32), 'router_w': jax.random.normal(k2, (E, H), jnp.float32) * scale_h, 'w_gate': jax.random.normal(k3, (E, H, F), jnp.float32) * scale_h, 'w_up': jax.random.normal(k4, (E, H, F), jnp.float32) * scale_h, 'w_down': jax.random.normal(k5, (E, F, H), jnp.float32) * scale_f}
    _L2_ffn_all = _L2_ffn_setup()
    _L2_ffn_in = {k: v for k, v in _L2_ffn_all.items() if k in ('router_w', 'w_gate', 'w_up', 'w_down')}
    del _L2_ffn_all

    def _L3_xattn_setup():
        import jax, jax.numpy as jnp
        import numpy as np
        EPS = 1e-05

        def rmsnorm(x, g, eps=EPS):
            var = jnp.mean(jnp.square(x), axis=-1, keepdims=True)
            return x * jax.lax.rsqrt(var + eps) * g
        key = jax.random.key(seed)
        ks = jax.random.split(key, 8)
        B, Sq, Skv = (2, 1024, 128)
        dim, cdim, H, D = (512, 256, 16, 128)
        inner = H * D
        s = lambda f: 1.0 / np.sqrt(f)
        return {'hidden_states': jax.random.normal(ks[0], (B, Sq, dim), jnp.float32), 'encoder_hidden_states': jax.random.normal(ks[1], (B, Skv, cdim), jnp.float32), 'Wq': jax.random.normal(ks[2], (dim, inner), jnp.float32) * s(dim), 'Wk': jax.random.normal(ks[3], (cdim, inner), jnp.float32) * s(cdim), 'Wv': jax.random.normal(ks[4], (cdim, inner), jnp.float32) * s(cdim), 'Wo': jax.random.normal(ks[5], (inner, dim), jnp.float32) * s(inner), 'gq': jnp.ones((D,), jnp.float32), 'gk': jnp.ones((D,), jnp.float32)}
    _L3_xattn_all = _L3_xattn_setup()
    _L3_xattn_in = {k: v for k, v in _L3_xattn_all.items() if k in ('Wq', 'Wk', 'Wv', 'Wo', 'gq', 'gk')}
    del _L3_xattn_all

    def _L3_ffn_setup():
        import jax, jax.numpy as jnp
        import numpy as np
        BLOCK_SIZE = 64
        SCALER_BLOCK_SIZE = 64
        NF4 = jnp.array([-1.0, -0.6962, -0.5251, -0.3949, -0.2844, -0.1848, -0.0911, 0.0, 0.0796, 0.1609, 0.2461, 0.3379, 0.4407, 0.5626, 0.723, 1.0], dtype=jnp.bfloat16)

        def nf4_quantize(w):
            flat = w.reshape(-1)
            n_blocks = flat.size // BLOCK_SIZE
            blocks = flat.reshape(n_blocks, BLOCK_SIZE)
            scalers_1 = jnp.max(jnp.abs(blocks), axis=1)
            scaler_mean = scalers_1.mean()
            centered = scalers_1 - scaler_mean
            nsb = n_blocks // SCALER_BLOCK_SIZE
            sb = centered.reshape(nsb, SCALER_BLOCK_SIZE)
            s_absmax = jnp.max(jnp.abs(sb), axis=1, keepdims=True)
            qf = 256.0 / (2.0 * s_absmax)
            q_scalers = jnp.clip(jnp.round(sb * qf), -128, 127).astype(jnp.int8).reshape(-1)
            scaled = (blocks / scalers_1[:, None]).reshape(-1)
            idx = jnp.argmin(jnp.abs(scaled[:, None] - NF4), axis=-1).astype(jnp.uint8)
            packed = idx[::2] << 4 | idx[1::2]
            return (q_scalers, qf[:, 0], scaler_mean, packed)

        def nf4_dequantize(q_scalers, qf, scaler_mean, packed, shape):
            first = NF4[(packed >> 4).astype(jnp.int32)]
            second = NF4[(packed & 15).astype(jnp.int32)]
            nsb = qf.shape[0]
            deq_scalers = (q_scalers.reshape(nsb, SCALER_BLOCK_SIZE) / qf[:, None]).reshape(-1).astype(jnp.bfloat16) + scaler_mean
            rep = jnp.repeat(deq_scalers, BLOCK_SIZE // 2)
            sf = first * rep
            ss = second * rep
            return jnp.stack([sf, ss], axis=-1).reshape(shape)

        def nf4_roundtrip(w):
            return nf4_dequantize(*nf4_quantize(w), w.shape)
        key = jax.random.key(seed)
        k0, k1, k2, k3 = jax.random.split(key, 4)
        d_model, d_ff = (512, 1408)
        x = jax.random.normal(k0, (4, 512, d_model), dtype=jnp.bfloat16)
        weight1 = jax.random.normal(k1, (d_ff, d_model), dtype=jnp.bfloat16) * 0.02
        weight2 = jax.random.normal(k2, (d_ff, d_model), dtype=jnp.bfloat16) * 0.02
        weight3 = jax.random.normal(k3, (d_model, d_ff), dtype=jnp.bfloat16) * 0.02
        return {'x': x, 'weight1': weight1, 'weight2': weight2, 'weight3': weight3}
    _L3_ffn_all = _L3_ffn_setup()
    _L3_ffn_in = {k: v for k, v in _L3_ffn_all.items() if k in ('weight1', 'weight2', 'weight3')}
    del _L3_ffn_all
    return {'x': x, 'ctx_1024': ctx_1024, 'L0_xattn_in_proj_w': _L0_xattn_in['in_proj_w'], 'L0_xattn_conv_w': _L0_xattn_in['conv_w'], 'L0_xattn_conv_b': _L0_xattn_in['conv_b'], 'L0_xattn_x_proj_w': _L0_xattn_in['x_proj_w'], 'L0_xattn_dt_proj_w': _L0_xattn_in['dt_proj_w'], 'L0_xattn_dt_proj_b': _L0_xattn_in['dt_proj_b'], 'L0_xattn_A_log': _L0_xattn_in['A_log'], 'L0_xattn_D': _L0_xattn_in['D'], 'L0_ffn_norm_w': _L0_ffn_in['norm_w'], 'L0_ffn_gate_w': _L0_ffn_in['gate_w'], 'L0_ffn_w13': _L0_ffn_in['w13'], 'L0_ffn_w2': _L0_ffn_in['w2'], 'L0_ffn_shared_gate_w': _L0_ffn_in['shared_gate_w'], 'L0_ffn_shared_up_w': _L0_ffn_in['shared_up_w'], 'L0_ffn_shared_down_w': _L0_ffn_in['shared_down_w'], 'L1_xattn_in_proj_w': _L1_xattn_in['in_proj_w'], 'L1_xattn_conv_w': _L1_xattn_in['conv_w'], 'L1_xattn_conv_b': _L1_xattn_in['conv_b'], 'L1_xattn_x_proj_w': _L1_xattn_in['x_proj_w'], 'L1_xattn_dt_proj_w': _L1_xattn_in['dt_proj_w'], 'L1_xattn_dt_proj_b': _L1_xattn_in['dt_proj_b'], 'L1_xattn_A_log': _L1_xattn_in['A_log'], 'L1_xattn_D': _L1_xattn_in['D'], 'L1_ffn_Wg': _L1_ffn_in['Wg'], 'L1_ffn_bg': _L1_ffn_in['bg'], 'L1_ffn_Wgate': _L1_ffn_in['Wgate'], 'L1_ffn_bgate': _L1_ffn_in['bgate'], 'L1_ffn_Wup': _L1_ffn_in['Wup'], 'L1_ffn_bup': _L1_ffn_in['bup'], 'L1_ffn_Wdown': _L1_ffn_in['Wdown'], 'L1_ffn_bdown': _L1_ffn_in['bdown'], 'L1_ffn_Ws_up': _L1_ffn_in['Ws_up'], 'L1_ffn_bs_up': _L1_ffn_in['bs_up'], 'L1_ffn_Ws_down': _L1_ffn_in['Ws_down'], 'L1_ffn_bs_down': _L1_ffn_in['bs_down'], 'L2_xattn_Wq': _L2_xattn_in['Wq'], 'L2_xattn_bq': _L2_xattn_in['bq'], 'L2_xattn_Wk': _L2_xattn_in['Wk'], 'L2_xattn_bk': _L2_xattn_in['bk'], 'L2_ffn_router_w': _L2_ffn_in['router_w'], 'L2_ffn_w_gate': _L2_ffn_in['w_gate'], 'L2_ffn_w_up': _L2_ffn_in['w_up'], 'L2_ffn_w_down': _L2_ffn_in['w_down'], 'L3_xattn_Wq': _L3_xattn_in['Wq'], 'L3_xattn_Wk': _L3_xattn_in['Wk'], 'L3_xattn_Wv': _L3_xattn_in['Wv'], 'L3_xattn_Wo': _L3_xattn_in['Wo'], 'L3_xattn_gq': _L3_xattn_in['gq'], 'L3_xattn_gk': _L3_xattn_in['gk'], 'L3_ffn_weight1': _L3_ffn_in['weight1'], 'L3_ffn_weight2': _L3_ffn_in['weight2'], 'L3_ffn_weight3': _L3_ffn_in['weight3']}

def reference(x, ctx_1024, L0_xattn_in_proj_w, L0_xattn_conv_w, L0_xattn_conv_b, L0_xattn_x_proj_w, L0_xattn_dt_proj_w, L0_xattn_dt_proj_b, L0_xattn_A_log, L0_xattn_D, L0_ffn_norm_w, L0_ffn_gate_w, L0_ffn_w13, L0_ffn_w2, L0_ffn_shared_gate_w, L0_ffn_shared_up_w, L0_ffn_shared_down_w, L1_xattn_in_proj_w, L1_xattn_conv_w, L1_xattn_conv_b, L1_xattn_x_proj_w, L1_xattn_dt_proj_w, L1_xattn_dt_proj_b, L1_xattn_A_log, L1_xattn_D, L1_ffn_Wg, L1_ffn_bg, L1_ffn_Wgate, L1_ffn_bgate, L1_ffn_Wup, L1_ffn_bup, L1_ffn_Wdown, L1_ffn_bdown, L1_ffn_Ws_up, L1_ffn_bs_up, L1_ffn_Ws_down, L1_ffn_bs_down, L2_xattn_Wq, L2_xattn_bq, L2_xattn_Wk, L2_xattn_bk, L2_ffn_router_w, L2_ffn_w_gate, L2_ffn_w_up, L2_ffn_w_down, L3_xattn_Wq, L3_xattn_Wk, L3_xattn_Wv, L3_xattn_Wo, L3_xattn_gq, L3_xattn_gk, L3_ffn_weight1, L3_ffn_weight2, L3_ffn_weight3):
    import jax
    import jax.numpy as jnp

    def _L0_xattn_ref(hidden_states, z, in_proj_w, conv_w, conv_b, x_proj_w, dt_proj_w, dt_proj_b, A_log, D):
        import jax, jax.numpy as jnp
        import numpy as np
        import math
        B, L, DM = (2, 512, 256)
        DS, DC, EXP = (16, 4, 2)
        DI = EXP * DM
        DR = math.ceil(DM / 16)
        DT_MIN, DT_MAX, DT_FLOOR = (0.001, 0.1, 0.0001)

        def _ssm_forward(hidden_states, z, in_proj_w, conv_w, conv_b, x_proj_w, dt_proj_w, dt_proj_b, A_log, D):
            b = hidden_states.shape[0]
            x = jnp.einsum('ed,bld->bel', in_proj_w, hidden_states)
            xp = jnp.pad(x, ((0, 0), (0, 0), (DC - 1, 0)))
            xc = jax.lax.conv_general_dilated(xp, conv_w[:, None, :], window_strides=(1,), padding='VALID', dimension_numbers=('NCH', 'OIH', 'NCH'), feature_group_count=DI)
            u = jax.nn.silu(xc + conv_b[None, :, None])
            x_dbl = jnp.einsum('ke,bel->bkl', x_proj_w, u)
            dt_lo = x_dbl[:, :DR]
            Bm = x_dbl[:, DR:DR + DS]
            Cm = x_dbl[:, DR + DS:]
            delta = jax.nn.softplus(jnp.einsum('er,brl->bel', dt_proj_w, dt_lo) + dt_proj_b[None, :, None])
            A = -jnp.exp(A_log)

            def step(state, xs):
                d_t, B_t, C_t, u_t = xs
                dA = jnp.exp(d_t[..., None] * A)
                state = state * dA + (d_t * u_t)[..., None] * B_t[:, None, :]
                y_t = jnp.einsum('ben,bn->be', state, C_t)
                return (state, y_t)
            xs = (jnp.moveaxis(delta, -1, 0), jnp.moveaxis(Bm, -1, 0), jnp.moveaxis(Cm, -1, 0), jnp.moveaxis(u, -1, 0))
            state0 = jnp.zeros((b, DI, DS), delta.dtype)
            _, ys = jax.lax.scan(step, state0, xs)
            y = jnp.moveaxis(ys, 0, -1)
            y = y + D[None, :, None] * u
            y = y * jax.nn.silu(z)
            return jnp.swapaxes(y, 1, 2)
        return _ssm_forward(hidden_states, z, in_proj_w, conv_w, conv_b, x_proj_w, dt_proj_w, dt_proj_b, A_log, D)

    def _L0_ffn_ref(hidden_states, norm_w, gate_w, w13, w2, shared_gate_w, shared_up_w, shared_down_w):
        import jax, jax.numpy as jnp
        import numpy as np
        H = 512
        I = 256
        E = 32
        K = 4
        N_SHARED = 1
        EPS = 1e-06

        def _rmsnorm(x, w, eps=EPS):
            var = jnp.mean(jnp.square(x), axis=-1, keepdims=True)
            return x * jax.lax.rsqrt(var + eps) * w

        def _moe_core(x, gate_w, w13, w2):
            T = x.shape[0]
            N = T * K
            C = 2 * N // E
            logits = jnp.einsum('th,eh->te', x.astype(jnp.float32), gate_w.astype(jnp.float32))
            scores = jax.nn.softmax(logits, axis=-1)
            topk_w, topk_ids = jax.lax.top_k(scores, K)
            topk_w = topk_w / jnp.sum(topk_w, axis=-1, keepdims=True)
            flat_ids = topk_ids.reshape(-1)
            flat_w = topk_w.reshape(-1)
            order = jnp.argsort(flat_ids)
            sorted_eid = flat_ids[order]
            tok = order // K
            counts = jnp.zeros((E,), jnp.int32).at[flat_ids].add(1)
            starts = jnp.cumsum(counts) - counts
            pos = jnp.arange(N) - starts[sorted_eid]
            buf = jnp.zeros((E, C, x.shape[1]), x.dtype).at[sorted_eid, pos].set(x[tok], mode='drop')
            gu = jnp.einsum('ech,ehf->ecf', buf, w13)
            g, u = jnp.split(gu, 2, axis=-1)
            act = jax.nn.silu(g) * u
            eo = jnp.einsum('eci,eih->ech', act, w2)
            out_slots = eo[sorted_eid, pos]
            routed = jnp.zeros_like(x).at[tok].add(out_slots * flat_w[order][:, None])
            return routed
        B, S, Hd = hidden_states.shape
        residual = hidden_states
        h = _rmsnorm(hidden_states, norm_w)
        x = h.reshape(-1, Hd)
        routed = _moe_core(x, gate_w, w13, w2)
        shared = jax.nn.silu(x @ shared_gate_w) * (x @ shared_up_w) @ shared_down_w
        out = residual + (routed + shared).reshape(B, S, Hd)
        return out

    def _L1_xattn_ref(hidden_states, z, in_proj_w, conv_w, conv_b, x_proj_w, dt_proj_w, dt_proj_b, A_log, D):
        import jax, jax.numpy as jnp
        import numpy as np
        B_, L_, D_MODEL = (4, 512, 256)
        D_STATE, D_CONV, EXPAND = (16, 4, 2)
        D_INNER = EXPAND * D_MODEL
        DT_RANK = (D_MODEL + 15) // 16

        def silu(x):
            return x * jax.nn.sigmoid(x)
        Bsz, L, _ = hidden_states.shape
        d_inner, _, d_conv = conv_w.shape
        dt_rank = dt_proj_w.shape[1]
        d_state = A_log.shape[1]
        x = jnp.einsum('bld,ed->bel', hidden_states, in_proj_w)
        xc = jax.lax.conv_general_dilated(x, conv_w, window_strides=(1,), padding=[(d_conv - 1, 0)], feature_group_count=d_inner, dimension_numbers=('NCH', 'OIH', 'NCH'))
        x = silu(xc + conv_b[None, :, None])
        x_dbl = jnp.einsum('bdl,ed->bel', x, x_proj_w)
        dt_low, Bm, Cm = jnp.split(x_dbl, [dt_rank, dt_rank + d_state], axis=1)
        dt = jnp.einsum('brl,dr->bdl', dt_low, dt_proj_w)
        dt = jax.nn.softplus(dt + dt_proj_b[None, :, None])
        A = -jnp.exp(A_log)
        dt_t = jnp.moveaxis(dt, -1, 0)
        B_t = jnp.moveaxis(Bm, -1, 0)
        C_t = jnp.moveaxis(Cm, -1, 0)
        u_t = jnp.moveaxis(x, -1, 0)

        def step(state, inp):
            d, b, c, u = inp
            dA = jnp.exp(d[..., None] * A)
            state = state * dA + (d * u)[..., None] * b[:, None, :]
            y = jnp.einsum('bdn,bn->bd', state, c)
            return (state, y)
        state0 = jnp.zeros((Bsz, d_inner, d_state), x.dtype)
        _, ys = jax.lax.scan(step, state0, (dt_t, B_t, C_t, u_t))
        y = jnp.moveaxis(ys, 0, 2)
        y = y + D[None, :, None] * x
        y = y * silu(z)
        return jnp.swapaxes(y, 1, 2)

    def _L1_ffn_ref(x, Wg, bg, Wgate, bgate, Wup, bup, Wdown, bdown, Ws_up, bs_up, Ws_down, bs_down):
        import jax, jax.numpy as jnp
        import numpy as np
        B, S, D = (4, 512, 512)
        E = 8
        N_SHARE = 2
        N_ROUTED = E - N_SHARE
        H = 2048 // E
        b, s, d = x.shape
        T = b * s
        n = Wgate.shape[0]
        xf = x.reshape(T, d)
        gate = xf @ Wg + bg
        vals, ids = jax.lax.top_k(gate, n)
        rows = jnp.arange(T)[:, None]
        masked = jnp.full_like(gate, -jnp.inf).at[rows, ids].set(vals)
        probs = jax.nn.softmax(masked, axis=-1)
        routed_mask = (ids[:, :, None] == jnp.arange(n)).any(axis=1)
        w = probs[:, :n] * routed_mask
        g = jnp.einsum('td,ndh->tnh', xf, Wgate) + bgate
        u = jnp.einsum('td,ndh->tnh', xf, Wup) + bup
        h = jax.nn.silu(g) * u
        eo = jnp.einsum('tnh,nhd->tnd', h, Wdown) + bdown
        routed_out = jnp.einsum('tnd,tn->td', eo, w)
        share = jax.nn.silu(xf @ Ws_up + bs_up) @ Ws_down + bs_down
        return (routed_out + share).reshape(b, s, d)

    def _L2_xattn_ref(teacher_logits, teacher_features, Wq, bq, Wk, bk):
        import jax, jax.numpy as jnp
        import numpy as np
        query = jnp.einsum('bnc,dc->bnd', teacher_features, Wq) + bq
        key = jnp.einsum('bnc,dc->bnd', teacher_features, Wk) + bk
        energy = jnp.einsum('bnd,bmd->bnm', query, key)
        attention = jax.nn.softmax(energy, axis=-1)
        x_m = jnp.einsum('bln,bmn->blm', teacher_logits, attention)
        return x_m

    def _L2_ffn_ref(hidden_states, router_w, w_gate, w_up, w_down):
        import jax, jax.numpy as jnp
        import numpy as np
        B, S, H = (2, 256, 512)
        E, K, F = (64, 8, 192)
        CAP = 128
        b, s, h = hidden_states.shape
        T = b * s
        xf = hidden_states.reshape(T, h)
        logits = xf @ router_w.T
        scores = jax.nn.softmax(logits.astype(jnp.float32), axis=-1)
        topk_w, topk_idx = jax.lax.top_k(scores, K)
        topk_w = topk_w / (topk_w.sum(axis=-1, keepdims=True) + 1e-20)
        slot_expert = topk_idx.reshape(-1)
        slot_token = jnp.repeat(jnp.arange(T), K)
        onehot = jax.nn.one_hot(slot_expert, E, dtype=jnp.int32)
        pos = (jnp.cumsum(onehot, axis=0) * onehot).sum(-1) - 1
        valid = pos < CAP
        dest = jnp.where(valid, slot_expert * CAP + pos, E * CAP)
        buf = jnp.zeros((E * CAP + 1, h), xf.dtype).at[dest].set(xf[slot_token])
        xb = buf[:E * CAP].reshape(E, CAP, h)
        gate = jnp.einsum('ech,ehf->ecf', xb, w_gate)
        up = jnp.einsum('ech,ehf->ecf', xb, w_up)
        hmid = jax.nn.silu(gate) * up
        yb = jnp.einsum('ecf,efh->ech', hmid, w_down).reshape(E * CAP, h)
        yb = jnp.concatenate([yb, jnp.zeros((1, h), yb.dtype)], axis=0)
        slot_out = yb[dest] * topk_w.reshape(-1)[:, None].astype(yb.dtype)
        out = jnp.zeros((T, h), yb.dtype).at[slot_token].add(slot_out)
        return out.reshape(b, s, h)

    def _L3_xattn_ref(hidden_states, encoder_hidden_states, Wq, Wk, Wv, Wo, gq, gk):
        import jax, jax.numpy as jnp
        import numpy as np
        EPS = 1e-05

        def rmsnorm(x, g, eps=EPS):
            var = jnp.mean(jnp.square(x), axis=-1, keepdims=True)
            return x * jax.lax.rsqrt(var + eps) * g
        B, Sq, _ = hidden_states.shape
        Skv = encoder_hidden_states.shape[1]
        D = gq.shape[0]
        H = Wq.shape[1] // D
        scale = 1.0 / np.sqrt(D)
        q = (hidden_states @ Wq).reshape(B, Sq, H, D)
        k = (encoder_hidden_states @ Wk).reshape(B, Skv, H, D)
        v = (encoder_hidden_states @ Wv).reshape(B, Skv, H, D)
        q = rmsnorm(q, gq)
        k = rmsnorm(k, gk)
        scores = jnp.einsum('bqhd,bkhd->bhqk', q, k) * scale
        attn = jax.nn.softmax(scores, axis=-1)
        out = jnp.einsum('bhqk,bkhd->bqhd', attn, v)
        out = out.reshape(B, Sq, H * D)
        return out @ Wo

    def _L3_ffn_ref(x, weight1, weight2, weight3):
        import jax, jax.numpy as jnp
        import numpy as np
        BLOCK_SIZE = 64
        SCALER_BLOCK_SIZE = 64
        NF4 = jnp.array([-1.0, -0.6962, -0.5251, -0.3949, -0.2844, -0.1848, -0.0911, 0.0, 0.0796, 0.1609, 0.2461, 0.3379, 0.4407, 0.5626, 0.723, 1.0], dtype=jnp.bfloat16)

        def nf4_quantize(w):
            flat = w.reshape(-1)
            n_blocks = flat.size // BLOCK_SIZE
            blocks = flat.reshape(n_blocks, BLOCK_SIZE)
            scalers_1 = jnp.max(jnp.abs(blocks), axis=1)
            scaler_mean = scalers_1.mean()
            centered = scalers_1 - scaler_mean
            nsb = n_blocks // SCALER_BLOCK_SIZE
            sb = centered.reshape(nsb, SCALER_BLOCK_SIZE)
            s_absmax = jnp.max(jnp.abs(sb), axis=1, keepdims=True)
            qf = 256.0 / (2.0 * s_absmax)
            q_scalers = jnp.clip(jnp.round(sb * qf), -128, 127).astype(jnp.int8).reshape(-1)
            scaled = (blocks / scalers_1[:, None]).reshape(-1)
            idx = jnp.argmin(jnp.abs(scaled[:, None] - NF4), axis=-1).astype(jnp.uint8)
            packed = idx[::2] << 4 | idx[1::2]
            return (q_scalers, qf[:, 0], scaler_mean, packed)

        def nf4_dequantize(q_scalers, qf, scaler_mean, packed, shape):
            first = NF4[(packed >> 4).astype(jnp.int32)]
            second = NF4[(packed & 15).astype(jnp.int32)]
            nsb = qf.shape[0]
            deq_scalers = (q_scalers.reshape(nsb, SCALER_BLOCK_SIZE) / qf[:, None]).reshape(-1).astype(jnp.bfloat16) + scaler_mean
            rep = jnp.repeat(deq_scalers, BLOCK_SIZE // 2)
            sf = first * rep
            ss = second * rep
            return jnp.stack([sf, ss], axis=-1).reshape(shape)

        def nf4_roundtrip(w):
            return nf4_dequantize(*nf4_quantize(w), w.shape)
        w1 = nf4_roundtrip(weight1)
        w2 = nf4_roundtrip(weight2)
        w3 = nf4_roundtrip(weight3)
        a = jnp.einsum('bsd,fd->bsf', x, w1)
        b = jnp.einsum('bsd,fd->bsf', x, w2)
        h = jax.nn.silu(a) * b
        return jnp.einsum('bsf,df->bsd', h, w3)
    x = x + _L0_xattn_ref(ctx_1024, _layernorm(x, axis=-1), L0_xattn_in_proj_w, L0_xattn_conv_w, L0_xattn_conv_b, L0_xattn_x_proj_w, L0_xattn_dt_proj_w, L0_xattn_dt_proj_b, L0_xattn_A_log, L0_xattn_D)
    x = x + _L0_ffn_ref(_layernorm(x, axis=-1), L0_ffn_norm_w, L0_ffn_gate_w, L0_ffn_w13, L0_ffn_w2, L0_ffn_shared_gate_w, L0_ffn_shared_up_w, L0_ffn_shared_down_w)
    x = x + _L1_xattn_ref(ctx_1024, _layernorm(x, axis=-1), L1_xattn_in_proj_w, L1_xattn_conv_w, L1_xattn_conv_b, L1_xattn_x_proj_w, L1_xattn_dt_proj_w, L1_xattn_dt_proj_b, L1_xattn_A_log, L1_xattn_D)
    x = x + _L1_ffn_ref(_layernorm(x, axis=-1), L1_ffn_Wg, L1_ffn_bg, L1_ffn_Wgate, L1_ffn_bgate, L1_ffn_Wup, L1_ffn_bup, L1_ffn_Wdown, L1_ffn_bdown, L1_ffn_Ws_up, L1_ffn_bs_up, L1_ffn_Ws_down, L1_ffn_bs_down)
    x = x + _L2_xattn_ref(_layernorm(x, axis=-1), ctx_1024, L2_xattn_Wq, L2_xattn_bq, L2_xattn_Wk, L2_xattn_bk)
    x = x + _L2_ffn_ref(_layernorm(x, axis=-1), L2_ffn_router_w, L2_ffn_w_gate, L2_ffn_w_up, L2_ffn_w_down)
    x = x + _L3_xattn_ref(_layernorm(x, axis=-1), ctx_1024, L3_xattn_Wq, L3_xattn_Wk, L3_xattn_Wv, L3_xattn_Wo, L3_xattn_gq, L3_xattn_gk)
    x = x + _L3_ffn_ref(_layernorm(x, axis=-1), L3_ffn_weight1, L3_ffn_weight2, L3_ffn_weight3)
    return x

_drawn_inputs = setup_inputs


def setup_inputs(seed=0):
    import zlib

    import numpy as np

    out = dict(_drawn_inputs(seed))
    spreads = {'L0_xattn_conv_b': (0.0, 0.1),
     'L0_xattn_D': (1.0, 0.2),
     'L0_ffn_norm_w': (1.0, 0.2),
     'L1_xattn_D': (1.0, 0.6),
     'L1_ffn_bg': (0.0, 2.0),
     'L1_ffn_bgate': (0.0, 2.0),
     'L1_ffn_bup': (0.0, 2.0),
     'L1_ffn_bdown': (0.0, 2.0),
     'L1_ffn_bs_up': (0.0, 2.0),
     'L1_ffn_bs_down': (0.0, 0.8),
     'L2_xattn_bq': (0.0, 0.8),
     'L2_xattn_bk': (0.0, 2.0),
     'L3_xattn_gq': (1.0, 0.6),
     'L3_xattn_gk': (1.0, 0.6)}
    factors = {'L0_xattn_dt_proj_w': 3.546,
     'L1_xattn_in_proj_w': 5.233,
     'L1_xattn_conv_w': 5.386,
     'L1_xattn_conv_b': 8.0,
     'L1_xattn_x_proj_w': 8.0,
     'L1_xattn_dt_proj_w': 8.0,
     'L1_xattn_dt_proj_b': 8.0,
     'L1_xattn_A_log': 8.0,
     'L1_ffn_Wg': 4.811,
     'L1_ffn_Wgate': 7.283,
     'L1_ffn_Wup': 7.188,
     'L1_ffn_Wdown': 6.897,
     'L1_ffn_Ws_up': 8.0,
     'L1_ffn_Ws_down': 8.0,
     'L2_xattn_Wq': 8.0,
     'L2_xattn_Wk': 8.0,
     'L2_ffn_router_w': 8.0,
     'L2_ffn_w_gate': 8.0,
     'L2_ffn_w_up': 8.0,
     'L2_ffn_w_down': 8.0,
     'L3_xattn_Wq': 8.0,
     'L3_xattn_Wk': 8.0,
     'L3_xattn_Wv': 8.0,
     'L3_xattn_Wo': 8.0,
     'L3_ffn_weight1': 8.0,
     'L3_ffn_weight2': 8.0,
     'L3_ffn_weight3': 8.0}
    for name, (base, spread) in spreads.items():
        noise = np.random.default_rng([zlib.crc32(name.encode()), seed]).standard_normal(out[name].shape)
        drawn = base * np.exp(spread * noise) if base else spread * noise
        out[name] = jnp.asarray(drawn.astype(out[name].dtype))
    for name, factor in factors.items():
        out[name] = (out[name] * factor).astype(out[name].dtype)
    return out
```

```python
from contextlib import ExitStack

import concourse.bass as bass
from concourse import mybir

F32 = mybir.dt.float32
BF16 = mybir.dt.bfloat16
I32 = mybir.dt.int32
U32 = mybir.dt.uint32
ACT = mybir.ActivationFunctionType
ALU = mybir.AluOpType
AX = mybir.AxisListType

P = 128
B = 4
L = 512
D = 512
T = B * L
NT = T // P
LT = L // P
KD = D // P
DC = 256
KC = DC // P
NS = 16
DR = 16
LN_EPS = 1e-5
EXP_FLOOR = -87.33654

ds = bass.ds


class Stage:

    def __init__(self, nc, name):
        self.nc, self.name, self.ctx, self.sems = nc, name, ExitStack(), []

    def __enter__(self):
        self.ctx.__enter__()
        return self

    def sb(self, name, shape, dt=F32):
        return self.ctx.enter_context(self.nc.sbuf_tensor(f"{self.name}_{name}", shape, dt))

    def ps(self, name, shape, dt=F32):
        return self.ctx.enter_context(self.nc.psum_tensor(f"{self.name}_{name}", shape, dt))

    def sem(self, name):
        s = self.ctx.enter_context(self.nc.semaphore(f"{self.name}_{name}"))
        self.sems.append(s)
        return s

    def sems_of(self, name, n):
        return [self.sem(f"{name}{i}") for i in range(n)]

    def block(self):
        for s in self.sems:
            self.nc.gpsimd.sem_inc(s, 1)
        self.nc.all_engine_barrier(sem_only=True)
        return self.nc.Block()

    def __exit__(self, *exc):
        if exc[0] is None:
            for s in self.sems:
                self.nc.gpsimd.sem_clear(s)
        return self.ctx.__exit__(*exc)


class Own:

    def __init__(self, eng, sem):
        self.eng, self.sem, self.base, self.n = eng, sem, 0, 0

    def turn(self, i, per):
        self.start, self.per = self.base + self.n, per
        self.base, self.n = self.start + i * per, 0

    def turns_over(self, count):
        assert self.n == self.per, (self.n, self.per)
        self.base, self.n = self.start + count * self.per, 0

    def step(self, ins):
        ins.then_inc(self.sem, 1)
        self.n += 1

    def settle(self):
        self.eng.wait_ge(self.sem, self.base + self.n + 1)

    def link(self, ins):
        self.step(ins)
        self.settle()


def take_wait(eng, sem):
    eng.sem_inc(sem, 1)


def channels_first(ap):
    return ap.rearrange("(k p) n -> p k n", p=P)



def layer_norm(nc, g, name, zT=None, rms_weight=None, z_dram=None, router=None, keep_stats=None):
    with Stage(nc, name) as st:
        bn6 = st.sb("bn6", [P, NT, 6])
        mv = st.sb("mv", [P, NT, 2])
        std = st.sb("std", [P, NT])
        std2 = st.sb("std2", [P, NT])
        eps = st.sb("eps", [P, 2])
        z = st.sb("z", [P, 2, D])
        zTs = st.sb("zTs", [P, 2, D])
        psT = st.ps("psT", [P, 2, D])
        own_dve = st.sem("own_dve")
        own_act = st.sem("own_act")
        var_ready = st.sem("var_ready")
        std_ready = st.sem("std_ready")
        z_ready = st.sem("z_ready")
        turned = st.sems_of("turned", 2)
        taken = st.sems_of("taken", 2)
        z_stored = st.sems_of("z_stored", 2)
        consts_in = st.sem("consts_in")
        rms = rms_weight is not None
        if rms:
            w_sb = st.sb("w", [P, D])
        if router:
            router.allocate(st)

        with st.block() as block:

            @block.sync
            def _(sp):
                if rms:
                    sp.dma_start(w_sb[:], rms_weight.rearrange("(a n) -> a n", a=1).broadcast_to([P, D])).then_inc(consts_in, 16)
                if router:
                    router.load(sp)
                if z_dram is not None:
                    rows = z_dram.rearrange("(t p) n -> p t n", p=P)
                    with sp.Fori(0, NT // 2) as i:
                        for s in range(2):
                            sp.wait_ge(z_ready, i * 2 + s + 2)
                            sp.dma_start(rows[:, ds(i * 2 + s, 1), :], z[:, s:s + 1, :]).then_inc(z_stored[s], 16)
                    for s in range(2):
                        sp.wait_ge(z_stored[s], 16 * (NT // 2) + 1)

            @block.vector
            def _(dve):
                own = Own(dve, own_dve)
                own.step(dve.memset(eps[:, 0:1], LN_EPS))
                own.link(dve.memset(eps[:, 1:2], 1e-6))
                with dve.Fori(0, NT) as t:
                    own.turn(t, 1)
                    own.step(dve.bn_stats(bn6[:, ds(t, 1), :], g.x[:, ds(t, 1), :]))
                own.turns_over(NT)
                own.settle()
                for t in range(NT):
                    own.step(dve.bn_aggr(mv[:, t, :], bn6[:, t, :]))
                own.settle()
                dve.tensor_copy(g.mean[:], mv[:, :, 0]).then_inc(var_ready, 1)
                dve.wait_ge(std_ready, 2)
                own.link(dve.reciprocal(g.rstd[:], std[:]))
                if rms:
                    own.link(dve.tensor_tensor(std2[:], mv[:, :, 1], g.rstd[:], ALU.mult))
                    own.step(dve.tensor_copy(g.ln_rstd[:], g.rstd[:]))
                    dve.tensor_tensor(std2[:], std2[:], g.rstd[:], ALU.mult).then_inc(var_ready, 1)
                    dve.wait_ge(std_ready, 3)
                    own.link(dve.reciprocal(std[:], std2[:]))
                    own.link(dve.tensor_tensor(g.rstd[:], g.rstd[:], std[:], ALU.mult))
                    dve.wait_ge(consts_in, 17)
                own.link(dve.scalar_tensor_tensor(g.shift[:], g.mean[:], -1.0, g.rstd[:], ALU.mult, ALU.mult))
                if router:
                    router.prepare(dve, own)
                if zT is None:
                    return
                with dve.Fori(0, NT // 2) as i:
                    own.turn(i, 2 * (int(rms) + (router.STEPS if router else 0)))
                    for s in range(2):
                        dve.wait_ge(turned[s], i + 1)
                        if z_dram is not None:
                            dve.wait_ge(z_stored[s], i * 16 + 1)
                        t = i * 2 + s
                        out = dve.tensor_scalar(z[:, s, :], g.x[:, ds(t, 1), :].rearrange("p a n -> p (a n)"),
                                                g.rstd[:, ds(t, 1)], g.shift[:, ds(t, 1)], ALU.mult, ALU.add)
                        if rms:
                            own.link(out)
                            out = dve.tensor_tensor(z[:, s, :], z[:, s, :], w_sb[:], ALU.mult)
                        out.then_inc(z_ready, 1)
                        if router:
                            router.choose(dve, own, i, s)
                own.turns_over(NT // 2)

            @block.scalar
            def _(act):
                act.wait_ge(own_dve, 3)
                act.wait_ge(var_ready, 2)
                act.activation(std[:], mv[:, :, 1], ACT.Sqrt, bias=eps[:, 0:1]).then_inc(std_ready, 1)
                if rms:
                    act.wait_ge(var_ready, 3)
                    act.wait_ge(std_ready, 2)
                    act.activation(std2[:], std2[:], ACT.Sqrt, bias=eps[:, 1:2]).then_inc(std_ready, 1)
                if zT is None:
                    return
                with act.Fori(0, NT // 2) as i:
                    for s in range(2):
                        act.wait_ge(turned[s], i + 2)
                        if router:
                            router.wait_for_reader(act, i, s)
                            act.activation(zTs[:, s, :], psT[:, s, :], ACT.Copy).then_inc(router.zTs_ready, 1)
                        act.activation(zT[:, :, ds((i * 2 + s) * P, P)],
                                       psT[:, s, :].rearrange("p (k n) -> p k n", k=KD), ACT.Copy).then_inc(taken[s], 1)
                        if router:
                            router.exponentials(act, i, s)

            @block.tensor
            def _(pe):
                if zT is None:
                    return
                with pe.Fori(0, NT // 2) as i:
                    for s in range(2):
                        pe.wait_ge(z_ready, i * 2 + s + 2)
                        pe.wait_ge(taken[s], i + 1)
                        for k in range(KD):
                            last = pe.transpose(psT[:, s, k * P:(k + 1) * P], z[:, s, k * P:(k + 1) * P], g.ident[:])
                        last.then_inc(turned[s], 1)
                        if router:
                            router.matmuls(pe, i, s, zTs)

            @block.gpsimd
            def _(pool):
                if router:
                    router.scatter(pool)


class Router:

    def __init__(self, nc, g, E, K, C, gateT, keep_overflow, eps):
        self.nc, self.g, self.E, self.K, self.C, self.gateT = nc, g, E, K, C, gateT
        self.keep_overflow = keep_overflow
        self.eps = eps
        self.STEPS = 24 if keep_overflow else 25

    def allocate(self, st):
        E, K = self.E, self.K
        self.wg = st.sb("wg", [P, KD, E])
        self.iota = st.sb("iota", [P, E])
        self.iota_i = st.sb("iota_i", [P, E], I32)
        self.row = st.sb("row", [P, 1])
        self.row_i = st.sb("row_i", [P, 1], I32)
        self.tok = st.sb("tok", [P, 1])
        self.dump = st.sb("dump", [P, 2, K])
        self.dump_i = st.sb("dump_i", [P, 2, K], I32)
        self.tok_i = st.sb("tok_i", [P, 2], I32)
        self.logits = st.sb("logits", [P, 2, E])
        self.best = st.sb("best", [P, 2, 8])
        self.which = st.sb("which", [P, 2, 8], U32)
        self.e_all = st.sb("e_all", [P, 2, E])
        self.e_best = st.sb("e_best", [P, 2, 8])
        self.z_sum = st.sb("z_sum", [P, 2])
        self.small = st.sb("small", [P, 2, 8, 8])
        self.onehot = st.sb("onehot", [P, 2, K, E])
        self.masked = st.sb("masked", [P, 2, K, E])
        self.mask = st.sb("mask", [P, 2, E])
        self.before = st.sb("before", [P, E])
        self.slot_i = st.sb("slot_i", [P, 2, K], I32)
        self.psR = st.ps("psR", [P, 2, 512])
        self.psC = st.ps("psC", [P, 2, 512])
        self.zTs_ready = st.sem("zTs_ready")
        self.router_in = st.sem("router_in")
        self.iotas = st.sem("iotas")
        self.tick = st.sem("tick")
        self.pool_tick = st.sem("pool_tick")
        self.logits_done = st.sem("logits_done")
        self.clamped = st.sem("clamped")
        self.exps_done = st.sem("exps_done")
        self.mask_ready = st.sem("mask_ready")
        self.counted = st.sem("counted")
        self.slots_ready = st.sem("slots_ready")
        self.table_zeroed = self.g.pool_sem(f"{st.name}_table_zeroed")
        self.scattered = [self.g.pool_sem(f"{st.name}_scattered{i}") for i in range(2)]
        self.slots_used = st.sem("slots_used")

    def load(self, sp):
        sp.dma_start(self.wg[:], self.gateT).then_inc(self.router_in, 16)

    def prepare(self, dve, own):
        dve.wait_ge(self.iotas, 4)
        own.step(dve.tensor_copy(self.iota[:], self.iota_i[:]))
        own.step(dve.tensor_copy(self.tok[:], self.row_i[:]))
        own.step(dve.tensor_copy(self.dump[:], self.dump_i[:]))
        own.link(dve.memset(self.before[:], 0.0))

    def matmuls(self, pe, i, s, zTs):
        E = self.E
        if s == 0:
            pe.wait_ge(self.router_in, 17)
        pe.wait_ge(self.zTs_ready, i * 2 + s + 2)
        for k in range(KD):
            last = pe.matmul(self.psR[:, s, 0:E], zTs[:, s, k * P:(k + 1) * P], self.wg[:, k, :],
                             start=(k == 0), stop=(k == KD - 1))
        last.then_inc(self.logits_done, 1)
        pe.wait_ge(self.mask_ready, i * 2 + s + 2)
        pe.matmul(self.psC[:, s, 0:E], self.g.earlier[:], self.mask[:, s, :], start=True, stop=False)
        pe.matmul(self.psC[:, s, 0:E], self.g.ones[:], self.before[:], start=False, stop=True).then_inc(self.counted, 1)

    def wait_for_reader(self, act, i, s):
        act.wait_ge(self.logits_done, i * 2 + 1)

    def exponentials(self, act, i, s):
        act.wait_ge(self.clamped, i * 2 + s + 2)
        act.activation(self.e_all[:, s, :], self.logits[:, s, :], ACT.Exp,
                       accum_out=self.z_sum[:, s:s + 1]).then_inc(self.exps_done, 1)
        act.activation(self.e_best[:, s, :], self.best[:, s, :], ACT.Exp).then_inc(self.exps_done, 1)

    def choose(self, dve, own, i, s):
        E, K, C, g, n = self.E, self.K, self.C, self.g, i * 2 + s
        v = lambda j: self.small[:, s, j, 0:K]
        top, lg = self.best[:, s, :], self.logits[:, s, :]
        dve.wait_ge(self.logits_done, n + 2)
        own.link(dve.tensor_copy(lg, self.psR[:, s, 0:E]))
        take_wait(dve, self.tick)
        own.link(dve.max(top, lg))
        own.link(dve.tensor_scalar(lg, lg, top[:, 0:1], EXP_FLOOR, ALU.subtract, ALU.max))
        take_wait(dve, self.tick)
        dve.max(top, lg).then_inc(self.clamped, 1)
        dve.wait_ge(self.clamped, n + 2)
        take_wait(dve, self.tick)
        own.link(dve.max_index(self.which[:, s, :], top, lg))
        own.link(dve.tensor_copy(self.small[:, s, 0, :], self.which[:, s, :]))
        own.link(dve.tensor_tensor(self.onehot[:, s, :, :], self.iota[:].unsqueeze(1).broadcast_to([P, K, E]),
                                   v(0).unsqueeze(2).broadcast_to([P, K, E]), ALU.is_equal))
        dve.tensor_reduce(self.mask[:, s, :], self.onehot[:, s, :, :].rearrange("p k e -> p e k"), AX.X, ALU.add).then_inc(self.mask_ready, 1)
        dve.wait_ge(self.mask_ready, n + 2)
        dve.wait_ge(self.counted, n + 2)
        own.step(dve.tensor_tensor(self.before[:], self.before[:], self.mask[:, s, :], ALU.add))
        own.link(dve.tensor_tensor(self.masked[:, s, :, :], self.onehot[:, s, :, :],
                                   self.psC[:, s, 0:E].unsqueeze(1).broadcast_to([P, K, E]), ALU.mult))
        own.link(dve.tensor_reduce(v(1), self.masked[:, s, :, :], AX.X, ALU.add))
        own.step(dve.tensor_scalar(v(2), v(1), float(C - 1), None, ALU.min))
        own.step(dve.tensor_scalar(v(3), v(1), float(C), None, ALU.is_ge))
        own.link(dve.scalar_tensor_tensor(v(4), v(0), float(C), v(1), ALU.mult, ALU.add))
        own.step(dve.scalar_tensor_tensor(g.slot_of[:, ds(n, 1), 0:K].rearrange("p a k -> p (a k)"), v(0), float(C), v(2), ALU.mult, ALU.add))
        own.link(dve.tensor_tensor(v(5), self.dump[:, s, :], v(4), ALU.subtract))
        own.link(dve.tensor_tensor(v(5), v(5), v(3), ALU.mult))
        dve.wait_ge(self.slots_used, i * 2 + 1)
        own.step(dve.tensor_copy(self.tok_i[:, s:s + 1], self.tok[:]))
        own.link(dve.tensor_tensor(self.slot_i[:, s, :], v(4), v(5), ALU.add))
        dve.tensor_scalar(self.tok[:], self.tok[:], float(P), None, ALU.add).then_inc(self.slots_ready, 1)
        dve.wait_ge(self.exps_done, 2 * n + 2 + 1)
        own.link(dve.reciprocal(self.small[:, s, 6, 0:1], self.z_sum[:, s:s + 1]))
        own.link(dve.tensor_scalar(v(5), self.e_best[:, s, 0:K], self.small[:, s, 6, 0:1], None, ALU.mult))
        own.link(dve.tensor_reduce(self.small[:, s, 6, 1:2], v(5), AX.X, ALU.add))
        own.link(dve.tensor_scalar(self.small[:, s, 6, 1:2], self.small[:, s, 6, 1:2], self.eps, None, ALU.add))
        own.link(dve.reciprocal(self.small[:, s, 6, 2:3], self.small[:, s, 6, 1:2]))
        own.link(dve.tensor_scalar(v(5), v(5), self.small[:, s, 6, 2:3], None, ALU.mult))
        w = g.weight_of[:, ds(n, 1), 0:K].rearrange("p a k -> p (a k)")
        if self.keep_overflow:
            own.step(dve.tensor_copy(w, v(5)))
        else:
            own.link(dve.tensor_scalar(v(3), v(3), -1.0, 1.0, ALU.mult, ALU.add))
            own.step(dve.tensor_tensor(w, v(5), v(3), ALU.mult))

    def scatter(self, pool):
        g, E, K, C = self.g, self.E, self.K, self.C
        pool.iota(self.iota_i[:], [[1, E]], base=0, channel_multiplier=0).then_inc(self.iotas, 1)
        pool.iota(self.row_i[:], [[0, 1]], base=0, channel_multiplier=1).then_inc(self.iotas, 1)
        pool.iota(self.dump_i[:], [[P, 2 * K]], base=E * C, channel_multiplier=1).then_inc(self.iotas, 1)
        table = g.slot_token[0:E * C + 2 * K * P]
        pool.dma_start(table.rearrange("(p n) a -> p (n a)", p=P), g.zeros_i[:, 0:E * C // P + 2 * K]).then_inc(self.table_zeroed, 16)
        pool.wait_ge(self.table_zeroed, 16)
        with pool.Fori(0, NT // 2) as i:
            for s in range(2):
                pool.wait_ge(self.slots_ready, i * 2 + s + 2)
                take_wait(pool, self.pool_tick)
                for k in range(K):
                    pool.indirect_dma_start(table, bass.IndirectOffsetOnAxis(ap=self.slot_i[:, s, k:k + 1], axis=0),
                                            self.tok_i[:, s:s + 1], None).then_inc(self.scattered[s], 16)
                pool.wait_ge(self.scattered[s], 16 * K * (i + 1))
                pool.sem_inc(self.slots_used, 1)



def mixer(nc, g, name, w):
    ET = D // P
    with Stage(nc, name) as st:
        ctxT = st.sb("ctxT", [P, KC, T])
        w_in = st.sb("w_in", [P, KC, D])
        w_x = st.sb("w_x", [P, ET, DR + 2 * NS])
        w_dt = st.sb("w_dt", [DR, D])
        cols = st.sb("cols", [P, ET, 7 + NS])
        A = st.sb("A", [P, ET, NS])
        diagD = st.sb("diagD", [P, ET, P])
        xpad = st.sb("xpad", [P, ET, L + 3])
        u = st.sb("u", [P, ET, L])
        delta = st.sb("delta", [P, ET, L])
        du = st.sb("du", [P, ET, L])
        gate = st.sb("gate", [P, ET, L])
        x_dbl = st.sb("x_dbl", [DR + 2 * NS, L])
        decay = st.sb("decay", [P, 2, ET, L])
        h = st.sb("h", [P, 4, ET, L])
        bc = st.sb("bc", [P, 4, 2, L])
        conv, soft = h[:, 0, :, :], h[:, 1, :, :]
        tail, relu = h[:, 2, :, :], h[:, 3, :, :]
        yT = h[:, 0, :, :]
        psY = st.ps("psY", [P, ET, L])
        psA = st.ps("psA", [P, 4, L])
        bc_rows = nc.dram_tensor(f"{name}_bc_rows", (B, NS, 2, L), F32).ap()

        weights_in = st.sem("weights_in")
        own_dve = st.sem("own_dve")
        own_act = st.sem("own_act")
        own_pool = st.sem("own_pool")
        a_exp = st.sem("a_exp")
        projected = st.sem("projected")
        padded = st.sem("padded")
        convolved = st.sem("convolved")
        u_ready = st.sem("u_ready")
        dbl_done = st.sem("dbl_done")
        dbl_copied = st.sem("dbl_copied")
        step_done = st.sem("step_done")
        logs_ready = st.sem("logs_ready")
        relu_ready = st.sem("relu_ready")
        abs_done = st.sem("abs_done")
        exp_done = st.sem("exp_done")
        plus_one = st.sem("plus_one")
        delta_ready = st.sem("delta_ready")
        rows_stored = st.sem("rows_stored")
        bc_in = st.sems_of("bc_in", 4)
        decayed = st.sem("decayed")
        scanned = st.sems_of("scanned", 2)
        weighted = st.sems_of("weighted", 4)
        summed = st.sems_of("summed", 4)
        y_done = st.sem("y_done")
        gate_ready = st.sem("gate_ready")
        y_gated = st.sem("y_gated")
        y_turned = st.sem("y_turned")
        added = st.sem("added")

        flat = lambda ap: ap.rearrange("p e n -> p (e n)")

        with st.block() as block:

            @block.sync
            def _(sp):
                for dst, src in ((ctxT[:], g.ctxT), (w_in[:], w["in_projT"]), (w_x[:], w["x_projT"]),
                                 (w_dt[:], w["dt_projT"]), (cols[:], w["cols"])):
                    sp.dma_start(dst, src).then_inc(weights_in, 16)
                with sp.Fori(0, B) as b:
                    sp.wait_ge(dbl_copied, b + 2)
                    for half in range(2):
                        sp.dma_start(bc_rows[ds(b, 1), :, half, :].rearrange("b n l -> (b n) l"),
                                     x_dbl[DR + half * NS:DR + (half + 1) * NS, :]).then_inc(rows_stored, 16)
                    with sp.Fori(0, NS // 4) as i:
                        for j in range(4):
                            sp.wait_ge(rows_stored, 32 * b + 32 + 1)
                            sp.wait_ge(weighted[j], b * 4 + i + 1)
                            sp.dma_start(bc[:, j, :, :].rearrange("p a l -> p (a l)"),
                                         bc_rows[ds(b, 1), ds(i * 4 + j, 1), :, :].rearrange("b n a l -> (b n) (a l)")
                                         .broadcast_to([P, 2 * L])).then_inc(bc_in[j], 16)

            @block.tensor
            def _(pe):
                pe.wait_ge(weights_in, 81)
                pe.wait_ge(own_dve, 1 + ET + 1)
                with pe.Fori(0, B) as b:
                    pe.wait_ge(added, b * LT + 1)
                    for et in range(ET):
                        for k in range(KC):
                            last = pe.matmul(psA[:, et, :], w_in[:, k, et * P:(et + 1) * P],
                                             ctxT[:, k, ds(b * L, L)], start=(k == 0), stop=(k == KC - 1))
                        last.then_inc(projected, 1)
                    for et in range(ET):
                        pe.wait_ge(u_ready, b * ET + et + 2)
                        last = pe.matmul(psA[0:DR + 2 * NS, 0, :], w_x[:, et, :], u[:, et, :],
                                         start=(et == 0), stop=(et == ET - 1))
                    last.then_inc(dbl_done, 1)
                    for et in range(ET):
                        pe.matmul(psY[:, et, :], diagD[:, et, :], u[:, et, :], start=True, stop=False,
                                  skip_group_check=True)
                    pe.wait_ge(dbl_copied, b + 2)
                    for et in range(ET):
                        last = pe.matmul(psA[:, et, :], w_dt[:, et * P:(et + 1) * P], x_dbl[0:DR, :], start=True, stop=True)
                        last.then_inc(step_done, 1)
                    with pe.Fori(0, NS // 4 - 1) as i:
                        for j in range(4):
                            pe.wait_ge(weighted[j], b * 4 + i + 2)
                            for et in range(ET):
                                last = pe.matmul(psY[:, et, :], g.ident[:], h[:, j, et, :], start=False, stop=False,
                                                 skip_group_check=True)
                            last.then_inc(summed[j], 1)
                    for j in range(4):
                        pe.wait_ge(weighted[j], b * 4 + 4 + 1)
                        for et in range(ET):
                            last = pe.matmul(psY[:, et, :], g.ident[:], h[:, j, et, :], start=False, stop=(j == 3),
                                             skip_group_check=True)
                        last.then_inc(summed[j], 1)
                    pe.wait_ge(y_gated, b + 2)
                    for lt in range(LT):
                        for et in range(ET):
                            last = pe.transpose(psA[:, lt, et * P:(et + 1) * P], yT[:, et, lt * P:(lt + 1) * P], g.ident[:])
                        last.then_inc(y_turned, 1)

            @block.scalar
            def _(act):
                act.wait_ge(weights_in, 81)
                act.activation(A[:], cols[:, :, 7:7 + NS], ACT.Exp).then_inc(a_exp, 1)
                act.wait_ge(own_dve, 2 + ET + 1)
                own = Own(act, own_act)
                with act.Fori(0, B) as b:
                    own.turn(b, 1)
                    for et in range(ET):
                        act.wait_ge(projected, b * ET + et + 2)
                        act.activation(xpad[:, et, 3:3 + L], psA[:, et, :], ACT.Copy).then_inc(padded, 1)
                    for et in range(ET):
                        act.wait_ge(convolved, b * ET + et + 2)
                        act.activation(u[:, et, :], conv[:, et, :], ACT.Silu, bias=cols[:, et, 4:5]).then_inc(u_ready, 1)
                    for et in range(ET):
                        last = act.activation(gate[:, et, :], g.x[:, ds(b * ET + et, 1), :].rearrange("p a n -> p (a n)"), ACT.Silu,
                                              bias=g.shift[:, ds(b * ET + et, 1)], scale=g.rstd[:, ds(b * ET + et, 1)])
                    last.then_inc(gate_ready, 1)
                    act.wait_ge(dbl_done, b + 2)
                    act.activation(x_dbl[:], psA[0:DR + 2 * NS, 0, :], ACT.Copy).then_inc(dbl_copied, 1)
                    for et in range(ET):
                        act.wait_ge(step_done, b * ET + et + 2)
                        last = act.activation(relu[:, et, :], psA[:, et, :], ACT.Identity, bias=cols[:, et, 5:6])
                    own.link(last)
                    act.activation(flat(delta[:]), flat(relu), ACT.Abs).then_inc(abs_done, 1)
                    act.wait_ge(abs_done, b + 2)
                    act.activation(flat(soft), flat(delta[:]), ACT.Exp, scale=-1.0).then_inc(exp_done, 1)
                    act.wait_ge(plus_one, b + 2)
                    act.activation(flat(delta[:]), flat(tail), ACT.Ln).then_inc(logs_ready, 1)
                    act.wait_ge(delta_ready, b + 2)
                    with act.Fori(0, NS // 2) as i:
                        for s in range(2):
                            act.wait_ge(scanned[s], b * (NS // 2) + i + 1)
                            for et in range(ET):
                                last = act.activation(decay[:, s, et, :], delta[:, et, :], ACT.Exp,
                                                      scale=A[:, et, ds(i * 2 + s, 1)])
                            last.then_inc(decayed, 1)
                own.turns_over(B)

            @block.vector
            def _(dve):
                own = Own(dve, own_dve)
                own.step(dve.memset(xpad[:, :, 0:3], 0.0))
                dve.wait_ge(weights_in, 81)
                for et in range(ET):
                    own.step(dve.tensor_scalar(diagD[:, et, :], g.ident[:], cols[:, et, 6:7], None, ALU.mult))
                dve.wait_ge(a_exp, 2)
                own.link(dve.tensor_scalar(A[:], A[:], -1.0, None, ALU.mult))
                with dve.Fori(0, B) as b:
                    own.turn(b, 3 * ET + 4 + NS)
                    for et in range(ET):
                        dve.wait_ge(padded, b * ET + et + 2)
                        own.link(dve.tensor_scalar(conv[:, et, :], xpad[:, et, 0:L], cols[:, et, 0:1], None, ALU.mult))
                        for tap in range(1, 4):
                            out = dve.scalar_tensor_tensor(conv[:, et, :], xpad[:, et, tap:tap + L], cols[:, et, tap:tap + 1],
                                                           conv[:, et, :], ALU.mult, ALU.add)
                            if tap < 3:
                                own.link(out)
                            else:
                                out.then_inc(convolved, 1)
                    dve.wait_ge(abs_done, b + 2)
                    dve.tensor_scalar(flat(relu), flat(relu), 0.0, None, ALU.max).then_inc(relu_ready, 1)
                    dve.wait_ge(exp_done, b + 2)
                    dve.tensor_scalar(flat(tail), flat(soft), 1.0, None, ALU.add).then_inc(plus_one, 1)
                    dve.wait_ge(logs_ready, b + 2)
                    own.link(dve.scalar_tensor_tensor(flat(delta[:]), flat(tail), 1.0, flat(delta[:]), ALU.is_gt, ALU.mult))
                    own.link(dve.scalar_tensor_tensor(flat(tail), flat(tail), -1.0, flat(soft), ALU.add, ALU.subtract))
                    dve.wait_ge(relu_ready, b + 2)
                    own.link(dve.tensor_tensor(flat(tail), flat(relu), flat(tail), ALU.subtract))
                    dve.tensor_tensor(flat(delta[:]), flat(delta[:]), flat(tail), ALU.add).then_inc(delta_ready, 1)
                    dve.wait_ge(delta_ready, b + 2)
                    own.step(dve.tensor_tensor(flat(du[:]), flat(delta[:]), flat(u[:]), ALU.mult))
                    inner = own.n
                    with dve.Fori(0, NS // 4) as i:
                        for j in range(4):
                            n = i * 4 + j
                            if j == 0:
                                dve.wait_ge(own_dve, own.base + inner + 1)
                            dve.wait_ge(bc_in[j], (b * 4 + i) * 16 + 16 + 1)
                            dve.wait_ge(summed[j], b * 4 + i + 1)
                            dve.tensor_tensor(h[:, j, :, :], du[:], bc[:, j, 0, :].unsqueeze(1).broadcast_to([P, ET, L]),
                                              ALU.mult).then_inc(own_dve, 1)
                            dve.wait_ge(own_dve, own.base + inner + n + 2)
                            dve.wait_ge(decayed, b * NS + n + 2)
                            for et in range(ET):
                                last = dve.tensor_tensor_scan(h[:, j, et, :], decay[:, j % 2, et, :], h[:, j, et, :], 0.0,
                                                              ALU.mult, ALU.add)
                            last.then_inc(scanned[j % 2], 1)
                    own.n += NS
                    for j in range(4):
                        dve.wait_ge(summed[j], b * 4 + 4 + 1)
                    dve.wait_ge(gate_ready, b + 2)
                    dve.tensor_tensor(flat(yT), flat(psY[:]), flat(gate[:]), ALU.mult).then_inc(y_gated, 1)
                    for lt in range(LT):
                        dve.wait_ge(y_turned, b * LT + lt + 2)
                        x_tile = g.x[:, ds(b * LT + lt, 1), :].rearrange("p a n -> p (a n)")
                        dve.tensor_tensor(x_tile, x_tile, psA[:, lt, :], ALU.add).then_inc(added, 1)
                own.turns_over(B)

            @block.gpsimd
            def _(pool):
                with pool.Fori(0, B * NS // 4) as i:
                    for j in range(4):
                        pool.wait_ge(scanned[j % 2], i * 2 + j // 2 + 2)
                        pool.tensor_tensor(h[:, j, :, :], h[:, j, :, :], bc[:, j, 1, :].unsqueeze(1).broadcast_to([P, ET, L]),
                                           ALU.mult).then_inc(weighted[j], 1)



def experts_wide(nc, g, name, E, C, F, w13, w2):
    CT, FT = C // P, F // P
    with Stage(nc, name) as st:
        idx = st.sb("idx", [P, 2, CT], I32)
        wa = st.sb("wa", [P, 2, KD, 2 * F])
        wb = st.sb("wb", [P, 2, FT, D])
        xg = st.sb("xg", [P, 2, CT, D])
        xgT = st.sb("xgT", [P, 2, KD, C])
        act_g = st.sb("act_g", [P, 2, C])
        hT = st.sb("hT", [P, FT, C])
        out = st.sb("out", [P, 2, CT, D])
        psT = st.ps("psT", [P, 2, C])
        psG = st.ps("psG", [P, 2 * FT, C])
        psO = st.ps("psO", [P, 2, D])
        own_act = st.sem("own_act")
        idx_in = st.sems_of("idx_in", 2)
        w_in = st.sems_of("w_in", 2)
        gathered = [g.pool_sem(f"{name}_gathered{i}") for i in range(2)]
        pool_tick = st.sem("pool_tick")
        turned = st.sem("turned")
        xgT_ready = st.sem("xgT_ready")
        gated = st.sem("gated")
        silu_done = st.sem("silu_done")
        h_ready = st.sem("h_ready")
        down = st.sem("down")
        out_ready = st.sem("out_ready")
        stored = st.sems_of("stored", 2)
        table = g.slot_token[0:E * C].rearrange("(e p j) a -> p e (j a)", p=P, j=CT)
        rows_out = g.slot_rows[0:E * C, :].rearrange("(e p j) n -> p e (j n)", p=P, j=CT)

        with st.block() as block:

            @block.sync
            def _(sp):
                def load(e, s):
                    sp.dma_start(idx[:, s, :], table[:, ds(e, 1), :].rearrange("p a j -> p (a j)")).then_inc(idx_in[s], 16)
                    sp.dma_start(wa[:, s, :, :], w13[ds(e, 1), :, :].rearrange("e (k p) n -> p (e k) n", p=P)).then_inc(w_in[s], 16)
                    sp.dma_start(wb[:, s, :, :], w2[ds(e, 1), :, :].rearrange("e (k p) n -> p (e k) n", p=P)).then_inc(w_in[s], 16)

                def store(e, s, done):
                    sp.wait_ge(out_ready, done * CT + 1)
                    sp.dma_start(rows_out[:, ds(e, 1), :].rearrange("p a n -> p (a n)"),
                                 out[:, s, :, :].rearrange("p j n -> p (j n)")).then_inc(stored[s], 16)

                for s in range(2):
                    load(s, s)
                with sp.Fori(1, E // 2) as i:
                    for s in range(2):
                        sp.wait_ge(down, (i * 2 + s - 1) * CT + 1)
                        load(i * 2 + s, s)
                        store(i * 2 + s - 2, s, i * 2 + s - 1)
                for s in range(2):
                    store(E - 2 + s, s, E - 1 + s)
                for s in range(2):
                    sp.wait_ge(stored[s], 16 * (E // 2) + 1)

            @block.gpsimd
            def _(pool):
                with pool.Fori(0, E // 2) as i:
                    for s in range(2):
                        pool.wait_ge(idx_in[s], i * 16 + 16 + 1)
                        pool.wait_ge(turned, i * 8 + 1)
                        take_wait(pool, pool_tick)
                        for j in range(CT):
                            pool.indirect_dma_start(xg[:, s, j, :], None, g.z_rows,
                                                    bass.IndirectOffsetOnAxis(ap=idx[:, s, j:j + 1], axis=0)).then_inc(gathered[s], 16)

            def turns(eng, first, body):
                first(0, 0)
                with eng.Fori(0, E // 2 - 1) as i:
                    for s in range(2):
                        body(i * 2 + s, s, True)
                body(E - 2, 0, True)
                body(E - 1, 1, False)

            @block.tensor
            def _(pe):
                def turn(e, s):
                    pe.wait_ge(gathered[s], (e + 2 - s) * 8 * CT)
                    for k in range(KD):
                        pe.wait_ge(xgT_ready, e * KD + (k if k else 1))
                        for j in range(CT):
                            last = pe.transpose(psT[:, k % 2, j * P:(j + 1) * P], xg[:, s, j, k * P:(k + 1) * P], g.ident[:])
                        last.then_inc(turned, 1)

                def body(e, s, more):
                    pe.wait_ge(w_in[s], (e + 2 - s) * 16 + 1)
                    pe.wait_ge(h_ready, e * FT + 1)
                    for f in range(FT):
                        for half in range(2):
                            for k in range(KD):
                                if f == half == 0:
                                    pe.wait_ge(xgT_ready, e * KD + k + 2)
                                last = pe.matmul(psG[:, half * FT + f, :], wa[:, s, k, (half * FT + f) * P:(half * FT + f + 1) * P],
                                                 xgT[:, s, k, :], start=(k == 0), stop=(k == KD - 1))
                            last.then_inc(gated, 1)
                    if more:
                        turn(e + 1, 1 - s)
                    pe.wait_ge(h_ready, (e + 1) * FT + 1)
                    for j in range(CT):
                        pe.wait_ge(out_ready, e * CT + (j if j else 1))
                        for f in range(FT):
                            last = pe.matmul(psO[:, j % 2, :], hT[:, f, j * P:(j + 1) * P], wb[:, s, f, :],
                                             start=(f == 0), stop=(f == FT - 1))
                        last.then_inc(down, 1)

                turns(pe, turn, body)

            @block.scalar
            def _(act):
                def take(e, s):
                    for k in range(KD):
                        act.wait_ge(turned, e * KD + k + 2)
                        act.activation(xgT[:, s, k, :], psT[:, k % 2, :], ACT.Copy).then_inc(xgT_ready, 1)

                def body(e, s, more):
                    for f in range(FT):
                        act.wait_ge(gated, e * 2 * FT + 2 * f + 2)
                        act.wait_ge(h_ready, e * FT + 1)
                        act.activation(act_g[:, f, :], psG[:, f, :], ACT.Silu).then_inc(silu_done, 1)
                    if more:
                        take(e + 1, 1 - s)

                turns(act, take, body)

            @block.vector
            def _(dve):
                def body(e, s, more):
                    for f in range(FT):
                        dve.wait_ge(gated, e * 2 * FT + 2 * f + 3)
                        dve.wait_ge(silu_done, e * FT + f + 2)
                        dve.wait_ge(down, e * CT + 1)
                        dve.tensor_tensor(hT[:, f, :], act_g[:, f, :], psG[:, FT + f, :], ALU.mult).then_inc(h_ready, 1)
                    dve.wait_ge(stored[s], (e - s) * 8 + 1)
                    for j in range(CT):
                        dve.wait_ge(down, e * CT + j + 2)
                        dve.tensor_copy(out[:, s, j, :], psO[:, j % 2, :]).then_inc(out_ready, 1)

                turns(dve, lambda e, s: None, body)


def combine(nc, g, name, slots, K, keep_norm):
    with Stage(nc, name) as st:
        rows = st.sb("rows", [P, 2, K, D])
        idx = st.sb("idx", [P, 2, K], U32)
        z = st.sb("z", [P, D])
        own_dve = st.sem("own_dve")
        idx_ready = st.sem("idx_ready")
        gathered = [g.pool_sem(f"{name}_gathered{i}") for i in range(2)]
        used = st.sems_of("used", 2)
        pool_tick = st.sem("pool_tick")
        per = K - 1 + (2 if keep_norm else 0)
        with st.block() as block:

            @block.gpsimd
            def _(pool):
                with pool.Fori(0, NT // 2) as i:
                    for s in range(2):
                        pool.wait_ge(used[s], i + 1)
                        pool.tensor_copy(idx[:, s, :], g.slot_of[:, ds(i * 2 + s, 1), 0:K].rearrange("p a k -> p (a k)")).then_inc(idx_ready, 1)
                        pool.wait_ge(idx_ready, i * 2 + s + 2)
                        take_wait(pool, pool_tick)
                        for k in range(K):
                            pool.indirect_dma_start(rows[:, s, k, :], None, g.slot_rows[0:slots, :],
                                                    bass.IndirectOffsetOnAxis(ap=idx[:, s, k:k + 1], axis=0)).then_inc(gathered[s], 16)

            @block.vector
            def _(dve):
                own = Own(dve, own_dve)
                with dve.Fori(0, NT // 2) as i:
                    own.turn(i, 2 * per)
                    for s in range(2):
                        t = i * 2 + s
                        x_tile = g.x[:, ds(t, 1), :].rearrange("p a n -> p (a n)")
                        if keep_norm:
                            own.link(dve.tensor_scalar(z[:], x_tile, g.mean[:, ds(t, 1)], g.ln_rstd[:, ds(t, 1)], ALU.subtract, ALU.mult))
                            own.link(dve.tensor_tensor(x_tile, x_tile, z[:], ALU.add))
                        dve.wait_ge(gathered[s], (i + 1) * 16 * K)
                        for k in range(K):
                            out = dve.scalar_tensor_tensor(x_tile, rows[:, s, k, :],
                                                           g.weight_of[:, ds(t, 1), k:k + 1].rearrange("p a k -> p (a k)"),
                                                           x_tile, ALU.mult, ALU.add)
                            if k < K - 1:
                                own.link(out)
                            else:
                                out.then_inc(used[s], 1)
                own.turns_over(NT // 2)


def experts_narrow(nc, g, name, E, C, F, w_gate, w_up, w_down):
    FH = F // 2
    with Stage(nc, name) as st:
        idx = st.sb("idx", [P, 2, 1], I32)
        wa = st.sb("wa", [P, 2, KD, 2 * F])
        wb = st.sb("wb", [FH, 2, 2, D])
        xg = st.sb("xg", [P, 2, D])
        xgT = st.sb("xgT", [P, 2, KD, P])
        act_g = st.sb("act_g", [P, F])
        hid = st.sb("hid", [P, F])
        hT = st.sb("hT", [FH, 2, P])
        out = st.sb("out", [P, 2, D])
        psT = st.ps("psT", [P, 2, D])
        psG = st.ps("psG", [P, 2, 512])
        psH = st.ps("psH", [P, 512])
        psO = st.ps("psO", [P, 2, D])
        idx_in = st.sems_of("idx_in", 2)
        w_in = st.sems_of("w_in", 2)
        gathered = [g.pool_sem(f"{name}_gathered{i}") for i in range(2)]
        pool_tick = st.sem("pool_tick")
        turned = st.sem("turned")
        xgT_ready = st.sem("xgT_ready")
        gated = st.sem("gated")
        silu_done = st.sem("silu_done")
        hid_ready = st.sem("hid_ready")
        hid_turned = st.sem("hid_turned")
        hT_ready = st.sem("hT_ready")
        down = st.sem("down")
        out_ready = st.sem("out_ready")
        stored = st.sems_of("stored", 2)
        table = g.slot_token[0:E * C].rearrange("(e p) a -> p e a", p=P)
        rows_out = g.slot_rows[0:E * C, :].rearrange("(e p) n -> p e n", p=P)

        with st.block() as block:

            @block.sync
            def _(sp):
                def load(e, s):
                    sp.dma_start(idx[:, s, :], table[:, ds(e, 1), :].rearrange("p e a -> p (e a)")).then_inc(idx_in[s], 16)
                    sp.dma_start(wa[:, s, :, 0:F], w_gate[ds(e, 1), :, :].rearrange("e (k p) n -> p (e k) n", p=P)).then_inc(w_in[s], 16)
                    sp.dma_start(wa[:, s, :, F:2 * F], w_up[ds(e, 1), :, :].rearrange("e (k p) n -> p (e k) n", p=P)).then_inc(w_in[s], 16)
                    sp.dma_start(wb[:, s, :, :], w_down[ds(e, 1), :, :].rearrange("e (k p) n -> p (e k) n", p=FH)).then_inc(w_in[s], 16)

                def store(e, s, done):
                    sp.wait_ge(out_ready, done + 1)
                    sp.dma_start(rows_out[:, ds(e, 1), :].rearrange("p a n -> p (a n)"), out[:, s, :]).then_inc(stored[s], 16)

                for s in range(2):
                    load(s, s)
                with sp.Fori(1, E // 2) as i:
                    for s in range(2):
                        sp.wait_ge(down, i * 2 + s)
                        load(i * 2 + s, s)
                        store(i * 2 + s - 2, s, i * 2 + s - 1)
                for s in range(2):
                    store(E - 2 + s, s, E - 1 + s)
                for s in range(2):
                    sp.wait_ge(stored[s], 16 * (E // 2) + 1)

            @block.gpsimd
            def _(pool):
                with pool.Fori(0, E // 2) as i:
                    for s in range(2):
                        pool.wait_ge(idx_in[s], i * 16 + 16 + 1)
                        pool.wait_ge(turned, i * 2 + 1)
                        take_wait(pool, pool_tick)
                        pool.indirect_dma_start(xg[:, s, :], None, g.z_rows,
                                                bass.IndirectOffsetOnAxis(ap=idx[:, s, 0:1], axis=0)).then_inc(gathered[s], 16)

            @block.tensor
            def _(pe):
                with pe.Fori(0, E // 2) as i:
                    for s in range(2):
                        e = i * 2 + s
                        pe.wait_ge(gathered[s], i * 16 + 16)
                        pe.wait_ge(xgT_ready, i * 2 + 1)
                        for k in range(KD):
                            last = pe.transpose(psT[:, s, k * P:(k + 1) * P], xg[:, s, k * P:(k + 1) * P], g.ident[:])
                        last.then_inc(turned, 1)
                        pe.wait_ge(w_in[s], i * 48 + 48 + 1)
                        pe.wait_ge(xgT_ready, e + 2)
                        pe.wait_ge(hid_ready, i * 2 + 1)
                        for k in range(KD):
                            last = pe.matmul(psG[:, s, 0:2 * F], xgT[:, s, k, :], wa[:, s, k, :], start=(k == 0), stop=(k == KD - 1))
                        last.then_inc(gated, 1)
                        pe.wait_ge(hid_ready, e + 2)
                        for f in range(2):
                            last = pe.transpose(psH[0:FH, f * P:(f + 1) * P], hid[:, f * FH:(f + 1) * FH], g.ident[:])
                        last.then_inc(hid_turned, 1)
                        pe.wait_ge(hT_ready, e + 2)
                        pe.wait_ge(out_ready, i * 2 + 1)
                        for f in range(2):
                            last = pe.matmul(psO[:, s, :], hT[:, f, :], wb[:, s, f, :], start=(f == 0), stop=(f == 1))
                        last.then_inc(down, 1)

            @block.scalar
            def _(act):
                with act.Fori(0, E // 2) as i:
                    for s in range(2):
                        e = i * 2 + s
                        act.wait_ge(turned, e + 2)
                        act.wait_ge(gated, i * 2 + 1)
                        act.activation(xgT[:, s, :, :].rearrange("p k n -> p (k n)"), psT[:, s, :], ACT.Copy).then_inc(xgT_ready, 1)
                        act.wait_ge(gated, e + 2)
                        act.wait_ge(hid_ready, e + 1)
                        act.activation(act_g[:], psG[:, s, 0:F], ACT.Silu).then_inc(silu_done, 1)

            @block.vector
            def _(dve):
                with dve.Fori(0, E // 2) as i:
                    for s in range(2):
                        e = i * 2 + s
                        dve.wait_ge(silu_done, e + 2)
                        dve.wait_ge(hid_turned, e + 1)
                        dve.tensor_tensor(hid[:], act_g[:], psG[:, s, F:2 * F], ALU.mult).then_inc(hid_ready, 1)
                        dve.wait_ge(hid_turned, e + 2)
                        dve.wait_ge(down, e + 1)
                        dve.tensor_copy(hT[:].rearrange("p f n -> p (f n)"), psH[0:FH, 0:2 * P]).then_inc(hT_ready, 1)
                        dve.wait_ge(stored[s], i * 16 + 1)
                        dve.wait_ge(down, e + 2)
                        dve.tensor_copy(out[:, s, :], psO[:, s, :]).then_inc(out_ready, 1)



def shared_expert(nc, g, name, zT, F, w_gate, w_up, w_down):
    FT, G = F // P, 512
    with Stage(nc, name) as st:
        wg = st.sb("wg", [P, KD, F])
        wu = st.sb("wu", [P, KD, F])
        wd = st.sb("wd", [P, FT, D])
        act_g = st.sb("act_g", [P, FT, G])
        hT = st.sb("hT", [P, FT, G])
        psG = st.ps("psG", [P, 2, FT, G])
        psO = st.ps("psO", [P, 2, D])
        w_in = st.sem("w_in")
        gated = st.sem("gated")
        silu_done = st.sem("silu_done")
        h_ready = st.sem("h_ready")
        down = st.sem("down")
        added = st.sem("added")
        GT = G // P
        with st.block() as block:

            @block.sync
            def _(sp):
                for dst, src in ((wg, w_gate), (wu, w_up), (wd, w_down)):
                    sp.dma_start(dst[:], channels_first(src)).then_inc(w_in, 16)

            @block.tensor
            def _(pe):
                pe.wait_ge(w_in, 49)
                with pe.Fori(0, T // G) as i:
                    pe.wait_ge(h_ready, i * FT + 1)
                    for f in range(FT):
                        for half, w in enumerate((wg, wu)):
                            for k in range(KD):
                                last = pe.matmul(psG[:, half, f, :], w[:, k, f * P:(f + 1) * P], zT[:, k, ds(i * G, G)],
                                                 start=(k == 0), stop=(k == KD - 1))
                            last.then_inc(gated, 1)
                    pe.wait_ge(h_ready, (i + 1) * FT + 1)
                    for j in range(GT):
                        pe.wait_ge(added, (i * GT + j - 1 if j else i * GT) + 1)
                        for f in range(FT):
                            last = pe.matmul(psO[:, j % 2, :], hT[:, f, j * P:(j + 1) * P], wd[:, f, :],
                                             start=(f == 0), stop=(f == FT - 1))
                        last.then_inc(down, 1)

            @block.scalar
            def _(act):
                with act.Fori(0, T // G) as i:
                    for f in range(FT):
                        act.wait_ge(gated, i * 2 * FT + 2 * f + 2)
                        act.wait_ge(h_ready, i * FT + 1)
                        act.activation(act_g[:, f, :], psG[:, 0, f, :], ACT.Silu).then_inc(silu_done, 1)

            @block.vector
            def _(dve):
                with dve.Fori(0, T // G) as i:
                    for f in range(FT):
                        dve.wait_ge(gated, i * 2 * FT + 2 * f + 2 + 1)
                        dve.wait_ge(silu_done, i * FT + f + 2)
                        dve.wait_ge(down, i * GT + 1)
                        dve.tensor_tensor(hT[:, f, :], act_g[:, f, :], psG[:, 1, f, :], ALU.mult).then_inc(h_ready, 1)
                    for j in range(GT):
                        dve.wait_ge(down, i * GT + j + 2)
                        x_tile = g.x[:, ds(i * GT + j, 1), :].rearrange("p a n -> p (a n)")
                        dve.tensor_tensor(x_tile, x_tile, psO[:, j % 2, :], ALU.add).then_inc(added, 1)


class SoftRouter:

    def __init__(self, g, E, n, gateT, bias):
        self.g, self.E, self.n, self.gateT, self.bias = g, E, n, gateT, bias
        self.STEPS = 11

    def allocate(self, st):
        E = self.E
        self.wg = st.sb("wg", [P, KD, E])
        self.bias_sb = st.sb("bias", [P, E])
        self.iota = st.sb("iota", [P, E])
        self.iota_i = st.sb("iota_i", [P, E], I32)
        self.logits = st.sb("logits", [P, 2, E])
        self.best = st.sb("best", [P, 2, 8])
        self.which = st.sb("which", [P, 2, 8], U32)
        self.which_f = st.sb("which_f", [P, 2, 8])
        self.e_all = st.sb("e_all", [P, 2, E])
        self.total = st.sb("total", [P, 2, 2])
        self.onehot = st.sb("onehot", [P, 2, self.n, E])
        self.mask = st.sb("mask", [P, 2, E])
        self.psR = st.ps("psR", [P, 2, 512])
        self.zTs_ready = st.sem("zTs_ready")
        self.router_in = st.sem("router_in")
        self.iotas = st.sem("iotas")
        self.tick = st.sem("tick")
        self.logits_done = st.sem("logits_done")
        self.clamped = st.sem("clamped")
        self.exps_done = st.sem("exps_done")
        self.chosen = st.sem("chosen")

    def load(self, sp):
        sp.dma_start(self.wg[:], self.gateT).then_inc(self.router_in, 16)
        sp.dma_start(self.bias_sb[:], self.bias.rearrange("(a n) -> a n", a=1).broadcast_to([P, self.E])).then_inc(self.router_in, 16)

    def prepare(self, dve, own):
        dve.wait_ge(self.iotas, 2)
        dve.wait_ge(self.router_in, 33)
        own.link(dve.tensor_copy(self.iota[:], self.iota_i[:]))

    def matmuls(self, pe, i, s, zTs):
        E = self.E
        if s == 0:
            pe.wait_ge(self.router_in, 33)
        pe.wait_ge(self.zTs_ready, i * 2 + s + 2)
        pe.wait_ge(self.chosen, i * 2 + 1)
        for k in range(KD):
            last = pe.matmul(self.psR[:, s, 0:E], zTs[:, s, k * P:(k + 1) * P], self.wg[:, k, :],
                             start=(k == 0), stop=(k == KD - 1))
        last.then_inc(self.logits_done, 1)

    def wait_for_reader(self, act, i, s):
        act.wait_ge(self.logits_done, i * 2 + 1)

    def exponentials(self, act, i, s):
        act.wait_ge(self.clamped, i * 2 + s + 2)
        act.activation(self.e_all[:, s, :], self.logits[:, s, :], ACT.Exp).then_inc(self.exps_done, 1)

    def choose(self, dve, own, i, s):
        E, n, t = self.E, self.n, i * 2 + s
        lg, top = self.logits[:, s, :], self.best[:, s, :]
        dve.wait_ge(self.logits_done, t + 2)
        own.link(dve.tensor_tensor(lg, self.psR[:, s, 0:E], self.bias_sb[:], ALU.add))
        take_wait(dve, self.tick)
        own.link(dve.max(top, lg))
        take_wait(dve, self.tick)
        own.link(dve.max_index(self.which[:, s, :], top, lg))
        own.link(dve.tensor_copy(self.which_f[:, s, :], self.which[:, s, :]))
        own.link(dve.tensor_tensor(self.onehot[:, s, :, :], self.iota[:].unsqueeze(1).broadcast_to([P, n, E]),
                                   self.which_f[:, s, 0:n].unsqueeze(2).broadcast_to([P, n, E]), ALU.is_equal))
        own.link(dve.tensor_reduce(self.mask[:, s, :], self.onehot[:, s, :, :].rearrange("p k e -> p e k"), AX.X, ALU.add))
        dve.tensor_scalar(lg, lg, top[:, 0:1], None, ALU.subtract).then_inc(self.clamped, 1)
        dve.wait_ge(self.exps_done, t + 2)
        own.link(dve.tensor_tensor(self.e_all[:, s, :], self.e_all[:, s, :], self.mask[:, s, :], ALU.mult))
        own.link(dve.tensor_reduce(self.total[:, s, 0:1], self.e_all[:, s, :], AX.X, ALU.add))
        own.link(dve.reciprocal(self.total[:, s, 1:2], self.total[:, s, 0:1]))
        own.link(dve.tensor_scalar(self.e_all[:, s, :], self.e_all[:, s, :], self.total[:, s, 1:2], None, ALU.mult))
        own.step(dve.tensor_copy(self.g.weight_of[:, ds(t, 1), 0:E], self.e_all[:, s:s + 1, :]))
        dve.wait_ge(self.exps_done, t + 2)
        dve.tensor_copy(self.which_f[:, s, :], self.which[:, s, :]).then_inc(self.chosen, 1)

    def scatter(self, pool):
        pool.iota(self.iota_i[:], [[1, self.E]], base=0, channel_multiplier=0).then_inc(self.iotas, 1)


def soft_experts(nc, g, name, zT, N, F, w_gate, b_gate, w_up, b_up, w_down, b_down, s_up, sb_up, s_down, sb_down):
    FT, G, ST = F // P, 512, 512 // P
    GT, NG = G // P, T // G
    with Stage(nc, name) as st:
        wa = st.sb("wa", [P, 2, KD, 2 * F])
        wd = st.sb("wd", [P, 2, FT, D])
        cols = st.sb("cols", [P, 2, N, FT])
        cols_s = st.sb("cols_s", [P, ST])
        bd = st.sb("bd", [P, N, D])
        bs = st.sb("bs", [P, D])
        ws = st.sb("ws", [P, KD, 512])
        wsd = st.sb("wsd", [P, ST, D])
        act_g = st.sb("act_g", [P, 2, G])
        hT = st.sb("hT", [P, ST, G])
        tmp = st.sb("tmp", [P, 2, D])
        psG = st.ps("psG", [P, 2 * FT, G])
        psO = st.ps("psO", [P, 2, D])
        consts_in = st.sem("consts_in")
        w_in = st.sems_of("w_in", 2)
        gated = st.sem("gated")
        silu_done = st.sem("silu_done")
        h_ready = st.sem("h_ready")
        down = st.sem("down")
        taken = st.sem("taken")
        own_dve = st.sem("own_dve")
        s_gated = st.sem("s_gated")
        s_h = st.sem("s_h")
        s_down_done = st.sem("s_down_done")
        s_taken = st.sem("s_taken")
        with st.block() as block:

            @block.sync
            def _(sp):
                for dst, src in ((ws[:], channels_first(s_up)), (cols_s[:], sb_up), (cols[:, 0, :, :], b_gate), (cols[:, 1, :, :], b_up),
                                 (wsd[:], channels_first(s_down)), (bs[:], sb_down.rearrange("(a n) -> a n", a=1).broadcast_to([P, D])),
                                 (bd[:].rearrange("p n d -> p (n d)"), b_down.rearrange("(a n) d -> a (n d)", a=1).broadcast_to([P, N * D]))):
                    sp.dma_start(dst, src).then_inc(consts_in, 16)

                def load(e, s):
                    for dst, src, k in ((wa[:, s, :, 0:F], w_gate, P), (wa[:, s, :, F:2 * F], w_up, P), (wd[:, s, :, :], w_down, P)):
                        sp.dma_start(dst, src[ds(e, 1), :, :].rearrange("e (k p) n -> p (e k) n", p=P)).then_inc(w_in[s], 16)

                for s in range(2):
                    load(s, s)
                with sp.Fori(1, N // 2) as i:
                    for s in range(2):
                        sp.wait_ge(down, (i * 2 + s - 1) * NT + 1)
                        load(i * 2 + s, s)

            @block.tensor
            def _(pe):
                pe.wait_ge(consts_in, 113)
                with pe.Fori(0, NG) as i:
                    pe.wait_ge(s_h, i * ST + 1)
                    for f in range(ST):
                        for k in range(KD):
                            last = pe.matmul(psG[:, f, :], ws[:, k, f * P:(f + 1) * P], zT[:, k, ds(i * G, G)],
                                             start=(k == 0), stop=(k == KD - 1))
                        last.then_inc(s_gated, 1)
                    pe.wait_ge(s_h, (i + 1) * ST + 1)
                    for j in range(GT):
                        pe.wait_ge(s_taken, (i * GT + j - 1 if j else i * GT) + 1)
                        for f in range(ST):
                            last = pe.matmul(psO[:, j % 2, :], hT[:, f, j * P:(j + 1) * P], wsd[:, f, :],
                                             start=(f == 0), stop=(f == ST - 1))
                        last.then_inc(s_down_done, 1)
                pe.wait_ge(s_taken, NT + 1)
                with pe.Fori(0, N // 2) as e2:
                    for s in range(2):
                        with pe.Fori(0, NG) as i:
                            pe.wait_ge(w_in[s], e2 * 48 + 48 + 1)
                            u = (e2 * 2 + s) * NG + i
                            pe.wait_ge(h_ready, u * FT + 1)
                            for f in range(FT):
                                for half in range(2):
                                    for k in range(KD):
                                        last = pe.matmul(psG[:, half * FT + f, :], wa[:, s, k, half * F + f * P:half * F + (f + 1) * P],
                                                         zT[:, k, ds(i * G, G)], start=(k == 0), stop=(k == KD - 1))
                                    last.then_inc(gated, 1)
                            pe.wait_ge(h_ready, (u + 1) * FT + 1)
                            for j in range(GT):
                                pe.wait_ge(taken, (u * GT + j - 1 if j else u * GT) + 1)
                                for f in range(FT):
                                    last = pe.matmul(psO[:, j % 2, :], hT[:, f, j * P:(j + 1) * P], wd[:, s, f, :],
                                                     start=(f == 0), stop=(f == FT - 1))
                                last.then_inc(down, 1)

            @block.scalar
            def _(act):
                act.wait_ge(consts_in, 113)
                with act.Fori(0, NG) as i:
                    for f in range(ST):
                        act.wait_ge(s_gated, i * ST + f + 2)
                        act.wait_ge(s_down_done, i * GT + 1)
                        act.activation(hT[:, f, :], psG[:, f, :], ACT.Silu, bias=cols_s[:, f:f + 1]).then_inc(s_h, 1)
                with act.Fori(0, N) as e:
                    with act.Fori(0, NG) as i:
                        u = e * NG + i
                        for f in range(FT):
                            act.wait_ge(gated, u * 2 * FT + 2 * f + 2)
                            act.wait_ge(h_ready, u * FT + 1)
                            act.activation(act_g[:, f, :], psG[:, f, :], ACT.Silu,
                                           bias=cols[:, 0, ds(e, 1), f:f + 1].rearrange("p a b -> p (a b)")).then_inc(silu_done, 1)

            @block.vector
            def _(dve):
                own = Own(dve, own_dve)
                dve.wait_ge(consts_in, 113)
                with dve.Fori(0, NT // 2) as i:
                    own.turn(i, 2)
                    for s in range(2):
                        dve.wait_ge(s_down_done, i * 2 + s + 2)
                        x_tile = g.x[:, ds(i * 2 + s, 1), :].rearrange("p a n -> p (a n)")
                        own.link(dve.tensor_tensor(tmp[:, s, :], psO[:, s, :], bs[:], ALU.add))
                        dve.tensor_tensor(x_tile, x_tile, tmp[:, s, :], ALU.add).then_inc(s_taken, 1)
                own.turns_over(NT // 2)
                with dve.Fori(0, N) as e:
                    with dve.Fori(0, NG) as i:
                        u = e * NG + i
                        for f in range(FT):
                            dve.wait_ge(gated, u * 2 * FT + 2 * f + 2 + 1)
                            dve.wait_ge(silu_done, u * FT + f + 2)
                            dve.wait_ge(down, u * GT + 1)
                            dve.scalar_tensor_tensor(hT[:, f, :], psG[:, FT + f, :],
                                                     cols[:, 1, ds(e, 1), f:f + 1].rearrange("p a b -> p (a b)"),
                                                     act_g[:, f, :], ALU.add, ALU.mult).then_inc(h_ready, 1)
                        for j in range(GT):
                            n = u * GT + j
                            dve.wait_ge(down, n + 2)
                            dve.tensor_tensor(tmp[:, j % 2, :], psO[:, j % 2, :], bd[:, ds(e, 1), :].rearrange("p a n -> p (a n)"),
                                              ALU.add).then_inc(taken, 1)
                            dve.wait_ge(taken, n + 2)
                            x_tile = g.x[:, ds(i * GT + j, 1), :].rearrange("p a n -> p (a n)")
                            dve.scalar_tensor_tensor(x_tile, tmp[:, j % 2, :],
                                                     g.weight_of[:, ds(i * GT + j, 1), ds(e, 1)].rearrange("p a k -> p (a k)"),
                                                     x_tile, ALU.mult, ALU.add).then_inc(own_dve, 1)



def feature_attention(nc, g, name, zT, wqT, bq, wkT, bk):
    MT = L // P
    with Stage(nc, name) as st:
        ctxT = st.sb("ctxT", [P, KC, T])
        wq = st.sb("wq", [P, KC, P])
        wk = st.sb("wk", [P, KC, P])
        bias = st.sb("bias", [P, 2])
        qkT = st.sb("qkT", [P, 2, L])
        att = st.sb("att", [P, MT, L])
        attT = st.sb("attT", [P, MT, L])
        zs = st.sb("zs", [P, KD, L])
        top = st.sb("top", [P, MT])
        den = st.sb("den", [P, MT])
        psQ = st.ps("psQ", [P, 2, L])
        psE = st.ps("psE", [P, 2, L])
        psT = st.ps("psT", [P, 2, L])
        psO = st.ps("psO", [P, 2, L])
        w_in = st.sem("w_in")
        projected = st.sem("projected")
        qk_ready = st.sem("qk_ready")
        scored = st.sem("scored")
        maxed = st.sem("maxed")
        exps = st.sem("exps")
        inverse = st.sem("inverse")
        att_ready = st.sem("att_ready")
        turned = st.sem("turned")
        attT_ready = st.sem("attT_ready")
        z_copied = st.sem("z_copied")
        mixed = st.sem("mixed")
        added = st.sem("added")
        with st.block() as block:

            @block.sync
            def _(sp):
                for dst, src in ((ctxT[:], g.ctxT), (wq[:], wqT), (wk[:], wkT), (bias[:, 0:1], bq.rearrange("(n a) -> n a", a=1)),
                                 (bias[:, 1:2], bk.rearrange("(n a) -> n a", a=1))):
                    sp.dma_start(dst, src).then_inc(w_in, 16)

            @block.tensor
            def _(pe):
                pe.wait_ge(w_in, 81)
                with pe.Fori(0, B) as b:
                    pe.wait_ge(qk_ready, b * 2 + 1)
                    for half, w in enumerate((wq, wk)):
                        for k in range(KC):
                            last = pe.matmul(psQ[:, half, :], w[:, k, :], ctxT[:, k, ds(b * L, L)], start=(k == 0), stop=(k == KC - 1))
                        last.then_inc(projected, 1)
                    pe.wait_ge(qk_ready, b * 2 + 2 + 1)
                    for j in range(MT):
                        pe.wait_ge(exps, (b * MT + j - 1 if j else b * MT) + 1)
                        pe.matmul(psE[:, j % 2, :], qkT[:, 0, j * P:(j + 1) * P], qkT[:, 1, :], start=True, stop=True).then_inc(scored, 1)
                    pe.wait_ge(att_ready, (b + 1) * MT + 1)
                    for k in range(MT):
                        pe.wait_ge(attT_ready, (b * MT + k - 1 if k else b * MT) + 1)
                        for j in range(MT):
                            last = pe.transpose(psT[:, k % 2, j * P:(j + 1) * P], att[:, j, k * P:(k + 1) * P], g.ident[:])
                        last.then_inc(turned, 1)
                    pe.wait_ge(attT_ready, (b + 1) * MT + 1)
                    pe.wait_ge(z_copied, b + 2)
                    for j in range(LT):
                        pe.wait_ge(added, (b * LT + j - 1 if j else b * LT) + 1)
                        for k in range(MT):
                            last = pe.matmul(psO[:, j % 2, :], zs[:, k, j * P:(j + 1) * P], attT[:, k, :], start=(k == 0), stop=(k == MT - 1))
                        last.then_inc(mixed, 1)

            @block.scalar
            def _(act):
                act.wait_ge(w_in, 81)
                with act.Fori(0, B) as b:
                    for half in range(2):
                        act.wait_ge(projected, b * 2 + half + 2)
                        act.wait_ge(scored, b * MT + 1)
                        act.activation(qkT[:, half, :], psQ[:, half, :], ACT.Identity, bias=bias[:, half:half + 1]).then_inc(qk_ready, 1)
                    for j in range(MT):
                        act.wait_ge(maxed, b * MT + j + 2)
                        act.wait_ge(turned, b * MT + 1)
                        act.activation(att[:, j, :], psE[:, j % 2, :], ACT.Exp, bias=top[:, j:j + 1], accum_out=den[:, j:j + 1]).then_inc(exps, 1)
                    for k in range(MT):
                        act.wait_ge(turned, b * MT + k + 2)
                        act.wait_ge(mixed, b * LT + 1)
                        act.activation(attT[:, k, :], psT[:, k % 2, :], ACT.Copy).then_inc(attT_ready, 1)

            @block.vector
            def _(dve):
                with dve.Fori(0, B) as b:
                    for j in range(MT):
                        dve.wait_ge(scored, b * MT + j + 2)
                        dve.wait_ge(exps, b * MT + 1)
                        dve.tensor_reduce(top[:, j:j + 1], psE[:, j % 2, :], AX.X, ALU.max, negate=True).then_inc(maxed, 1)
                    for j in range(MT):
                        dve.wait_ge(exps, b * MT + j + 2)
                        dve.reciprocal(den[:, j:j + 1], den[:, j:j + 1]).then_inc(inverse, 1)
                        dve.wait_ge(inverse, b * MT + j + 2)
                        dve.tensor_scalar(att[:, j, :], att[:, j, :], den[:, j:j + 1], None, ALU.mult).then_inc(att_ready, 1)
                    for j in range(LT):
                        dve.wait_ge(mixed, b * LT + j + 2)
                        x_tile = g.x[:, ds(b * LT + j, 1), :].rearrange("p a n -> p (a n)")
                        dve.tensor_tensor(x_tile, x_tile, psO[:, j % 2, :], ALU.add).then_inc(added, 1)

            @block.gpsimd
            def _(pool):
                with pool.Fori(0, B) as b:
                    pool.wait_ge(mixed, b * LT + 1)
                    pool.tensor_copy(zs[:], zT[:, :, ds(b * L, L)]).then_inc(z_copied, 1)



def cross_attention(nc, g, name, zT, wq, wk, wv, wo, gq, gk):
    H, J = 16, L // P
    SCALE = P ** -0.5
    with Stage(nc, name) as st:
        ctxT = st.sb("ctxT", [P, KC, T])
        wo_sb = st.sb("wo", [P, H, D])
        w_head = st.sb("w_head", [P, 2, 8, P])
        gains = st.sb("gains", [P, 2])
        gain = st.sb("gain", [P, 1])
        eps = st.sb("eps", [P, 1])
        cs = st.sb("cs", [P, KC, L])
        qT = st.sb("qT", [P, 2, L])
        kT = st.sb("kT", [P, 2, L])
        v = st.sb("v", [P, 2, J, P])
        sq = st.sb("sq", [P, 2, L])
        rk = st.sb("rk", [P, L])
        rq = st.sb("rq", [P, 2, J])
        top = st.sb("top", [P, J])
        den = st.sb("den", [P, J])
        prob = st.sb("prob", [P, J, L])
        probT = st.sb("probT", [P, J, L])
        oT = st.sb("oT", [P, H, L])
        psP = st.ps("psP", [P, 2, L])
        psV = st.ps("psV", [P, J, P])
        psK = st.ps("psK", [P, L])
        psS = st.ps("psS", [P, 2, L])
        psT = st.ps("psT", [P, 2, L])
        w_in = st.sem("w_in")
        own_dve = st.sem("own_dve")
        own_act = st.sem("own_act")
        head_in = st.sems_of("head_in", 2)
        projected = st.sem("projected")
        squared = st.sem("squared")
        copied = st.sem("copied")
        summed = st.sem("summed")
        rk_ready = st.sem("rk_ready")
        front_done = st.sem("front_done")
        scored = st.sem("scored")
        maxed = st.sem("maxed")
        exps = st.sem("exps")
        inverse = st.sem("inverse")
        prob_ready = st.sem("prob_ready")
        turned = st.sem("turned")
        probT_ready = st.sem("probT_ready")
        mixed = st.sem("mixed")
        out_copied = st.sem("out_copied")
        ctx_copied = st.sem("ctx_copied")
        y_done = st.sem("y_done")
        added = st.sem("added")
        q_taken = st.sem("q_taken")
        kT_ready = st.sem("kT_ready")
        reduced = st.sem("reduced")

        with st.block() as block:

            @block.sync
            def _(sp):
                for dst, src in ((ctxT[:], g.ctxT), (wo_sb[:], channels_first(wo)), (gains[:, 0:1], gq.rearrange("(n a) -> n a", a=1)),
                                 (gains[:, 1:2], gk.rearrange("(n a) -> n a", a=1))):
                    sp.dma_start(dst, src).then_inc(w_in, 16)
                with sp.Fori(0, B) as b:
                    with sp.Fori(0, H // 2) as i:
                        for s in range(2):
                            sp.wait_ge(projected, (b * H + i * 2) * 3 + 1)
                            for k0, k1, w in ((0, 4, wq), (4, 6, wk), (6, 8, wv)):
                                sp.dma_start(w_head[:, s, k0:k1, :], w[:, :, ds(i * (2 * P) + s * P, P)]).then_inc(head_in[s], 16)

            def turns(eng, front, back, end):
                with eng.Fori(0, B) as b:
                    front(b, b * H, 0)
                    with eng.Fori(0, H // 2 - 1) as i:
                        for s in range(2):
                            back(b, i * 2 + s, b * H + i * 2 + s, s, True)
                    back(b, H - 2, b * H + H - 2, 0, True)
                    back(b, H - 1, b * H + H - 1, 1, False)
                    end(b)

            @block.tensor
            def _(pe):
                pe.wait_ge(w_in, 65)

                def project_q(b, m, s):
                    pe.wait_ge(head_in[s], (m + 2) * 24 + 1 if s == 0 else (m + 1) * 24 + 1)
                    for k in range(KD):
                        last = pe.matmul(psP[:, 0, :], w_head[:, s, k, :], zT[:, k, ds(b * L, L)], start=(k == 0), stop=(k == KD - 1))
                    last.then_inc(projected, 1)

                def project_kv(b, m, s):
                    pe.wait_ge(kT_ready, m + 1)
                    for k in range(KC):
                        last = pe.matmul(psP[:, 1, :], w_head[:, s, 4 + k, :], ctxT[:, k, ds(b * L, L)], start=(k == 0), stop=(k == KC - 1))
                    last.then_inc(projected, 1)
                    pe.wait_ge(ctx_copied, b + 2)
                    pe.wait_ge(rk_ready, m * 2 + 1)
                    for j in range(J):
                        for k in range(KC):
                            last = pe.matmul(psV[:, j, :], cs[:, k, j * P:(j + 1) * P], w_head[:, s, 6 + k, :], start=(k == 0), stop=(k == KC - 1))
                    last.then_inc(projected, 1)
                    pe.wait_ge(squared, m * 2 + 3)
                    pe.matmul(psK[:], g.ones[:], sq[:, 1, :], start=True, stop=True).then_inc(summed, 1)

                def sum_q(m):
                    pe.wait_ge(copied, m + 2)
                    for j in range(J):
                        last = pe.matmul(psV[:, 0, j:j + 1], sq[:, 0, j * P:(j + 1) * P], g.ones[:, 0:1], start=True, stop=True)
                    last.then_inc(summed, 1)

                def front(b, m, s):
                    project_q(b, m, s)
                    project_kv(b, m, s)
                    sum_q(m)

                def scores(m, s, tiles):
                    for j in tiles:
                        pe.wait_ge(exps, m * J + j if j else m * J + 1)
                        pe.matmul(psS[:, j % 2, :], qT[:, s, j * P:(j + 1) * P], kT[:, s, :], start=True, stop=True).then_inc(scored, 1)

                def back(b, h, m, s, more):
                    pe.wait_ge(q_taken, m + 2)
                    pe.wait_ge(kT_ready, m + 2)
                    scores(m, s, (0, 1))
                    if more:
                        pe.wait_ge(out_copied, m + 1)
                        project_q(b, m + 1, 1 - s)
                    scores(m, s, (2, 3))
                    if more:
                        project_kv(b, m + 1, 1 - s)
                    pe.wait_ge(prob_ready, (m + 1) * J + 1)
                    for k in range(J):
                        pe.wait_ge(probT_ready, m * J + k if k else m * J + 1)
                        for j in range(J):
                            last = pe.transpose(psT[:, k % 2, j * P:(j + 1) * P], prob[:, j, k * P:(k + 1) * P], g.ident[:])
                        last.then_inc(turned, 1)
                    if more:
                        sum_q(m + 1)
                        pe.wait_ge(q_taken, m + 3)
                    for k in range(J):
                        pe.wait_ge(probT_ready, m * J + k + 2)
                        last = pe.matmul(psP[:, 0, :], v[:, s, k, :], probT[:, k, :], start=(k == 0), stop=(k == J - 1))
                    last.then_inc(mixed, 1)

                def end(b):
                    pe.wait_ge(out_copied, (b + 1) * H + 1)
                    for j in range(J):
                        pe.wait_ge(added, b * J + j if j else b * J + 1)
                        for h in range(H):
                            last = pe.matmul(psS[:, j % 2, :], oT[:, h, j * P:(j + 1) * P], wo_sb[:, h, :], start=(h == 0), stop=(h == H - 1))
                        last.then_inc(y_done, 1)
                    pe.wait_ge(added, (b + 1) * J + 1)

                turns(pe, front, back, end)

            @block.scalar
            def _(act):
                act.wait_ge(own_dve, 3)
                act.preload_act_table_set("natural_log_exp_and_others")

                def take_q(m, s):
                    act.wait_ge(projected, m * 3 + 2)
                    act.wait_ge(summed, m * 2 + 1)
                    act.activation(sq[:, 0, :], psP[:, 0, :], ACT.Square).then_inc(squared, 1)
                    act.activation(qT[:, s, :], psP[:, 0, :], ACT.Copy, scale=gain[:]).then_inc(q_taken, 1)

                def take_kv(m, s):
                    act.wait_ge(projected, m * 3 + 3)
                    act.activation(sq[:, 1, :], psP[:, 1, :], ACT.Square).then_inc(squared, 1)
                    act.wait_ge(projected, m * 3 + 4)
                    act.activation(v[:, s, :, :], psV[:], ACT.Copy).then_inc(copied, 1)
                    act.wait_ge(summed, m * 2 + 2)
                    act.wait_ge(kT_ready, m + 1)
                    act.activation(rk[:], psK[:], ACT.Ln, bias=eps[:], scale=1.0 / P).then_inc(own_act, 1)
                    act.wait_ge(own_act, m * 2 + 2)
                    act.activation(rk[:], rk[:], ACT.Exp, scale=-0.5).then_inc(rk_ready, 1)

                def norm_q(m, s):
                    act.wait_ge(summed, m * 2 + 3)
                    act.activation(rq[:, s, :], psV[:, 0, 0:J], ACT.Ln, bias=eps[:], scale=1.0 / P).then_inc(own_act, 1)
                    act.wait_ge(own_act, m * 2 + 3)
                    act.activation(rq[:, s, :], rq[:, s, :], ACT.Exp, scale=-0.5).then_inc(rk_ready, 1)

                def front(b, m, s):
                    take_q(m, s)
                    take_kv(m, s)
                    norm_q(m, s)

                def exponentials(m, s, tiles):
                    for j in tiles:
                        act.wait_ge(maxed, m * J + j + 2)
                        act.wait_ge(turned, m * J + 1)
                        act.activation(prob[:, j, :], psS[:, j % 2, :], ACT.Exp, bias=top[:, j:j + 1], scale=rq[:, s, j:j + 1],
                                       accum_out=den[:, j:j + 1]).then_inc(exps, 1)

                def back(b, h, m, s, more):
                    exponentials(m, s, (0, 1))
                    if more:
                        take_q(m + 1, 1 - s)
                    exponentials(m, s, (2, 3))
                    if more:
                        take_kv(m + 1, 1 - s)
                        norm_q(m + 1, 1 - s)
                    act.wait_ge(mixed, m + 2)
                    act.activation(oT[:, ds(h, 1), :], psP[:, 0:1, :], ACT.Copy).then_inc(out_copied, 1)

                turns(act, front, back, lambda b: act.wait_ge(y_done, (b + 1) * J + 1))

            @block.vector
            def _(dve):
                dve.wait_ge(w_in, 65)
                dve.memset(eps[:], 1e-5).then_inc(own_dve, 1)
                dve.tensor_tensor(gain[:], gains[:, 0:1], gains[:, 1:2], ALU.mult).then_inc(own_dve, 1)

                def norm_k(m, s):
                    dve.wait_ge(rk_ready, m * 2 + 2)
                    dve.tensor_tensor(kT[:, s, :], psP[:, 1, :], rk[:], ALU.mult).then_inc(kT_ready, 1)

                def scale_q(m, s):
                    dve.wait_ge(rk_ready, m * 2 + 3)
                    dve.tensor_scalar(rq[:, s, :], rq[:, s, :], SCALE, None, ALU.mult).then_inc(front_done, 1)

                def front(b, m, s):
                    norm_k(m, s)
                    scale_q(m, s)

                def back(b, h, m, s, more):
                    dve.wait_ge(front_done, m + 2)
                    for j in range(J):
                        n = m * J + j
                        dve.wait_ge(scored, n + 2)
                        dve.wait_ge(exps, m * J + 1)
                        dve.tensor_reduce(top[:, j:j + 1], psS[:, j % 2, :], AX.X, ALU.max, negate=True).then_inc(reduced, 1)
                        dve.wait_ge(reduced, n + 2)
                        dve.tensor_tensor(top[:, j:j + 1], top[:, j:j + 1], rq[:, s, j:j + 1], ALU.mult).then_inc(maxed, 1)
                    for j in range(J):
                        n = m * J + j
                        dve.wait_ge(exps, n + 2)
                        dve.reciprocal(den[:, j:j + 1], den[:, j:j + 1]).then_inc(inverse, 1)
                        dve.wait_ge(inverse, n + 2)
                        dve.tensor_scalar(prob[:, j, :], prob[:, j, :], den[:, j:j + 1], None, ALU.mult).then_inc(prob_ready, 1)
                    if more:
                        norm_k(m + 1, 1 - s)
                    for k in range(J):
                        dve.wait_ge(turned, m * J + k + 2)
                        dve.wait_ge(mixed, m + 1)
                        dve.tensor_copy(probT[:, k, :], psT[:, k % 2, :]).then_inc(probT_ready, 1)
                    if more:
                        scale_q(m + 1, 1 - s)

                def end(b):
                    for j in range(J):
                        dve.wait_ge(y_done, b * J + j + 2)
                        x_tile = g.x[:, ds(b * J + j, 1), :].rearrange("p a n -> p (a n)")
                        dve.tensor_tensor(x_tile, x_tile, psS[:, j % 2, :], ALU.add).then_inc(added, 1)

                turns(dve, front, back, end)

            @block.gpsimd
            def _(pool):
                pool.wait_ge(w_in, 65)
                with pool.Fori(0, B) as b:
                    pool.wait_ge(projected, b * H * 3 + 1)
                    pool.tensor_copy(cs[:], ctxT[:, :, ds(b * L, L)]).then_inc(ctx_copied, 1)



NF4 = [-1.0, -0.6962, -0.5251, -0.3949, -0.2844, -0.1848, -0.0911, 0.0, 0.0796, 0.1609, 0.2461, 0.3379, 0.4407, 0.5626, 0.723, 1.0]


def bf16_round(v):
    import struct
    n = struct.unpack("<I", struct.pack("<f", v))[0]
    n = (n + 0x7FFF + ((n >> 16) & 1)) & 0xFFFF0000
    return struct.unpack("<f", struct.pack("<I", n))[0]


CODES = [bf16_round(v) for v in NF4]
FIRST_OF = [-0.84375, -0.60546875, -0.45703125, -0.337890625, -0.234375, -0.1376953125, -0.04541015625, 0.0400390625,
            0.12060546875, 0.2041015625, 0.29296875, 0.390625, 0.50390625, 0.64453125, 0.86328125]
ROUND = 12582912.0


def quantized(nc, g, name, weights):
    N, BL = 5632, 64
    NB = N // BL
    GP = P * NB // (2 * BL)
    with Stage(nc, name) as st:
        w = st.sb("w", [P, N], BF16)
        scaled = st.sb("scaled", [P, N], BF16)
        step = st.sb("step", [P, N], BF16)
        above = st.sb("above", [P, N], BF16)
        value = st.sb("value", [P, N], BF16)
        s1 = st.sb("s1", [P, NB], BF16)
        inv = st.sb("inv", [P, NB])
        part = st.sb("part", [P, 2])
        mean = st.sb("mean", [P, 1], BF16)
        sb_ = st.sb("sb", [GP, 2, BL], BF16)
        top = st.sb("top", [GP, 2], BF16)
        qf = st.sb("qf", [GP, 2], BF16)
        qi = st.sb("qi", [GP, 2])
        q = st.sb("q", [GP, 2, BL], BF16)
        qr = st.sb("qr", [GP, 2, BL])
        deq = st.sb("deq", [GP, 2, BL], BF16)
        deqs = st.sb("deqs", [P, NB], BF16)
        psM = st.ps("psM", [P, 512])
        psT = st.ps("psT", [P, 2, 1024], BF16)
        own_dve = st.sem("own_dve")
        w_in = st.sem("w_in")
        part_ready = st.sem("part_ready")
        mean_done = st.sem("mean_done")
        scalers = st.sem("scalers")
        bounced = st.sem("bounced")
        deq_ready = st.sem("deq_ready")
        value_ready = st.sem("value_ready")
        turned = st.sem("turned")
        copied = st.sem("copied")
        rows = nc.dram_tensor(f"{name}_rows", (2, P * NB), BF16).ap()
        NW = len(weights)

        with st.block() as block:

            @block.sync
            def _(sp):
                for n, (src, _) in enumerate(weights):
                    if n:
                        sp.wait_ge(scalers, 2 * n + 1)
                    sp.dma_start(w[:], src).then_inc(w_in, 16)
                    sp.wait_ge(scalers, 2 * n + 2)
                    sp.dma_start(rows[0].rearrange("(p n) -> p n", p=P), s1[:]).then_inc(bounced, 16)
                    sp.wait_ge(bounced, 64 * n + 16 + 1)
                    sp.dma_start(sb_[:].rearrange("p a n -> p (a n)"), rows[0].rearrange("(p n) -> p n", p=GP)).then_inc(bounced, 16)
                    sp.wait_ge(deq_ready, n + 2)
                    sp.dma_start(rows[1].rearrange("(p n) -> p n", p=GP), deq[:].rearrange("p a n -> p (a n)")).then_inc(bounced, 16)
                    sp.wait_ge(bounced, 64 * n + 48 + 1)
                    sp.dma_start(deqs[:], rows[1].rearrange("(p n) -> p n", p=P)).then_inc(bounced, 16)

            @block.vector
            def _(dve):
                own = Own(dve, own_dve)
                for n in range(NW):
                    blocks = lambda ap: ap.rearrange("p (b c) -> p b c", c=BL)
                    dve.wait_ge(w_in, 16 * n + 16 + 1)
                    dve.tensor_reduce(s1[:], blocks(w[:]), AX.X, ALU.max, apply_absolute_value=True).then_inc(scalers, 1)
                    dve.wait_ge(scalers, 2 * n + 2)
                    own.step(dve.reciprocal(inv[:], s1[:]))
                    dve.tensor_reduce(part[:, 0:1], s1[:], AX.X, ALU.add).then_inc(part_ready, 1)
                    own.settle()
                    dve.tensor_tensor(blocks(scaled[:]), blocks(w[:]), inv[:].unsqueeze(2).broadcast_to([P, NB, BL]), ALU.mult).then_inc(scalers, 1)
                    dve.wait_ge(mean_done, n + 2)
                    own.link(dve.tensor_scalar(mean[:], psM[:, 0:1], 1.0 / (P * NB), None, ALU.mult))
                    dve.wait_ge(bounced, 64 * n + 32 + 1)
                    own.link(dve.tensor_scalar(sb_[:], sb_[:], mean[0:GP, :], None, ALU.subtract))
                    own.link(dve.tensor_reduce(top[:], sb_[:], AX.X, ALU.max, apply_absolute_value=True))
                    own.link(dve.tensor_scalar(top[:], top[:], 2.0, None, ALU.mult))
                    own.link(dve.reciprocal(qi[:], top[:]))
                    own.link(dve.tensor_scalar(qf[:], qi[:], 256.0, None, ALU.mult))
                    own.link(dve.tensor_tensor(q[:], sb_[:], qf[:].unsqueeze(2).broadcast_to([GP, 2, BL]), ALU.mult))
                    own.link(dve.tensor_scalar(qr[:], q[:], ROUND, -ROUND, ALU.add, ALU.add))
                    own.link(dve.tensor_scalar(qr[:], qr[:], -128.0, 127.0, ALU.max, ALU.min))
                    own.link(dve.reciprocal(qi[:], qf[:]))
                    own.link(dve.tensor_tensor(deq[:], qr[:], qi[:].unsqueeze(2).broadcast_to([GP, 2, BL]), ALU.mult))
                    dve.tensor_scalar(deq[:], deq[:], mean[0:GP, :], None, ALU.add).then_inc(deq_ready, 1)
                    if n:
                        dve.wait_ge(copied, 22 * n + 1)
                    for c in range(15):
                        code = c if c < 7 else c + 1
                        compare = (FIRST_OF[c], CODES[code], ALU.is_lt if c < 7 else ALU.is_ge, ALU.mult)
                        into = value if c < 7 else above
                        if c in (0, 7):
                            own.link(dve.tensor_scalar(into[:], scaled[:], *compare))
                        else:
                            own.link(dve.tensor_scalar(step[:], scaled[:], *compare))
                            own.link(dve.tensor_tensor(into[:], into[:], step[:], ALU.min if c < 7 else ALU.max))
                    own.link(dve.tensor_tensor(value[:], value[:], above[:], ALU.add))
                    dve.wait_ge(bounced, 64 * n + 64 + 1)
                    dve.tensor_tensor(blocks(value[:]), blocks(value[:]), deqs[:].unsqueeze(2).broadcast_to([P, NB, BL]), ALU.mult).then_inc(value_ready, 1)

            @block.tensor
            def _(pe):
                for n, (_, blocks_of) in enumerate(weights):
                    pe.wait_ge(part_ready, n + 2)
                    pe.matmul(psM[:, 0:1], g.ones[:], part[:, 0:1], start=True, stop=True).then_inc(mean_done, 1)
                    pe.wait_ge(value_ready, n + 2)
                    for i, (src, _) in enumerate(blocks_of(value)):
                        if i % 2 == 0 and (n * 22 + i // 2) >= 2:
                            pe.wait_ge(copied, n * 22 + i // 2)
                        last = pe.transpose(psT[:, (i // 2) % 2, (i % 2) * P:(i % 2 + 1) * P], src, g.ident16[:])
                        if i % 2:
                            last.then_inc(turned, 1)

            @block.scalar
            def _(act):
                for n, (_, blocks_of) in enumerate(weights):
                    pairs = blocks_of(value)
                    for i in range(22):
                        act.wait_ge(turned, n * 22 + i + 2)
                        act.activation(pairs[2 * i][1], psT[:, i % 2, 0:P], ACT.Copy)
                        act.activation(pairs[2 * i + 1][1], psT[:, i % 2, P:2 * P], ACT.Copy).then_inc(copied, 1)


def nf4_feed_forward(nc, g, name, zT, w1T, w2T, w3T, F):
    FT, G = F // P, 512
    GT = G // P
    with Stage(nc, name) as st:
        act_g = st.sb("act_g", [P, 2, G])
        hT = st.sb("hT", [P, FT, G])
        psG = st.ps("psG", [P, 2, 2, G])
        psO = st.ps("psO", [P, 2, D])
        gated = st.sem("gated")
        silu_done = st.sem("silu_done")
        h_ready = st.sem("h_ready")
        down = st.sem("down")
        added = st.sem("added")
        with st.block() as block:

            @block.tensor
            def _(pe):
                with pe.Fori(0, T // G) as i:
                    for f in range(FT):
                        pe.wait_ge(h_ready, (i * FT + f - 1 if f else i * FT) + 1)
                        for half, w in enumerate((w1T, w2T)):
                            for k in range(KD):
                                last = pe.matmul(psG[:, f % 2, half, :], w[:, k, f * P:(f + 1) * P], zT[:, k, ds(i * G, G)],
                                                 start=(k == 0), stop=(k == KD - 1))
                            last.then_inc(gated, 1)
                    pe.wait_ge(h_ready, (i + 1) * FT + 1)
                    for j in range(GT):
                        pe.wait_ge(added, (i * GT + j - 1 if j else i * GT) + 1)
                        for f in range(FT):
                            last = pe.matmul(psO[:, j % 2, :], hT[:, f, j * P:(j + 1) * P], w3T[:, f, :], start=(f == 0), stop=(f == FT - 1))
                        last.then_inc(down, 1)

            @block.scalar
            def _(act):
                with act.Fori(0, T // G) as i:
                    for f in range(FT):
                        act.wait_ge(gated, i * 2 * FT + 2 * f + 2)
                        act.wait_ge(h_ready, (i * FT + f - 1 if f else i * FT) + 1)
                        act.activation(act_g[:, f % 2, :], psG[:, f % 2, 0, :], ACT.Silu).then_inc(silu_done, 1)

            @block.vector
            def _(dve):
                with dve.Fori(0, T // G) as i:
                    for f in range(FT):
                        dve.wait_ge(gated, i * 2 * FT + 2 * f + 2 + 1)
                        dve.wait_ge(silu_done, i * FT + f + 2)
                        dve.wait_ge(down, i * GT + 1)
                        dve.tensor_tensor(hT[:, f, :], act_g[:, f % 2, :], psG[:, f % 2, 1, :], ALU.mult).then_inc(h_ready, 1)
                    for j in range(GT):
                        dve.wait_ge(down, i * GT + j + 2)
                        x_tile = g.x[:, ds(i * GT + j, 1), :].rearrange("p a n -> p (a n)")
                        dve.tensor_tensor(x_tile, x_tile, psO[:, j % 2, :], ALU.add).then_inc(added, 1)



class Globals:
    pass


def program(nc, a, out, stages=None):
    g = Globals()
    with ExitStack() as ctx:
        def sb(name, shape, dt=F32):
            return ctx.enter_context(nc.sbuf_tensor(name, shape, dt))

        g.x = sb("x_sb", [P, NT, D])
        g.mean, g.rstd, g.shift, g.ln_rstd = (sb(n, [P, NT]) for n in ("mean", "rstd", "shift", "ln_rstd"))
        g.weight_of = sb("weight_of", [P, NT, 8])
        g.slot_of = sb("slot_of", [P, NT, 8])
        g.ident, g.ones, g.earlier = (sb(n, [P, P]) for n in ("ident", "ones", "earlier"))
        g.ident16 = sb("ident16", [P, P], BF16)
        g.zeros_i = sb("zeros_i", [P, 144], I32)
        g.z_rows = nc.dram_tensor("z_rows", (T, D), F32).ap()
        g.slot_token = nc.dram_tensor("slot_token", (32 * 512 + 16 * P, 1), I32).ap()
        g.slot_rows = nc.dram_tensor("slot_rows", (32 * 512, D), F32).ap()
        g.pool_sem = lambda name: ctx.enter_context(nc.semaphore(name))
        g.ctxT = a["ctxT"]
        x_rows = a["x"].rearrange("(t p) n -> p t n", p=P)
        out_rows = out.rearrange("(t p) n -> p t n", p=P)

        with Stage(nc, "start") as st:
            x_in = st.sem("x_in")
            made = st.sem("made")
            with st.block() as block:

                @block.sync
                def _(sp):
                    sp.dma_start(g.x[:], x_rows).then_inc(x_in, 16)
                    sp.wait_ge(x_in, 17)

                @block.gpsimd
                def _(pool):
                    pool.memset(g.ident[:], 0.0).then_inc(made, 1)
                    pool.memset(g.ones[:], 1.0).then_inc(made, 1)
                    pool.memset(g.zeros_i[:], 0).then_inc(made, 1)
                    pool.wait_ge(made, 4)
                    pool.affine_select(out=g.ident[:], in_=g.ident[:], compare_op=ALU.not_equal, fill=1.0, base=0,
                                       pattern=[[-1, P]], channel_multiplier=1).then_inc(made, 1)
                    pool.affine_select(out=g.earlier[:], in_=g.ones[:], compare_op=ALU.is_gt, fill=0.0, base=0,
                                       pattern=[[1, P]], channel_multiplier=-1).then_inc(made, 1)
                    pool.wait_ge(made, 5)
                    pool.tensor_copy(g.ident16[:], g.ident[:])

        run = stages or range(8)
        if 0 in run:
            layer_norm(nc, g, "n0")
            mixer(nc, g, "m0", a["L0_xattn"])
        if 1 in run:
            w = a["L0_ffn"]
            with nc.sbuf_tensor("zT1", [P, KD, T], F32) as zT:
                layer_norm(nc, g, "n1", zT=zT, rms_weight=w["norm_w"], z_dram=g.z_rows,
                           router=Router(nc, g, 32, 4, 512, w["gateT"], True, 0.0))
                experts_wide(nc, g, "e1", 32, 512, 256, w["w13"], w["w2"])
                combine(nc, g, "c1", 32 * 512, 4, True)
                shared_expert(nc, g, "s1", zT, 256, w["shared_gate_w"], w["shared_up_w"], w["shared_down_w"])
        if 2 in run:
            layer_norm(nc, g, "n2")
            mixer(nc, g, "m2", a["L1_xattn"])
        if 3 in run:
            w = a["L1_ffn"]
            with nc.sbuf_tensor("zT3", [P, KD, T], F32) as zT:
                layer_norm(nc, g, "n3", zT=zT, router=SoftRouter(g, 8, 6, w["gate"], w["bg"]))
                soft_experts(nc, g, "e3", zT, 6, 256, w["Wgate"], w["bgate"], w["Wup"], w["bup"], w["Wdown"], w["bdown"],
                             w["Ws_up"], w["bs_up"], w["Ws_down"], w["bs_down"])
        if 4 in run:
            w = a["L2_xattn"]
            with nc.sbuf_tensor("zT4", [P, KD, T], F32) as zT:
                layer_norm(nc, g, "n4", zT=zT)
                feature_attention(nc, g, "a4", zT, w["WqT"], w["bq"], w["WkT"], w["bk"])
        if 5 in run:
            w = a["L2_ffn"]
            with nc.sbuf_tensor("zT5", [P, KD, T], F32) as zT:
                layer_norm(nc, g, "n5", zT=zT, z_dram=g.z_rows, router=Router(nc, g, 64, 8, 128, w["gateT"], False, 1e-20))
            experts_narrow(nc, g, "e5", 64, 128, 192, w["w_gate"], w["w_up"], w["w_down"])
            combine(nc, g, "c5", 64 * 128, 8, False)
        if 6 in run:
            w = a["L3_xattn"]
            with nc.sbuf_tensor("zT6", [P, KD, T], F32) as zT:
                layer_norm(nc, g, "n6", zT=zT)
                cross_attention(nc, g, "a6", zT, channels_first(w["Wq"]), channels_first(w["Wk"]), channels_first(w["Wv"]),
                                w["Wo"], w["gq"], w["gk"])
        if 7 in run:
            w = a["L3_ffn"]
            F = 1408
            RF = F // P
            with (nc.sbuf_tensor("w1T", [P, KD, F], F32) as w1T, nc.sbuf_tensor("w2T", [P, KD, F], F32) as w2T,
                  nc.sbuf_tensor("w3T", [P, RF, D], F32) as w3T):
                def rows_of_hidden(wT):
                    return lambda v: [(v[:, r * D + k * P:r * D + (k + 1) * P], wT[:, k, r * P:(r + 1) * P])
                                      for r in range(RF) for k in range(KD)]

                def rows_of_channels(v):
                    return [(v[:, c * F:(c + 1) * F].rearrange("p (n r) -> p r n", r=RF)[:, r, :],
                             w3T[:, r, :].rearrange("p (n c) -> p c n", c=4)[:, c, :])
                            for r in range(RF) for c in range(4)]

                quantized(nc, g, "q7", [(w["weight1"], rows_of_hidden(w1T)), (w["weight2"], rows_of_hidden(w2T)),
                                        (w["weight3"], rows_of_channels)])
                with nc.sbuf_tensor("zT7", [P, KD, T], F32) as zT:
                    layer_norm(nc, g, "n7", zT=zT)
                    nf4_feed_forward(nc, g, "f7", zT, w1T, w2T, w3T, F)

        with Stage(nc, "end") as st:
            x_out = st.sem("x_out")
            with st.block() as block:

                @block.sync
                def _(sp):
                    sp.dma_start(out_rows, g.x[:]).then_inc(x_out, 16)
                    sp.wait_ge(x_out, 17)



def laid_out(inputs):
    import numpy as np
    a = {k: np.asarray(v) for k, v in inputs.items()}

    def tiles(w, rows):
        return w.reshape(-1, rows, w.shape[-1]).transpose(1, 0, 2)

    out = {"x": a["x"].reshape(T, D), "ctxT": tiles(a["ctx_1024"].reshape(T, DC).T, P)}
    for n in ("L0_xattn", "L1_xattn"):
        cols = [a[f"{n}_conv_w"].reshape(D, 4), a[f"{n}_conv_b"][:, None], a[f"{n}_dt_proj_b"][:, None],
                a[f"{n}_D"][:, None], a[f"{n}_A_log"]]
        out[f"{n}/in_projT"] = tiles(a[f"{n}_in_proj_w"].T, P)
        out[f"{n}/x_projT"] = tiles(a[f"{n}_x_proj_w"].T, P)
        out[f"{n}/dt_projT"] = a[f"{n}_dt_proj_w"].T
        out[f"{n}/cols"] = tiles(np.concatenate(cols, axis=1), P)
    for n in ("norm_w", "w13", "w2", "shared_gate_w", "shared_up_w", "shared_down_w"):
        out[f"L0_ffn/{n}"] = a[f"L0_ffn_{n}"]
    out["L0_ffn/gateT"] = tiles(a["L0_ffn_gate_w"].T, P)
    for n in ("bg", "Wgate", "Wup", "Wdown", "bdown", "Ws_up", "Ws_down", "bs_down"):
        out[f"L1_ffn/{n}"] = a[f"L1_ffn_{n}"]
    out["L1_ffn/gate"] = tiles(a["L1_ffn_Wg"], P)
    for n in ("bgate", "bup"):
        out[f"L1_ffn/{n}"] = a[f"L1_ffn_{n}"].reshape(6, 2, P).transpose(2, 0, 1)
    out["L1_ffn/bs_up"] = a["L1_ffn_bs_up"].reshape(4, P).T
    for n in ("Wq", "Wk"):
        out[f"L2_xattn/{n}T"] = tiles(a[f"L2_xattn_{n}"].T, P)
    for n in ("bq", "bk"):
        out[f"L2_xattn/{n}"] = a[f"L2_xattn_{n}"]
    out["L2_ffn/gateT"] = tiles(a["L2_ffn_router_w"].T, P)
    for n in ("w_gate", "w_up", "w_down"):
        out[f"L2_ffn/{n}"] = a[f"L2_ffn_{n}"]
    for n in ("Wq", "Wk", "Wv", "Wo", "gq", "gk"):
        out[f"L3_xattn/{n}"] = a[f"L3_xattn_{n}"]
    for n in ("weight1", "weight2", "weight3"):
        out[f"L3_ffn/{n}"] = a[f"L3_ffn_{n}"].reshape(P, -1)
    return {k: np.ascontiguousarray(v) for k, v in out.items()}


def kernel(**inputs):
    import concourse.bacc as _bacc
    from concourse.bass_utils import run_bass_kernel_spmd as _run

    nc = _bacc.Bacc("TRN2", target_bir_lowering=False, num_devices=1)
    arrays, args = {}, {}
    for key, v in laid_out(inputs).items():
        dram = "in_" + key.replace("/", "_")
        arrays[dram] = v
        ap = nc.dram_tensor(dram, v.shape, mybir.dt.from_np(v.dtype), kind="ExternalInput").ap()
        group, _, leaf = key.partition("/")
        if leaf:
            args.setdefault(group, {})[leaf] = ap
        else:
            args[group] = ap
    out = nc.dram_tensor("out", (T, D), F32, kind="ExternalOutput").ap()
    program(nc, args, out)
    r = _run(nc, [arrays], core_ids=[0])
    return r.results[0]["out"].reshape(B, L, D)
```

```python
from contextlib import ExitStack

import concourse.bass as bass
from concourse import mybir

F32 = mybir.dt.float32
F32R = mybir.dt.float32r
BF16 = mybir.dt.bfloat16
I32 = mybir.dt.int32
U32 = mybir.dt.uint32
ACT = mybir.ActivationFunctionType
ALU = mybir.AluOpType
AX = mybir.AxisListType

P = 128
B = 4
L = 512
D = 512
T = B * L
NT = T // P
LT = L // P
Q = 4
NG = NT // Q
KD = D // P
DC = 256
KC = DC // P
NS = 16
DR = 16
LN_EPS = 1e-5
EXP_FLOOR = -87.33654

ds = bass.ds


class Stage:

    def __init__(self, nc, name):
        self.nc, self.name, self.ctx, self.sems = nc, name, ExitStack(), []

    def __enter__(self):
        self.ctx.__enter__()
        return self

    def sb(self, name, shape, dt=F32):
        return self.ctx.enter_context(self.nc.sbuf_tensor(f"{self.name}_{name}", shape, dt))

    def ps(self, name, shape, dt=F32):
        return self.ctx.enter_context(self.nc.psum_tensor(f"{self.name}_{name}", shape, dt))

    def sem(self, name):
        s = self.ctx.enter_context(self.nc.semaphore(f"{self.name}_{name}"))
        self.sems.append(s)
        return s

    def sems_of(self, name, n):
        return [self.sem(f"{name}{i}") for i in range(n)]

    def block(self):
        for s in self.sems:
            self.nc.gpsimd.sem_inc(s, 1)
        self.nc.all_engine_barrier(sem_only=True)
        return self.nc.Block()

    def __exit__(self, *exc):
        if exc[0] is None:
            for s in self.sems:
                self.nc.gpsimd.sem_clear(s)
        return self.ctx.__exit__(*exc)


class Own:

    def __init__(self, eng, sem):
        self.eng, self.sem, self.base, self.n = eng, sem, 0, 0

    def turn(self, i, per):
        self.start, self.per = self.base + self.n, per
        self.base, self.n = self.start + i * per, 0

    def turns_over(self, count):
        assert self.n == self.per, (self.n, self.per)
        self.base, self.n = self.start + count * self.per, 0

    def step(self, ins):
        ins.then_inc(self.sem, 1)
        self.n += 1

    def settle(self):
        self.eng.wait_ge(self.sem, self.base + self.n + 1)

    def link(self, ins):
        self.step(ins)
        self.settle()


def take_wait(eng, sem):
    eng.sem_inc(sem, 1)


def channels_first(ap):
    return ap.rearrange("(k p) n -> p k n", p=P)



def layer_norm(nc, g, name, zT, rms_weight=None, z_dram=None, router=None):
    with Stage(nc, name) as st:
        bn6 = st.sb("bn6", [P, NT, 6])
        mv = st.sb("mv", [P, NT, 2])
        std = st.sb("std", [P, NT])
        std2 = st.sb("std2", [P, NT])
        eps = st.sb("eps", [P, 2])
        z = st.sb("z", [P, NT, D])
        psT = st.ps("psT", [P, 2, D])
        own_dve = st.sem("own_dve")
        own_act = st.sem("own_act")
        var_ready = st.sem("var_ready")
        std_ready = st.sem("std_ready")
        z_ready = st.sem("z_ready")
        turned = st.sems_of("turned", 2)
        taken = st.sems_of("taken", 2)
        z_stored = st.sem("z_stored")
        consts_in = st.sem("consts_in")
        rms = rms_weight is not None
        if rms:
            w_sb = st.sb("w", [P, D])
        if router:
            router.allocate(st)

        with st.block() as block:

            @block.sync
            def _(sp):
                if rms:
                    sp.dma_start(w_sb[:], rms_weight.rearrange("(a n) -> a n", a=1).broadcast_to([P, D])).then_inc(consts_in, 16)
                if router:
                    router.load(sp)
                if z_dram is not None:
                    rows = z_dram.rearrange("(t p) n -> p t n", p=P)
                    with sp.Fori(0, NG) as r:
                        sp.wait_ge(z_ready, r * Q + Q + 1)
                        sp.dma_start(rows[:, ds(r * Q, Q), :], z[:, ds(r * Q, Q), :]).then_inc(z_stored, 16)
                    sp.wait_ge(z_stored, 16 * NG + 1)

            @block.vector
            def _(dve):
                own = Own(dve, own_dve)
                own.step(dve.memset(eps[:, 0:1], LN_EPS))
                own.link(dve.memset(eps[:, 1:2], 1e-6))
                with dve.Fori(0, NT) as t:
                    own.turn(t, 1)
                    own.step(dve.bn_stats(bn6[:, ds(t, 1), :], g.x[:, ds(t, 1), :]))
                own.turns_over(NT)
                own.settle()
                for t in range(NT):
                    own.step(dve.bn_aggr(mv[:, t, :], bn6[:, t, :]))
                own.settle()
                dve.tensor_copy(g.mean[:], mv[:, :, 0]).then_inc(var_ready, 1)
                dve.wait_ge(std_ready, 2)
                own.link(dve.reciprocal(g.rstd[:], std[:]))
                if rms:
                    own.link(dve.tensor_tensor(std2[:], mv[:, :, 1], g.rstd[:], ALU.mult))
                    own.step(dve.tensor_copy(g.ln_rstd[:], g.rstd[:]))
                    dve.tensor_tensor(std2[:], std2[:], g.rstd[:], ALU.mult).then_inc(var_ready, 1)
                    dve.wait_ge(std_ready, 3)
                    own.link(dve.reciprocal(std[:], std2[:]))
                    own.link(dve.tensor_tensor(g.rstd[:], g.rstd[:], std[:], ALU.mult))
                    dve.wait_ge(consts_in, 17)
                own.link(dve.scalar_tensor_tensor(g.shift[:], g.mean[:], -1.0, g.rstd[:], ALU.mult, ALU.mult))
                if router:
                    router.prepare(dve, own)
                with dve.Fori(0, NT) as t:
                    own.turn(t, int(rms))
                    z_tile = z[:, ds(t, 1), :].rearrange("p a n -> p (a n)")
                    out = dve.tensor_scalar(z_tile, g.x[:, ds(t, 1), :].rearrange("p a n -> p (a n)"),
                                            g.rstd[:, ds(t, 1)], g.shift[:, ds(t, 1)], ALU.mult, ALU.add)
                    if rms:
                        own.link(out)
                        out = dve.tensor_tensor(z_tile, z_tile, w_sb[:], ALU.mult)
                    out.then_inc(z_ready, 1)
                own.turns_over(NT)
                if router:
                    with dve.Fori(0, NG // 2) as i:
                        own.turn(i, 2 * router.STEPS)
                        for s in range(2):
                            router.choose(dve, own, i, s)
                    own.turns_over(NG // 2)

            @block.scalar
            def _(act):
                act.wait_ge(own_dve, 3)
                act.wait_ge(var_ready, 2)
                act.activation(std[:], mv[:, :, 1], ACT.Sqrt, bias=eps[:, 0:1]).then_inc(std_ready, 1)
                if rms:
                    act.wait_ge(var_ready, 3)
                    act.wait_ge(std_ready, 2)
                    act.activation(std2[:], std2[:], ACT.Sqrt, bias=eps[:, 1:2]).then_inc(std_ready, 1)
                with act.Fori(0, NT // 2) as i:
                    for s in range(2):
                        act.wait_ge(turned[s], i + 2)
                        act.activation(zT[:, :, ds((i * 2 + s) * P, P)],
                                       psT[:, s, :].rearrange("p (k n) -> p k n", k=KD), ACT.Copy).then_inc(taken[s], 1)
                if router:
                    with act.Fori(0, NG) as r:
                        router.exponentials(act, r)

            @block.tensor
            def _(pe):
                if router:
                    pe.wait_ge(router.router_in, router.LOADS * 16 + 1)
                for t in range(NT):
                    pe.wait_ge(z_ready, t + 2)
                    pe.wait_ge(taken[t % 2], t // 2 + 1)
                    for k in range(KD):
                        last = pe.transpose(psT[:, t % 2, k * P:(k + 1) * P], z[:, t, k * P:(k + 1) * P], g.ident[:])
                    last.then_inc(turned[t % 2], 1)
                    if router and t:
                        router.logits_of(pe, t - 1, zT, taken)
                if router:
                    router.logits_of(pe, NT - 1, zT, taken)
                if router:
                    with pe.Fori(0, NG) as r:
                        router.count(pe, r)

            @block.gpsimd
            def _(pool):
                if router:
                    router.scatter(pool)


def of_group(ap, r):
    return ap[:, ds(r * Q, Q)]


class Router:
    LOADS = 1

    def __init__(self, nc, g, E, K, C, gateT, keep_overflow, eps):
        self.nc, self.g, self.E, self.K, self.C, self.gateT = nc, g, E, K, C, gateT
        self.keep_overflow = keep_overflow
        self.eps = eps
        self.STEPS = 36 if keep_overflow else 37

    def allocate(self, st):
        E, K = self.E, self.K
        self.wg = st.sb("wg", [P, KD, E])
        self.iota = st.sb("iota", [P, E])
        self.iota_i = st.sb("iota_i", [P, E], I32)
        self.tok = st.sb("tok", [P, Q])
        self.first_tok = st.sb("first_tok", [P, Q], I32)
        self.dump = st.sb("dump", [P, Q, K])
        self.dump_i = st.sb("dump_i", [P, Q, K], I32)
        self.tok_i = st.sb("tok_i", [P, 2, Q], I32)
        self.logits = st.sb("logits", [P, Q, E])
        self.best = st.sb("best", [P, Q, 8])
        self.which = st.sb("which", [P, Q, 8], U32)
        self.e_all = st.sb("e_all", [P, Q, E])
        self.e_best = st.sb("e_best", [P, Q, 8])
        self.per_token = st.sb("per_token", [P, 5, Q])
        self.small = st.sb("small", [P, 6, Q, K])
        self.onehot = st.sb("onehot", [P, Q * K, E])
        self.masked = st.sb("masked", [P, Q * K, E])
        self.mask = st.sb("mask", [P, Q, E])
        self.group_sum = st.sb("group_sum", [P, E])
        self.before = st.sb("before", [P, E])
        self.slot_i = st.sb("slot_i", [P, 2, Q, K], I32)
        self.psR = st.ps("psR", [P, NG, 512])
        self.psC = st.ps("psC", [P, Q, E])
        self.router_in = st.sem("router_in")
        self.iotas = st.sem("iotas")
        self.tick = st.sem("tick")
        self.pool_tick = st.sem("pool_tick")
        self.logits_done = st.sem("logits_done")
        self.clamped = st.sem("clamped")
        self.exps_done = st.sem("exps_done")
        self.mask_ready = st.sem("mask_ready")
        self.counted = st.sem("counted")
        self.slots_ready = st.sem("slots_ready")
        self.table_zeroed = self.g.pool_sem(f"{st.name}_table_zeroed")
        self.scattered = [self.g.pool_sem(f"{st.name}_scattered{i}") for i in range(2)]
        self.slots_used = st.sem("slots_used")

    def load(self, sp):
        sp.dma_start(self.wg[:], self.gateT).then_inc(self.router_in, 16)

    def prepare(self, dve, own):
        dve.wait_ge(self.iotas, 4)
        own.step(dve.tensor_copy(self.iota[:], self.iota_i[:]))
        own.step(dve.tensor_copy(self.tok[:], self.first_tok[:]))
        own.step(dve.tensor_copy(self.dump[:], self.dump_i[:]))
        own.link(dve.memset(self.before[:], 0.0))

    def logits_of(self, pe, t, zT, taken):
        E = self.E
        pe.wait_ge(taken[t % 2], t // 2 + 2)
        for k in range(KD):
            last = pe.matmul(self.psR[:, t // Q, t % Q * E:(t % Q + 1) * E], zT[:, k, t * P:(t + 1) * P], self.wg[:, k, :],
                             start=(k == 0), stop=(k == KD - 1))
        last.then_inc(self.logits_done, 1)

    def count(self, pe, r):
        pe.wait_ge(self.mask_ready, r + 2)
        for j in range(Q):
            pe.matmul(self.psC[:, j, :], self.g.earlier[:], self.mask[:, j, :], start=True, stop=False)
            for tile in range(j):
                pe.matmul(self.psC[:, j, :], self.g.ones[:], self.mask[:, tile, :], start=False, stop=False)
            last = pe.matmul(self.psC[:, j, :], self.g.ones[:], self.before[:], start=False, stop=True)
        last.then_inc(self.counted, 1)

    def exponentials(self, act, r):
        act.wait_ge(self.clamped, r + 2)
        act.activation(self.e_all[:], self.logits[:], ACT.Exp).then_inc(self.exps_done, 1)
        act.activation(self.e_best[:], self.best[:], ACT.Exp).then_inc(self.exps_done, 1)

    def choose(self, dve, own, i, s):
        E, K, C, g, r = self.E, self.K, self.C, self.g, i * 2 + s
        v = lambda n: self.small[:, n, :, :]
        per_token = lambda n: self.per_token[:, n, :]
        spread = lambda ap, n: ap.unsqueeze(2).broadcast_to([P, Q, n])
        top, lg = self.best, self.logits
        dve.wait_ge(self.logits_done, r * Q + Q + 1)
        own.link(dve.tensor_copy(lg[:], self.psR[:, ds(r, 1), 0:Q * E].rearrange("p a (j e) -> p (a j) e", j=Q)))
        take_wait(dve, self.tick)
        for j in range(Q):
            own.step(dve.max(top[:, j, :], lg[:, j, :]))
        own.settle()
        own.link(dve.tensor_tensor(lg[:], lg[:], spread(top[:, :, 0], E), ALU.subtract))
        own.link(dve.tensor_scalar(lg[:], lg[:], EXP_FLOOR, None, ALU.max))
        take_wait(dve, self.tick)
        for j in range(Q):
            last = dve.max(top[:, j, :], lg[:, j, :])
        last.then_inc(self.clamped, 1)
        dve.wait_ge(self.clamped, r + 2)
        take_wait(dve, self.tick)
        for j in range(Q):
            own.step(dve.max_index(self.which[:, j, :], top[:, j, :], lg[:, j, :]))
        own.settle()
        own.link(dve.tensor_copy(v(0), self.which[:, :, 0:K]))
        own.link(dve.tensor_tensor(self.onehot[:], self.iota[:].unsqueeze(1).broadcast_to([P, Q * K, E]),
                                   v(0).rearrange("p j k -> p (j k)").unsqueeze(2).broadcast_to([P, Q * K, E]), ALU.is_equal))
        dve.tensor_reduce(self.mask[:], self.onehot[:].rearrange("p (j k) e -> p j e k", j=Q), AX.X, ALU.add).then_inc(self.mask_ready, 1)
        dve.wait_ge(self.mask_ready, r + 2)
        own.step(dve.tensor_reduce(self.group_sum[:], self.mask[:].rearrange("p j e -> p e j"), AX.X, ALU.add))
        dve.wait_ge(self.counted, r + 2)
        for j in range(Q):
            own.step(dve.tensor_tensor(self.masked[:, j * K:(j + 1) * K, :], self.onehot[:, j * K:(j + 1) * K, :],
                                       self.psC[:, j, :].unsqueeze(1).broadcast_to([P, K, E]), ALU.mult))
        own.settle()
        own.step(dve.tensor_tensor(self.before[:], self.before[:], self.group_sum[:], ALU.add))
        own.link(dve.tensor_reduce(v(1).rearrange("p j k -> p (j k)"), self.masked[:], AX.X, ALU.add))
        own.step(dve.tensor_scalar(v(2), v(1), float(C - 1), None, ALU.min))
        own.step(dve.tensor_scalar(v(3), v(1), float(C), None, ALU.is_ge))
        own.link(dve.scalar_tensor_tensor(v(4), v(0), float(C), v(1), ALU.mult, ALU.add))
        own.step(dve.scalar_tensor_tensor(of_group(g.slot_of, r)[:, :, 0:K], v(0), float(C), v(2), ALU.mult, ALU.add))
        own.link(dve.tensor_tensor(v(5), self.dump[:], v(4), ALU.subtract))
        own.link(dve.tensor_tensor(v(5), v(5), v(3), ALU.mult))
        dve.wait_ge(self.slots_used, i * 2 + 1)
        own.step(dve.tensor_copy(self.tok_i[:, s, :], self.tok[:]))
        own.link(dve.tensor_tensor(self.slot_i[:, s, :, :], v(4), v(5), ALU.add))
        dve.tensor_scalar(self.tok[:], self.tok[:], float(Q * P), None, ALU.add).then_inc(self.slots_ready, 1)
        dve.wait_ge(self.exps_done, 2 * r + 2 + 1)
        own.link(dve.tensor_reduce(per_token(0), self.e_all[:], AX.X, ALU.add))
        own.link(dve.reciprocal(per_token(1), per_token(0)))
        own.link(dve.tensor_tensor(v(5), self.e_best[:, :, 0:K], spread(per_token(1), K), ALU.mult))
        own.link(dve.tensor_reduce(per_token(2), v(5), AX.X, ALU.add))
        own.link(dve.tensor_scalar(per_token(3), per_token(2), self.eps, None, ALU.add))
        own.link(dve.reciprocal(per_token(4), per_token(3)))
        own.link(dve.tensor_tensor(v(5), v(5), spread(per_token(4), K), ALU.mult))
        w = of_group(g.weight_of, r)[:, :, 0:K]
        if self.keep_overflow:
            own.step(dve.tensor_copy(w, v(5)))
        else:
            own.link(dve.tensor_scalar(v(3), v(3), -1.0, 1.0, ALU.mult, ALU.add))
            own.step(dve.tensor_tensor(w, v(5), v(3), ALU.mult))

    def scatter(self, pool):
        g, E, K, C = self.g, self.E, self.K, self.C
        pool.iota(self.iota_i[:], [[1, E]], base=0, channel_multiplier=0).then_inc(self.iotas, 1)
        pool.iota(self.first_tok[:], [[P, Q]], base=0, channel_multiplier=1).then_inc(self.iotas, 1)
        pool.iota(self.dump_i[:], [[P, Q * K]], base=E * C, channel_multiplier=1).then_inc(self.iotas, 1)
        table = g.slot_token[0:E * C + Q * K * P]
        pool.dma_start(table.rearrange("(p n) a -> p (n a)", p=P), g.zeros_i[:, 0:E * C // P + Q * K]).then_inc(self.table_zeroed, 16)
        pool.wait_ge(self.table_zeroed, 16)
        with pool.Fori(0, NG // 2) as i:
            for s in range(2):
                pool.wait_ge(self.slots_ready, i * 2 + s + 2)
                take_wait(pool, self.pool_tick)
                for j in range(Q):
                    for k in range(K):
                        pool.indirect_dma_start(table, bass.IndirectOffsetOnAxis(ap=self.slot_i[:, s, j, k:k + 1], axis=0),
                                                self.tok_i[:, s, j:j + 1], None).then_inc(self.scattered[s], 16)
                pool.wait_ge(self.scattered[s], 16 * Q * K * (i + 1))
                pool.sem_inc(self.slots_used, 1)





def mixer(nc, g, name, w):
    ET = D // P
    HT = ET // 2
    with Stage(nc, name) as st:
        ctxT = st.sb("ctxT", [P, KC, L])
        w_in = st.sb("w_in", [P, KC, D])
        w_x = st.sb("w_x", [P, ET, DR + 2 * NS])
        w_dt = st.sb("w_dt", [DR, D])
        cols = st.sb("cols", [P, ET, 7 + NS])
        A = st.sb("A", [P, ET, NS])
        diag = st.sb("diag", [P, 5, ET, P])
        xpad = st.sb("xpad", [P, ET, L + 3])
        u = st.sb("u", [P, ET, L])
        delta = st.sb("delta", [P, ET, L])
        delta_next = st.sb("delta_next", [P, ET, L])
        du = st.sb("du", [P, ET, L])
        gate = st.sb("gate", [P, ET, L])
        x_dbl = st.sb("x_dbl", [DR + 2 * NS, L])
        relu = st.sb("relu", [P, HT, L])
        soft = st.sb("soft", [P, HT, L])
        tail = st.sb("tail", [P, HT, L])
        decay = st.sb("decay", [P, 2, ET, L])
        h = st.sb("h", [P, 4, ET, L])
        bc = st.sb("bc", [P, 4, 2, L])
        bn6 = st.sb("bn6", [P, NT, 6])
        mv = st.sb("mv", [P, NT, 2])
        std = st.sb("std", [P, NT])
        eps = st.sb("eps", [P, 1])
        psY = st.ps("psY", [P, ET, L])
        psA = st.ps("psA", [P, 4, L])
        bc_rows = nc.dram_tensor(f"{name}_bc_rows", (B, NS, 2, L), F32).ap()

        weights_in = st.sem("weights_in")
        ctx_in = st.sem("ctx_in")
        own_dve = st.sem("own_dve")
        a_exp = st.sem("a_exp")
        stats = st.sem("stats")
        var_ready = st.sem("var_ready")
        std_ready = st.sem("std_ready")
        norm_ready = st.sem("norm_ready")
        projected = st.sem("projected")
        padded = st.sem("padded")
        convolved = st.sem("convolved")
        u_ready = st.sem("u_ready")
        dbl_done = st.sem("dbl_done")
        dbl_copied = st.sem("dbl_copied")
        step_done = st.sem("step_done")
        act_soft = st.sem("act_soft")
        dve_soft = st.sem("dve_soft")
        exp_done = st.sem("exp_done")
        plus_one = st.sem("plus_one")
        logs_ready = st.sem("logs_ready")
        delta_ready = st.sem("delta_ready")
        delta_copied = st.sem("delta_copied")
        du_ready = st.sem("du_ready")
        rows_stored = st.sem("rows_stored")
        bc_in = st.sems_of("bc_in", 4)
        sp_tick = st.sem("sp_tick")
        driven = st.sem("driven")
        decayed = st.sem("decayed")
        scanned = st.sems_of("scanned", 2)
        weighted = st.sems_of("weighted", 4)
        summed = st.sems_of("summed", 4)
        gate_ready = st.sem("gate_ready")
        y_gated = st.sem("y_gated")
        y_turned = st.sem("y_turned")
        added = st.sem("added")

        flat = lambda ap: ap.rearrange("p e n -> p (e n)")

        def sequences(eng, main):
            main(0, True, True)
            with eng.Fori(1, B - 1) as b:
                main(b, False, True)
            main(B - 1, False, False)

        with st.block() as block:

            @block.sync
            def _(sp):
                for dst, src in ((w_in[:], w["in_projT"]), (w_x[:], w["x_projT"]), (w_dt[:], w["dt_projT"]), (cols[:], w["cols"])):
                    sp.dma_start(dst, src).then_inc(weights_in, 16)

                def load_context(b):
                    sp.dma_start(ctxT[:], g.ctxT[:, :, ds(b * L, L)]).then_inc(ctx_in, 16)

                def store_rows(b):
                    sp.wait_ge(dbl_copied, b + 2)
                    take_wait(sp, sp_tick)
                    for half in range(2):
                        sp.dma_start(bc_rows[ds(b, 1), :, half, :].rearrange("b n l -> (b n) l"),
                                     x_dbl[DR + half * NS:DR + (half + 1) * NS, :]).then_inc(rows_stored, 16)

                def main(b, first, more):
                    if more:
                        sp.wait_ge(projected, b * ET + ET + 1)
                        take_wait(sp, sp_tick)
                        load_context(b + 1)
                    sp.wait_ge(rows_stored, 32 * b + 32 + 1)
                    take_wait(sp, sp_tick)
                    for n in range(NS):
                        sp.wait_ge(weighted[n % 4], b * 4 + n // 4 + 1)
                        take_wait(sp, sp_tick)
                        sp.dma_start(bc[:, n % 4, :, :].rearrange("p a l -> p (a l)"),
                                     bc_rows[ds(b, 1), n:n + 1, :, :].rearrange("b n a l -> (b n) (a l)")
                                     .broadcast_to([P, 2 * L])).then_inc(bc_in[n % 4], 16)
                        if n == 15 and more:
                            store_rows(b + 1)

                load_context(0)
                store_rows(0)
                sequences(sp, main)

            @block.tensor
            def _(pe):
                def project(b, ets):
                    for et in ets:
                        for k in range(KC):
                            last = pe.matmul(psA[:, et, :], w_in[:, k, et * P:(et + 1) * P], ctxT[:, k, :],
                                             start=(k == 0), stop=(k == KC - 1))
                        last.then_inc(projected, 1)

                def convolve(b, et):
                    pe.wait_ge(padded, b * ET + et + 2)
                    for tap in range(4):
                        last = pe.matmul(psA[:, et, :], diag[:, tap, et, :], xpad[:, et, tap:tap + L], start=(tap == 0), stop=(tap == 3))
                    last.then_inc(convolved, 1)

                def project_steps(b):
                    for et in range(ET):
                        pe.wait_ge(u_ready, b * ET + et + 2)
                        last = pe.matmul(psA[0:DR + 2 * NS, 0, :], w_x[:, et, :], u[:, et, :], start=(et == 0), stop=(et == ET - 1))
                    last.then_inc(dbl_done, 1)

                def widen_steps(b):
                    pe.wait_ge(dbl_copied, b + 2)
                    for et in range(ET):
                        pe.matmul(psA[:, et, :], w_dt[:, et * P:(et + 1) * P], x_dbl[0:DR, :], start=True, stop=True).then_inc(step_done, 1)

                def turn_output(b):
                    pe.wait_ge(y_gated, b + 2)
                    for lt in range(LT):
                        for et in range(ET):
                            last = pe.transpose(psA[:, lt, et * P:(et + 1) * P], gate[:, et, lt * P:(lt + 1) * P], g.ident[:])
                        last.then_inc(y_turned, 1)

                def main(b, first, more):
                    if not first:
                        turn_output(b - 1)
                    for et in range(ET):
                        pe.matmul(psY[:, et, :], diag[:, 4, et, :], u[:, et, :], start=True, stop=False, skip_group_check=True)
                    for n in range(NS):
                        pe.wait_ge(weighted[n % 4], b * 4 + n // 4 + 2)
                        for et in range(ET):
                            last = pe.matmul(psY[:, et, :], g.ident[:], h[:, n % 4, et, :], start=False, stop=(n == NS - 1),
                                             skip_group_check=True)
                        last.then_inc(summed[n % 4], 1)
                        if more:
                            if n == 1:
                                pe.wait_ge(ctx_in, 16 * b + 32 + 1)
                                pe.wait_ge(added, b * LT + 1)
                                project(b + 1, (0, 1))
                            elif n == 2:
                                project(b + 1, (2, 3))
                            elif 3 <= n < 7:
                                convolve(b + 1, n - 3)
                            elif n == 7:
                                project_steps(b + 1)
                            elif n == 9:
                                widen_steps(b + 1)

                pe.wait_ge(weights_in, 65)
                pe.wait_ge(ctx_in, 17)
                project(0, range(ET))
                pe.wait_ge(own_dve, 5 * ET + 2)
                for et in range(ET):
                    convolve(0, et)
                project_steps(0)
                widen_steps(0)
                sequences(pe, main)
                turn_output(B - 1)

            @block.scalar
            def _(act):
                def pad(b, ets):
                    for et in ets:
                        act.wait_ge(projected, b * ET + et + 2)
                        act.activation(xpad[:, et, 3:3 + L], psA[:, et, :], ACT.Copy).then_inc(padded, 1)

                def silus(b):
                    act.wait_ge(du_ready, b + 1)
                    for et in range(ET):
                        act.wait_ge(convolved, b * ET + et + 2)
                        act.activation(u[:, et, :], psA[:, et, :], ACT.Silu, bias=cols[:, et, 4:5]).then_inc(u_ready, 1)

                def gates(b):
                    act.wait_ge(y_turned, b * LT + 1)
                    act.wait_ge(norm_ready, 2)
                    for et in range(ET):
                        last = act.activation(gate[:, et, :], g.x[:, ds(b * ET + et, 1), :].rearrange("p a n -> p (a n)"), ACT.Silu,
                                              bias=g.shift[:, ds(b * ET + et, 1)], scale=g.rstd[:, ds(b * ET + et, 1)])
                    last.then_inc(gate_ready, 1)

                def copy_steps(b):
                    act.wait_ge(dbl_done, b + 2)
                    act.wait_ge(rows_stored, 32 * b + 1)
                    act.activation(x_dbl[:], psA[0:DR + 2 * NS, 0, :], ACT.Copy).then_inc(dbl_copied, 1)

                def exponential(b, r):
                    ets = range(r * HT, (r + 1) * HT)
                    log = flat(delta_next[:, r * HT:(r + 1) * HT, :])
                    act.wait_ge(delta_ready, b * 2 + r + 1)
                    for et in ets:
                        act.wait_ge(step_done, b * ET + et + 2)
                        act.activation(relu[:, et - r * HT, :], psA[:, et, :], ACT.Relu, bias=cols[:, et, 5:6])
                        last = act.activation(delta_next[:, et, :], psA[:, et, :], ACT.Abs, bias=cols[:, et, 5:6])
                    last.then_inc(act_soft, 1)
                    act.wait_ge(act_soft, b * 2 + r + 2)
                    act.activation(flat(soft[:]), log, ACT.Exp, scale=-1.0).then_inc(exp_done, 1)

                def logarithm(b, r):
                    log = flat(delta_next[:, r * HT:(r + 1) * HT, :])
                    act.wait_ge(plus_one, b * 2 + r + 2)
                    act.activation(log, flat(tail[:]), ACT.Ln).then_inc(logs_ready, 1)

                def main(b, first, more):
                    act.wait_ge(delta_ready, b * 2 + 3)
                    act.activation(flat(delta[:]), flat(delta_next[:]), ACT.Copy).then_inc(delta_copied, 1)
                    act.wait_ge(delta_copied, b + 2)
                    for n in range(NS):
                        act.wait_ge(scanned[n % 2], b * (NS // 2) + n // 2 + 1)
                        for et in range(ET):
                            last = act.activation(decay[:, n % 2, et, :], delta[:, et, :], ACT.Exp, scale=A[:, et, n:n + 1])
                        last.then_inc(decayed, 1)
                        if more and n == 5:
                            pad(b + 1, (0, 1))
                        if more and n == 6:
                            pad(b + 1, (2, 3))
                        if n == 9:
                            if more:
                                silus(b + 1)
                            gates(b)
                        if more and n == 11:
                            copy_steps(b + 1)
                        if more and n in (12, 14):
                            exponential(b + 1, (n - 12) // 2)
                        if more and n in (13, 15):
                            logarithm(b + 1, (n - 12) // 2)

                act.wait_ge(weights_in, 65)
                act.activation(A[:], cols[:, :, 7:7 + NS], ACT.Exp).then_inc(a_exp, 1)
                act.wait_ge(own_dve, 5 * ET + 3)
                pad(0, range(ET))
                act.wait_ge(var_ready, 2)
                act.activation(std[:], mv[:, :, 1], ACT.Sqrt, bias=eps[:]).then_inc(std_ready, 1)
                silus(0)
                copy_steps(0)
                for r in range(2):
                    exponential(0, r)
                    logarithm(0, r)
                sequences(act, main)

            @block.vector
            def _(dve):
                def one_plus(b, r):
                    dve.wait_ge(exp_done, b * 2 + r + 2)
                    dve.tensor_scalar(flat(tail[:]), flat(soft[:]), 1.0, None, ALU.add).then_inc(plus_one, 1)

                def softplus(b, r):
                    log = flat(delta_next[:, r * HT:(r + 1) * HT, :])
                    done = b * 6 + r * 3
                    dve.wait_ge(logs_ready, b * 2 + r + 2)
                    dve.scalar_tensor_tensor(log, flat(tail[:]), 1.0, log, ALU.is_gt, ALU.mult).then_inc(dve_soft, 1)
                    dve.wait_ge(dve_soft, done + 2)
                    dve.scalar_tensor_tensor(flat(tail[:]), flat(tail[:]), -1.0, flat(soft[:]), ALU.add, ALU.subtract).then_inc(dve_soft, 1)
                    dve.wait_ge(dve_soft, done + 3)
                    dve.tensor_tensor(flat(tail[:]), flat(relu[:]), flat(tail[:]), ALU.subtract).then_inc(dve_soft, 1)
                    dve.wait_ge(dve_soft, done + 4)
                    dve.tensor_tensor(log, log, flat(tail[:]), ALU.add).then_inc(delta_ready, 1)

                def gate_output(b):
                    for j in range(4):
                        dve.wait_ge(summed[j], b * 4 + 4 + 1)
                    dve.wait_ge(gate_ready, b + 2)
                    dve.tensor_tensor(flat(gate[:]), flat(psY[:]), flat(gate[:]), ALU.mult).then_inc(y_gated, 1)

                def add_output(b):
                    for lt in range(LT):
                        dve.wait_ge(y_turned, b * LT + lt + 2)
                        x_tile = g.x[:, ds(b * LT + lt, 1), :].rearrange("p a n -> p (a n)")
                        dve.tensor_tensor(x_tile, x_tile, psA[:, lt, :], ALU.add).then_inc(added, 1)

                def main(b, first, more):
                    dve.wait_ge(delta_ready, b * 2 + 3)
                    dve.tensor_tensor(flat(du[:]), flat(delta_next[:]), flat(u[:]), ALU.mult).then_inc(du_ready, 1)
                    dve.wait_ge(du_ready, b + 2)
                    for n in range(NS):
                        j = n % 4
                        dve.wait_ge(bc_in[j], (b * 4 + n // 4) * 16 + 16 + 1)
                        dve.wait_ge(summed[j], b * 4 + n // 4 + 1)
                        dve.tensor_tensor(h[:, j, :, :], du[:], bc[:, j, 0, :].unsqueeze(1).broadcast_to([P, ET, L]),
                                          ALU.mult).then_inc(driven, 1)
                        dve.wait_ge(driven, b * NS + n + 2)
                        dve.wait_ge(decayed, b * NS + n + 2)
                        for et in range(ET):
                            last = dve.tensor_tensor_scan(h[:, j, et, :], decay[:, n % 2, et, :], h[:, j, et, :], 0.0, ALU.mult, ALU.add)
                        last.then_inc(scanned[n % 2], 1)
                        if not first and n == 1:
                            gate_output(b - 1)
                        if not first and n == 2:
                            add_output(b - 1)
                        if more and n in (12, 14):
                            one_plus(b + 1, (n - 12) // 2)
                        if more and n in (13, 15):
                            softplus(b + 1, (n - 12) // 2)

                dve.memset(xpad[:, :, 0:3], 0.0).then_inc(own_dve, 1)
                dve.wait_ge(weights_in, 65)
                for tap, col in enumerate((0, 1, 2, 3, 6)):
                    for et in range(ET):
                        dve.tensor_scalar(diag[:, tap, et, :], g.ident[:], cols[:, et, col:col + 1], None, ALU.mult).then_inc(own_dve, 1)
                dve.wait_ge(a_exp, 2)
                dve.tensor_scalar(A[:], A[:], -1.0, None, ALU.mult).then_inc(own_dve, 1)
                dve.memset(eps[:], LN_EPS).then_inc(stats, 1)
                with dve.Fori(0, NT) as t:
                    dve.bn_stats(bn6[:, ds(t, 1), :], g.x[:, ds(t, 1), :]).then_inc(stats, 1)
                dve.wait_ge(stats, NT + 2)
                for t in range(NT):
                    dve.bn_aggr(mv[:, t, :], bn6[:, t, :]).then_inc(stats, 1)
                dve.wait_ge(stats, 2 * NT + 2)
                dve.tensor_copy(g.mean[:], mv[:, :, 0]).then_inc(var_ready, 1)
                dve.wait_ge(std_ready, 2)
                dve.reciprocal(g.rstd[:], std[:]).then_inc(stats, 1)
                dve.wait_ge(stats, 2 * NT + 3)
                dve.scalar_tensor_tensor(g.shift[:], g.mean[:], -1.0, g.rstd[:], ALU.mult, ALU.mult).then_inc(norm_ready, 1)
                for r in range(2):
                    one_plus(0, r)
                    softplus(0, r)
                sequences(dve, main)
                gate_output(B - 1)
                add_output(B - 1)

            @block.gpsimd
            def _(pool):
                with pool.Fori(0, B * NS // 4) as i:
                    for j in range(4):
                        pool.wait_ge(scanned[j % 2], i * 2 + j // 2 + 2)
                        pool.tensor_tensor(h[:, j, :, :], h[:, j, :, :], bc[:, j, 1, :].unsqueeze(1).broadcast_to([P, ET, L]),
                                           ALU.mult).then_inc(weighted[j], 1)



def experts_wide(nc, g, name, E, C, F, w13, w2):
    CT, FT = C // P, F // P
    with Stage(nc, name) as st:
        idx = st.sb("idx", [P, 2, CT], I32)
        wa = st.sb("wa", [P, KD, 2 * F])
        wa_high = st.sb("wa_high", [P, 2, KD, 2 * F], F32R)
        wa_low = st.sb("wa_low", [P, 2, KD, 2 * F], F32R)
        wb = st.sb("wb", [P, FT, D])
        wb_high = st.sb("wb_high", [P, FT, D], F32R)
        wb_low = st.sb("wb_low", [P, FT, D], F32R)
        xg = st.sb("xg", [P, 2, CT, D])
        xT_high = st.sb("xT_high", [P, KD, C], F32R)
        xT_low = st.sb("xT_low", [P, KD, C], F32R)
        act_g = st.sb("act_g", [P, 2, C])
        hidden = st.sb("hidden", [P, FT, C])
        h_high = st.sb("h_high", [P, FT, C], F32R)
        h_low = st.sb("h_low", [P, FT, C], F32R)
        out = st.sb("out", [P, 2, CT, D])
        psT = st.ps("psT", [P, 2, C])
        psG = st.ps("psG", [P, 2 * FT, C])
        psO = st.ps("psO", [P, 2, D])
        idx_in = st.sems_of("idx_in", 2)
        wa_in = st.sem("wa_in")
        wb_in = st.sem("wb_in")
        wa_high_ready = st.sem("wa_high_ready")
        wa_split = st.sem("wa_split")
        wb_high_ready = st.sem("wb_high_ready")
        wb_split = st.sem("wb_split")
        gathered = [g.pool_sem(f"{name}_gathered{i}") for i in range(2)]
        pool_tick = st.sem("pool_tick")
        turned = st.sem("turned")
        xT_high_ready = st.sem("xT_high_ready")
        xT_split = st.sem("xT_split")
        gated = st.sem("gated")
        silu_done = st.sem("silu_done")
        h_ready = st.sem("h_ready")
        h_high_ready = st.sem("h_high_ready")
        h_split = st.sem("h_split")
        down = st.sem("down")
        out_ready = st.sem("out_ready")
        stored = st.sems_of("stored", 2)
        table = g.slot_token[0:E * C].rearrange("(e p j) a -> p e (j a)", p=P, j=CT)
        rows_out = g.slot_rows[0:E * C, :].rearrange("(e p j) n -> p e (j n)", p=P, j=CT)

        with st.block() as block:

            @block.sync
            def _(sp):
                def load_idx(e, s):
                    sp.dma_start(idx[:, s, :], table[:, ds(e, 1), :].rearrange("p a j -> p (a j)")).then_inc(idx_in[s], 16)

                def load_wa(e):
                    sp.dma_start(wa[:], w13[ds(e, 1), :, :].rearrange("e (k p) n -> p (e k) n", p=P)).then_inc(wa_in, 16)

                def load_wb(e):
                    sp.dma_start(wb[:], w2[ds(e, 1), :, :].rearrange("e (k p) n -> p (e k) n", p=P)).then_inc(wb_in, 16)

                def body(e, s, next_a, next_b):
                    if next_a:
                        sp.wait_ge(wa_split, e + 3)
                        load_wa(e + 2)
                        load_idx(e + 2, s)
                    if next_b:
                        sp.wait_ge(wb_split, e + 2)
                        load_wb(e + 1)
                    sp.wait_ge(out_ready, (e + 1) * CT + 1)
                    sp.dma_start(rows_out[:, ds(e, 1), :].rearrange("p a n -> p (a n)"),
                                 out[:, s, :, :].rearrange("p j n -> p (j n)")).then_inc(stored[s], 16)

                load_idx(0, 0)
                load_wa(0)
                load_wb(0)
                load_idx(1, 1)
                sp.wait_ge(wa_split, 2)
                load_wa(1)
                with sp.Fori(0, E // 2 - 1) as i:
                    for s in range(2):
                        body(i * 2 + s, s, True, True)
                body(E - 2, 0, False, True)
                body(E - 1, 1, False, False)
                for s in range(2):
                    sp.wait_ge(stored[s], 16 * (E // 2) + 1)

            @block.gpsimd
            def _(pool):
                with pool.Fori(0, E // 2) as i:
                    for s in range(2):
                        pool.wait_ge(idx_in[s], i * 16 + 16 + 1)
                        pool.wait_ge(turned, i * 8 + 1)
                        take_wait(pool, pool_tick)
                        for j in range(CT):
                            pool.indirect_dma_start(xg[:, s, j, :], None, g.z_rows,
                                                    bass.IndirectOffsetOnAxis(ap=idx[:, s, j:j + 1], axis=0)).then_inc(gathered[s], 16)

            def turns(eng, first, body):
                first()
                with eng.Fori(0, E // 2 - 1) as i:
                    for s in range(2):
                        body(i * 2 + s, s, True)
                body(E - 2, 0, True)
                body(E - 1, 1, False)

            @block.tensor
            def _(pe):
                def product(dst, stationary, moving, first, last):
                    (a_high, a_low), (b_high, b_low) = stationary, moving
                    pe.matmul(dst, a_high, b_high, start=first, stop=False)
                    pe.matmul(dst, a_high, b_low, start=False, stop=False)
                    return pe.matmul(dst, a_low, b_high, start=False, stop=last)

                def turn(e, s, ks):
                    pe.wait_ge(gathered[s], (e + 2 - s) * 8 * CT)
                    for k in ks:
                        pe.wait_ge(xT_split, e * KD + (k if k else 1))
                        for j in range(CT):
                            last = pe.transpose(psT[:, k % 2, j * P:(j + 1) * P], xg[:, s, j, k * P:(k + 1) * P], g.ident[:])
                        last.then_inc(turned, 1)

                def multiply_down(e, j, f):
                    if f == 0:
                        pe.wait_ge(out_ready, e * CT + (j if j else 1))
                    pe.wait_ge(h_split, e * FT + f + 2)
                    rows = slice(j * P, (j + 1) * P)
                    last = product(psO[:, j % 2, :], (h_high[:, f, rows], h_low[:, f, rows]),
                                   (wb_high[:, f, :], wb_low[:, f, :]), f == 0, f == FT - 1)
                    if f == FT - 1:
                        last.then_inc(down, 1)

                def body(e, s, more):
                    pe.wait_ge(wa_split, e + 2)
                    pe.wait_ge(h_ready, e * FT + 1)
                    for f in range(FT):
                        for half in range(2):
                            units = slice((half * FT + f) * P, (half * FT + f + 1) * P)
                            for k in range(KD):
                                if f == half == 0:
                                    pe.wait_ge(xT_split, e * KD + k + 2)
                                last = product(psG[:, half * FT + f, :], (wa_high[:, s, k, units], wa_low[:, s, k, units]),
                                               (xT_high[:, k, :], xT_low[:, k, :]), k == 0, k == KD - 1)
                            last.then_inc(gated, 1)
                    if more:
                        turn(e + 1, 1 - s, (0, 1))
                    pe.wait_ge(wb_split, e + 2)
                    for j in range(2):
                        multiply_down(e, j, 0)
                    if more:
                        turn(e + 1, 1 - s, (2, 3))
                    for j in range(2):
                        multiply_down(e, j, 1)
                    for j in range(2, CT):
                        for f in range(FT):
                            multiply_down(e, j, f)

                turns(pe, lambda: turn(0, 0, range(KD)), body)

            @block.scalar
            def _(act):
                def wa_part(e, s):
                    act.wait_ge(wa_in, e * 16 + 16 + 1)
                    act.activation(wa_high[:, s, :, :], wa[:], ACT.Copy).then_inc(wa_high_ready, 1)

                def take(e, ks):
                    for k in ks:
                        act.wait_ge(turned, e * KD + k + 2)
                        act.activation(xT_high[:, k, :], psT[:, k % 2, :], ACT.Copy).then_inc(xT_high_ready, 1)

                def first():
                    wa_part(0, 0)
                    take(0, range(KD))

                def body(e, s, more):
                    if more:
                        wa_part(e + 1, 1 - s)
                    act.wait_ge(wb_in, e * 16 + 16 + 1)
                    act.wait_ge(down, e * CT + 1)
                    act.activation(wb_high[:], wb[:], ACT.Copy).then_inc(wb_high_ready, 1)
                    for f in range(FT):
                        act.wait_ge(gated, e * 2 * FT + 2 * f + 2)
                        act.wait_ge(h_ready, e * FT + 1)
                        act.activation(act_g[:, f, :], psG[:, f, :], ACT.Silu).then_inc(silu_done, 1)
                        if more and f == FT - 1:
                            take(e + 1, (0,))
                        act.wait_ge(h_ready, e * FT + f + 2)
                        act.activation(h_high[:, f, :], hidden[:, f, :], ACT.Copy).then_inc(h_high_ready, 1)
                    if more:
                        take(e + 1, range(1, KD))

                turns(act, first, body)

            @block.vector
            def _(dve):
                def rest(dst, src, high):
                    return dve.tensor_tensor(dst, src, high.bitcast(F32), ALU.subtract)

                def wa_part(e, s):
                    dve.wait_ge(wa_high_ready, e + 2)
                    rest(wa_low[:, s, :, :], wa[:], wa_high[:, s, :, :]).then_inc(wa_split, 1)

                def take(e, ks):
                    for k in ks:
                        dve.wait_ge(xT_high_ready, e * KD + k + 2)
                        rest(xT_low[:, k, :], psT[:, k % 2, :], xT_high[:, k, :]).then_inc(xT_split, 1)

                def first():
                    wa_part(0, 0)
                    take(0, range(KD))

                def body(e, s, more):
                    if more:
                        wa_part(e + 1, 1 - s)
                    dve.wait_ge(wb_high_ready, e + 2)
                    rest(wb_low[:], wb[:], wb_high[:]).then_inc(wb_split, 1)
                    for f in range(FT):
                        dve.wait_ge(gated, e * 2 * FT + 2 * f + 3)
                        dve.wait_ge(silu_done, e * FT + f + 2)
                        dve.tensor_tensor(hidden[:, f, :], act_g[:, f, :], psG[:, FT + f, :], ALU.mult).then_inc(h_ready, 1)
                        if more and f == FT - 1:
                            take(e + 1, (0,))
                        dve.wait_ge(h_high_ready, e * FT + f + 2)
                        dve.wait_ge(down, e * CT + 1)
                        rest(h_low[:, f, :], hidden[:, f, :], h_high[:, f, :]).then_inc(h_split, 1)
                    if more:
                        take(e + 1, range(1, KD))
                    dve.wait_ge(stored[s], (e - s) * 8 + 1)
                    for j in range(CT):
                        dve.wait_ge(down, e * CT + j + 2)
                        dve.tensor_copy(out[:, s, j, :], psO[:, j % 2, :]).then_inc(out_ready, 1)

                turns(dve, first, body)


class Gather:

    def __init__(self, g, st, K, slots):
        self.g, self.K, self.slots = g, K, slots
        self.rows = st.sb("rows", [P, 2, K, D])
        self.idx = st.sb("idx", [P, 2, K], U32)
        self.idx_ready = st.sem("idx_ready")
        self.gathered = [g.pool_sem(f"{st.name}_gathered{i}") for i in range(2)]
        self.used = st.sems_of("used", 2)
        self.pool_tick = st.sem("pool_tick")

    def rows_of_tiles(self, pool):
        K, idx = self.K, self.idx
        with pool.Fori(0, NT // 2) as i:
            for s in range(2):
                pool.wait_ge(self.used[s], i + 1)
                pool.tensor_copy(idx[:, s, :], self.g.slot_of[:, ds(i * 2 + s, 1), 0:K].rearrange("p a k -> p (a k)")).then_inc(self.idx_ready, 1)
                pool.wait_ge(self.idx_ready, i * 2 + s + 2)
                take_wait(pool, self.pool_tick)
                for k in range(K):
                    pool.indirect_dma_start(self.rows[:, s, k, :], None, self.g.slot_rows[0:self.slots, :],
                                            bass.IndirectOffsetOnAxis(ap=idx[:, s, k:k + 1], axis=0)).then_inc(self.gathered[s], 16)

    def add_rows(self, dve, own, t, i, s, x_tile):
        dve.wait_ge(self.gathered[s], (i + 1) * 16 * self.K)
        for k in range(self.K):
            out = dve.scalar_tensor_tensor(x_tile, self.rows[:, s, k, :],
                                           self.g.weight_of[:, ds(t, 1), k:k + 1].rearrange("p a k -> p (a k)"),
                                           x_tile, ALU.mult, ALU.add)
            if k < self.K - 1:
                own.link(out)
            else:
                out.then_inc(self.used[s], 1)


def combine(nc, g, name, slots, K):
    with Stage(nc, name) as st:
        gather = Gather(g, st, K, slots)
        own_dve = st.sem("own_dve")
        with st.block() as block:

            @block.gpsimd
            def _(pool):
                gather.rows_of_tiles(pool)

            @block.vector
            def _(dve):
                own = Own(dve, own_dve)
                with dve.Fori(0, NT // 2) as i:
                    own.turn(i, 2 * (K - 1))
                    for s in range(2):
                        t = i * 2 + s
                        gather.add_rows(dve, own, t, i, s, g.x[:, ds(t, 1), :].rearrange("p a n -> p (a n)"))
                own.turns_over(NT // 2)


def experts_narrow(nc, g, name, E, C, F, w_gate, w_up, w_down):
    FH, R = F // 2, 4
    with Stage(nc, name) as st:
        idx = st.sb("idx", [P, R, 1], I32)
        wa = st.sb("wa", [P, R, KD, 2 * F])
        wb = st.sb("wb", [FH, R, 2, D])
        xg = st.sb("xg", [P, R, D])
        xgT = st.sb("xgT", [P, 2, KD, P])
        act_g = st.sb("act_g", [P, F])
        hid = st.sb("hid", [P, F])
        hT = st.sb("hT", [FH, 2, P])
        out = st.sb("out", [P, 2, D])
        psT = st.ps("psT", [P, 2, D])
        psG = st.ps("psG", [P, 2, 512])
        psH = st.ps("psH", [P, 512])
        psO = st.ps("psO", [P, 2, D])
        idx_in = st.sems_of("idx_in", R)
        w_in = st.sems_of("w_in", R)
        gathered = [g.pool_sem(f"{name}_gathered{i}") for i in range(R)]
        pool_tick = st.sem("pool_tick")
        turned = st.sem("turned")
        xgT_ready = st.sem("xgT_ready")
        gated = st.sem("gated")
        silu_done = st.sem("silu_done")
        hid_ready = st.sem("hid_ready")
        hid_turned = st.sem("hid_turned")
        hT_ready = st.sem("hT_ready")
        down = st.sem("down")
        out_ready = st.sem("out_ready")
        stored = st.sems_of("stored", 2)
        table = g.slot_token[0:E * C].rearrange("(e p) a -> p e a", p=P)
        rows_out = g.slot_rows[0:E * C, :].rearrange("(e p) n -> p e n", p=P)

        def rounds(eng, body):
            for s in range(R):
                body(0, s)
            with eng.Fori(1, E // R - 1) as i:
                for s in range(R):
                    body(i, s)
            for s in range(R):
                body(E // R - 1, s)

        def is_first(i, s, count=1):
            return isinstance(i, int) and i * R + s < count

        def is_last(i, s):
            return isinstance(i, int) and i * R + s == E - 1

        with st.block() as block:

            @block.sync
            def _(sp):
                def load(i, s):
                    e = i * R + s
                    sp.dma_start(idx[:, s, :], table[:, ds(e, 1), :].rearrange("p e a -> p (e a)")).then_inc(idx_in[s], 16)
                    sp.dma_start(wa[:, s, :, 0:F], w_gate[ds(e, 1), :, :].rearrange("e (k p) n -> p (e k) n", p=P)).then_inc(w_in[s], 16)
                    sp.dma_start(wa[:, s, :, F:2 * F], w_up[ds(e, 1), :, :].rearrange("e (k p) n -> p (e k) n", p=P)).then_inc(w_in[s], 16)
                    sp.dma_start(wb[:, s, :, :], w_down[ds(e, 1), :, :].rearrange("e (k p) n -> p (e k) n", p=FH)).then_inc(w_in[s], 16)

                def body(i, s, more=True):
                    e = i * R + s
                    if more:
                        sp.wait_ge(down, e + 2)
                        load(i + 1, s)
                    sp.wait_ge(out_ready, e + 2)
                    sp.dma_start(rows_out[:, ds(e, 1), :].rearrange("p a n -> p (a n)"), out[:, s % 2, :]).then_inc(stored[s % 2], 16)

                for s in range(R):
                    load(0, s)
                with sp.Fori(0, E // R - 1) as i:
                    for s in range(R):
                        body(i, s)
                for s in range(R):
                    body(E // R - 1, s, more=False)
                for s in range(2):
                    sp.wait_ge(stored[s], 16 * (E // 2) + 1)

            @block.gpsimd
            def _(pool):
                def body(i, s):
                    pool.wait_ge(idx_in[s], i * 16 + 16 + 1)
                    if not is_first(i, s, R):
                        pool.wait_ge(turned, (i - 1) * R + s + 2)
                    take_wait(pool, pool_tick)
                    pool.indirect_dma_start(xg[:, s, :], None, g.z_rows,
                                            bass.IndirectOffsetOnAxis(ap=idx[:, s, 0:1], axis=0)).then_inc(gathered[s], 16)

                rounds(pool, body)

            @block.tensor
            def _(pe):
                def turn_rows(i, s):
                    e = i * R + s
                    pe.wait_ge(gathered[s % R], (i + s // R) * 16 + 16)
                    if not is_first(i, s, 2):
                        pe.wait_ge(xgT_ready, e)
                    for k in range(KD):
                        last = pe.transpose(psT[:, s % 2, k * P:(k + 1) * P], xg[:, s % R, k * P:(k + 1) * P], g.ident[:])
                    last.then_inc(turned, 1)

                def multiply_down(i, s):
                    e, before = i * R + s, (s - 1) % R
                    pe.wait_ge(hT_ready, e + 1)
                    if not is_first(i, s, 3):
                        pe.wait_ge(out_ready, e - 1)
                    for f in range(2):
                        last = pe.matmul(psO[:, before % 2, :], hT[:, f, :], wb[:, before, f, :], start=(f == 0), stop=(f == 1))
                    last.then_inc(down, 1)

                def body(i, s):
                    e = i * R + s
                    pe.wait_ge(w_in[s], i * 48 + 48 + 1)
                    pe.wait_ge(xgT_ready, e + 2)
                    if not is_first(i, s, 2):
                        pe.wait_ge(hid_ready, e)
                    for k in range(KD):
                        last = pe.matmul(psG[:, s % 2, 0:2 * F], xgT[:, s % 2, k, :], wa[:, s, k, :], start=(k == 0), stop=(k == KD - 1))
                    last.then_inc(gated, 1)
                    if not is_last(i, s):
                        turn_rows(i, s + 1)
                    if not is_first(i, s):
                        multiply_down(i, s)
                    pe.wait_ge(hid_ready, e + 2)
                    pe.wait_ge(hT_ready, e + 1)
                    for f in range(2):
                        last = pe.transpose(psH[0:FH, f * P:(f + 1) * P], hid[:, f * FH:(f + 1) * FH], g.ident[:])
                    last.then_inc(hid_turned, 1)

                turn_rows(0, 0)
                rounds(pe, body)
                multiply_down(E // R, 0)

            @block.scalar
            def _(act):
                def take_rows(i, s):
                    e = i * R + s
                    act.wait_ge(turned, e + 2)
                    if not is_first(i, s, 2):
                        act.wait_ge(gated, e)
                    act.activation(xgT[:, s % 2, :, :].rearrange("p k n -> p (k n)"), psT[:, s % 2, :], ACT.Copy).then_inc(xgT_ready, 1)

                def body(i, s):
                    e = i * R + s
                    act.wait_ge(gated, e + 2)
                    act.wait_ge(hid_ready, e + 1)
                    act.activation(act_g[:], psG[:, s % 2, 0:F], ACT.Silu).then_inc(silu_done, 1)
                    if not is_last(i, s):
                        take_rows(i, s + 1)

                take_rows(0, 0)
                rounds(act, body)

            @block.vector
            def _(dve):
                def copy_out(i, s):
                    e, before = i * R + s, (s - 1) % 2
                    dve.wait_ge(down, e + 1)
                    dve.wait_ge(stored[before], 16 * (i * (R // 2) + (s - 1) // 2) + 1)
                    dve.tensor_copy(out[:, before, :], psO[:, before, :]).then_inc(out_ready, 1)

                def body(i, s):
                    e = i * R + s
                    dve.wait_ge(silu_done, e + 2)
                    dve.wait_ge(hid_turned, e + 1)
                    dve.tensor_tensor(hid[:], act_g[:], psG[:, s % 2, F:2 * F], ALU.mult).then_inc(hid_ready, 1)
                    if not is_first(i, s):
                        copy_out(i, s)
                    dve.wait_ge(hid_turned, e + 2)
                    dve.wait_ge(down, e + 1)
                    dve.tensor_copy(hT[:].rearrange("p f n -> p (f n)"), psH[0:FH, 0:2 * P]).then_inc(hT_ready, 1)

                rounds(dve, body)
                copy_out(E // R, 0)



def combine_and_shared_expert(nc, g, name, slots, K, zT, F, w_gate, w_up, w_down):
    FT, G = F // P, 512
    GT = G // P
    with Stage(nc, name) as st:
        wg = st.sb("wg", [P, KD, F])
        wu = st.sb("wu", [P, KD, F])
        wd = st.sb("wd", [P, FT, D])
        act_g = st.sb("act_g", [P, FT, G])
        hT = st.sb("hT", [P, FT, G])
        gather = Gather(g, st, K, slots)
        z = st.sb("z", [P, D])
        psG = st.ps("psG", [P, 2, FT, G])
        psO = st.ps("psO", [P, 2, D])
        own_dve = st.sem("own_dve")
        w_in = st.sem("w_in")
        gated = st.sem("gated")
        silu_done = st.sem("silu_done")
        h_ready = st.sem("h_ready")
        down = st.sem("down")
        added = st.sem("added")
        with st.block() as block:

            @block.sync
            def _(sp):
                for dst, src in ((wg, w_gate), (wu, w_up), (wd, w_down)):
                    sp.dma_start(dst[:], channels_first(src)).then_inc(w_in, 16)

            @block.gpsimd
            def _(pool):
                gather.rows_of_tiles(pool)

            @block.tensor
            def _(pe):
                pe.wait_ge(w_in, 49)
                with pe.Fori(0, T // G) as i:
                    pe.wait_ge(h_ready, i * FT + 1)
                    for f in range(FT):
                        for half, w in enumerate((wg, wu)):
                            for k in range(KD):
                                last = pe.matmul(psG[:, half, f, :], w[:, k, f * P:(f + 1) * P], zT[:, k, ds(i * G, G)],
                                                 start=(k == 0), stop=(k == KD - 1))
                            last.then_inc(gated, 1)
                    pe.wait_ge(h_ready, (i + 1) * FT + 1)
                    for j in range(GT):
                        pe.wait_ge(added, (i * GT + j - 1 if j else i * GT) + 1)
                        for f in range(FT):
                            last = pe.matmul(psO[:, j % 2, :], hT[:, f, j * P:(j + 1) * P], wd[:, f, :],
                                             start=(f == 0), stop=(f == FT - 1))
                        last.then_inc(down, 1)

            @block.scalar
            def _(act):
                with act.Fori(0, T // G) as i:
                    for f in range(FT):
                        act.wait_ge(gated, i * 2 * FT + 2 * f + 2)
                        act.wait_ge(h_ready, i * FT + 1)
                        act.activation(act_g[:, f, :], psG[:, 0, f, :], ACT.Silu).then_inc(silu_done, 1)

            @block.vector
            def _(dve):
                own = Own(dve, own_dve)
                with dve.Fori(0, T // G) as i:
                    own.turn(i, GT * (2 + K - 1))
                    for j in range(GT):
                        t = i * GT + j
                        x_tile = g.x[:, ds(t, 1), :].rearrange("p a n -> p (a n)")
                        own.link(dve.tensor_scalar(z[:], x_tile, g.mean[:, ds(t, 1)], g.ln_rstd[:, ds(t, 1)], ALU.subtract, ALU.mult))
                        own.link(dve.tensor_tensor(x_tile, x_tile, z[:], ALU.add))
                        gather.add_rows(dve, own, t, i * (GT // 2) + j // 2, j % 2, x_tile)
                    for f in range(FT):
                        dve.wait_ge(gated, i * 2 * FT + 2 * f + 2 + 1)
                        dve.wait_ge(silu_done, i * FT + f + 2)
                        dve.wait_ge(down, i * GT + 1)
                        dve.tensor_tensor(hT[:, f, :], act_g[:, f, :], psG[:, 1, f, :], ALU.mult).then_inc(h_ready, 1)
                    for j in range(GT):
                        dve.wait_ge(down, i * GT + j + 2)
                        x_tile = g.x[:, ds(i * GT + j, 1), :].rearrange("p a n -> p (a n)")
                        dve.tensor_tensor(x_tile, x_tile, psO[:, j % 2, :], ALU.add).then_inc(added, 1)
                own.turns_over(T // G)


class SoftRouter:
    LOADS = 2

    def __init__(self, g, E, n, gateT, bias):
        self.g, self.E, self.n, self.gateT, self.bias = g, E, n, gateT, bias
        self.STEPS = 17

    def allocate(self, st):
        E, n = self.E, self.n
        self.wg = st.sb("wg", [P, KD, E])
        self.bias_sb = st.sb("bias", [P, E])
        self.iota = st.sb("iota", [P, E])
        self.iota_i = st.sb("iota_i", [P, E], I32)
        self.logits = st.sb("logits", [P, Q, E])
        self.best = st.sb("best", [P, Q, 8])
        self.which = st.sb("which", [P, Q, 8], U32)
        self.which_f = st.sb("which_f", [P, Q, n])
        self.e_all = st.sb("e_all", [P, Q, E])
        self.total = st.sb("total", [P, 2, Q])
        self.onehot = st.sb("onehot", [P, Q * n, E])
        self.mask = st.sb("mask", [P, Q, E])
        self.psR = st.ps("psR", [P, NG, 512])
        self.router_in = st.sem("router_in")
        self.iotas = st.sem("iotas")
        self.tick = st.sem("tick")
        self.logits_done = st.sem("logits_done")
        self.clamped = st.sem("clamped")
        self.exps_done = st.sem("exps_done")

    def load(self, sp):
        sp.dma_start(self.wg[:], self.gateT).then_inc(self.router_in, 16)
        sp.dma_start(self.bias_sb[:], self.bias.rearrange("(a n) -> a n", a=1).broadcast_to([P, self.E])).then_inc(self.router_in, 16)

    def prepare(self, dve, own):
        dve.wait_ge(self.iotas, 2)
        dve.wait_ge(self.router_in, 33)
        own.link(dve.tensor_copy(self.iota[:], self.iota_i[:]))

    logits_of = Router.logits_of

    def count(self, pe, r):
        pass

    def exponentials(self, act, r):
        act.wait_ge(self.clamped, r + 2)
        act.activation(self.e_all[:], self.logits[:], ACT.Exp).then_inc(self.exps_done, 1)

    def choose(self, dve, own, i, s):
        E, n, r = self.E, self.n, i * 2 + s
        lg, top = self.logits, self.best
        spread = lambda ap: ap.unsqueeze(2).broadcast_to([P, Q, E])
        dve.wait_ge(self.logits_done, r * Q + Q + 1)
        own.link(dve.tensor_tensor(lg[:], self.psR[:, ds(r, 1), 0:Q * E].rearrange("p a (j e) -> p (a j) e", j=Q),
                                   self.bias_sb[:].unsqueeze(1).broadcast_to([P, Q, E]), ALU.add))
        take_wait(dve, self.tick)
        for j in range(Q):
            own.step(dve.max(top[:, j, :], lg[:, j, :]))
        own.settle()
        take_wait(dve, self.tick)
        for j in range(Q):
            own.step(dve.max_index(self.which[:, j, :], top[:, j, :], lg[:, j, :]))
        own.settle()
        own.link(dve.tensor_copy(self.which_f[:], self.which[:, :, 0:n]))
        own.link(dve.tensor_tensor(self.onehot[:], self.iota[:].unsqueeze(1).broadcast_to([P, Q * n, E]),
                                   self.which_f[:].rearrange("p j k -> p (j k)").unsqueeze(2).broadcast_to([P, Q * n, E]), ALU.is_equal))
        own.link(dve.tensor_reduce(self.mask[:], self.onehot[:].rearrange("p (j k) e -> p j e k", j=Q), AX.X, ALU.add))
        dve.tensor_tensor(lg[:], lg[:], spread(top[:, :, 0]), ALU.subtract).then_inc(self.clamped, 1)
        dve.wait_ge(self.exps_done, r + 2)
        own.link(dve.tensor_tensor(self.e_all[:], self.e_all[:], self.mask[:], ALU.mult))
        own.link(dve.tensor_reduce(self.total[:, 0, :], self.e_all[:], AX.X, ALU.add))
        own.link(dve.reciprocal(self.total[:, 1, :], self.total[:, 0, :]))
        own.link(dve.tensor_tensor(self.e_all[:], self.e_all[:], spread(self.total[:, 1, :]), ALU.mult))
        own.link(dve.tensor_copy(of_group(self.g.weight_of, r)[:, :, 0:E], self.e_all[:]))

    def scatter(self, pool):
        pool.iota(self.iota_i[:], [[1, self.E]], base=0, channel_multiplier=0).then_inc(self.iotas, 1)


def soft_experts(nc, g, name, zT, N, F, w_gate, b_gate, w_up, b_up, w_down, b_down, s_up, sb_up, s_down, sb_down, nf4):
    FT, G, ST = F // P, 512, 512 // P
    GT, NG = G // P, T // G
    with Stage(nc, name) as st:
        wa = st.sb("wa", [P, 2, KD, 2 * F])
        wd = st.sb("wd", [P, 2, FT, D])
        cols = st.sb("cols", [P, 2, N, FT])
        cols_s = st.sb("cols_s", [P, ST])
        bd = st.sb("bd", [P, N, D])
        bs = st.sb("bs", [P, D])
        ws = st.sb("ws", [P, KD, 512])
        wsd = st.sb("wsd", [P, ST, D])
        act_g = st.sb("act_g", [P, 2, G])
        hT = st.sb("hT", [P, ST, G])
        tmp = st.sb("tmp", [P, 2, D])
        psG = st.ps("psG", [P, 2 * FT, G])
        psO = st.ps("psO", [P, 2, D])
        consts_in = st.sem("consts_in")
        w_in = st.sems_of("w_in", 2)
        gated = st.sem("gated")
        silu_done = st.sem("silu_done")
        h_ready = st.sem("h_ready")
        down = st.sem("down")
        taken = st.sem("taken")
        own_dve = st.sem("own_dve")
        s_gated = st.sem("s_gated")
        s_h = st.sem("s_h")
        s_down_done = st.sem("s_down_done")
        s_taken = st.sem("s_taken")
        nf4.allocate(st)
        with st.block() as block:

            @block.sync
            def _(sp):
                for dst, src in ((ws[:], channels_first(s_up)), (cols_s[:], sb_up), (cols[:, 0, :, :], b_gate), (cols[:, 1, :, :], b_up),
                                 (wsd[:], channels_first(s_down)), (bs[:], sb_down.rearrange("(a n) -> a n", a=1).broadcast_to([P, D])),
                                 (bd[:].rearrange("p n d -> p (n d)"), b_down.rearrange("(a n) d -> a (n d)", a=1).broadcast_to([P, N * D]))):
                    sp.dma_start(dst, src).then_inc(consts_in, 16)

                def load(e, s):
                    for dst, src, k in ((wa[:, s, :, 0:F], w_gate, P), (wa[:, s, :, F:2 * F], w_up, P), (wd[:, s, :, :], w_down, P)):
                        sp.dma_start(dst, src[ds(e, 1), :, :].rearrange("e (k p) n -> p (e k) n", p=P)).then_inc(w_in[s], 16)

                for s in range(2):
                    load(s, s)
                with sp.Fori(1, N // 2) as i:
                    for s in range(2):
                        sp.wait_ge(down, (i * 2 + s - 1) * NT + 1)
                        load(i * 2 + s, s)

            @block.tensor
            def _(pe):
                pe.wait_ge(consts_in, 113)
                with pe.Fori(0, NG) as i:
                    pe.wait_ge(s_h, i * ST + 1)
                    for f in range(ST):
                        for k in range(KD):
                            last = pe.matmul(psG[:, f, :], ws[:, k, f * P:(f + 1) * P], zT[:, k, ds(i * G, G)],
                                             start=(k == 0), stop=(k == KD - 1))
                        last.then_inc(s_gated, 1)
                    pe.wait_ge(s_h, (i + 1) * ST + 1)
                    for j in range(GT):
                        pe.wait_ge(s_taken, (i * GT + j - 1 if j else i * GT) + 1)
                        for f in range(ST):
                            last = pe.matmul(psO[:, j % 2, :], hT[:, f, j * P:(j + 1) * P], wsd[:, f, :],
                                             start=(f == 0), stop=(f == ST - 1))
                        last.then_inc(s_down_done, 1)
                pe.wait_ge(s_taken, NT + 1)
                with pe.Fori(0, N // 2) as e2:
                    def gate_up(part, f):
                        e, s, i = e2 * 2 + part // NG, part // NG, part % NG
                        u = e * NG + i
                        if f == 0 and i == 0:
                            pe.wait_ge(w_in[s], e2 * 48 + 48 + 1)
                        pe.wait_ge(h_ready, (u - 1) * FT + f + 2 if part else u * FT + 1)
                        for half in range(2):
                            for k in range(KD):
                                last = pe.matmul(psG[:, half * FT + f, :], wa[:, s, k, half * F + f * P:half * F + (f + 1) * P],
                                                 zT[:, k, i * G:(i + 1) * G], start=(k == 0), stop=(k == KD - 1))
                            last.then_inc(gated, 1)

                    def multiply_down(part):
                        s, u = part // NG, (e2 * 2 + part // NG) * NG + part % NG
                        pe.wait_ge(h_ready, (u + 1) * FT + 1)
                        for j in range(GT):
                            pe.wait_ge(taken, (u * GT + j - 1 if j else u * GT) + 1)
                            for f in range(FT):
                                last = pe.matmul(psO[:, j % 2, :], hT[:, part % 2 * FT + f, j * P:(j + 1) * P], wd[:, s, f, :],
                                                 start=(f == 0), stop=(f == FT - 1))
                            last.then_inc(down, 1)

                    for part in range(2 * NG):
                        gate_up(part, 0)
                        if part:
                            multiply_down(part - 1)
                        if part == 4:
                            nf4.sum_scalers(pe, e2)
                        gate_up(part, 1)
                    multiply_down(2 * NG - 1)

            @block.scalar
            def _(act):
                act.wait_ge(consts_in, 113)
                with act.Fori(0, NG) as i:
                    for f in range(ST):
                        act.wait_ge(s_gated, i * ST + f + 2)
                        act.wait_ge(s_down_done, i * GT + 1)
                        act.activation(hT[:, f, :], psG[:, f, :], ACT.Silu, bias=cols_s[:, f:f + 1]).then_inc(s_h, 1)
                with act.Fori(0, N) as e:
                    with act.Fori(0, NG) as i:
                        u = e * NG + i
                        for f in range(FT):
                            act.wait_ge(gated, u * 2 * FT + 2 * f + 2)
                            act.wait_ge(h_ready, u * FT + 1)
                            act.activation(act_g[:, f, :], psG[:, f, :], ACT.Silu,
                                           bias=cols[:, 0, ds(e, 1), f:f + 1].rearrange("p a b -> p (a b)")).then_inc(silu_done, 1)

            @block.vector
            def _(dve):
                own = Own(dve, own_dve)
                dve.wait_ge(consts_in, 113)
                with dve.Fori(0, NT // 2) as i:
                    own.turn(i, 2)
                    for s in range(2):
                        dve.wait_ge(s_down_done, i * 2 + s + 2)
                        x_tile = g.x[:, ds(i * 2 + s, 1), :].rearrange("p a n -> p (a n)")
                        own.link(dve.tensor_tensor(tmp[:, s, :], psO[:, s, :], bs[:], ALU.add))
                        dve.tensor_tensor(x_tile, x_tile, tmp[:, s, :], ALU.add).then_inc(s_taken, 1)
                own.turns_over(NT // 2)
                own_nf4 = Own(dve, nf4.own_nf4)
                with dve.Fori(0, N // 2) as e2:
                    own_nf4.turn(e2, nf4.STEPS)

                    def gate(part, f):
                        e, i = e2 * 2 + part // NG, part % NG
                        u = e * NG + i
                        dve.wait_ge(gated, u * 2 * FT + 2 * f + 2 + 1)
                        dve.wait_ge(silu_done, u * FT + f + 2)
                        dve.wait_ge(down, (u - 1) * GT + 1 if part else u * GT + 1)
                        dve.scalar_tensor_tensor(hT[:, part % 2 * FT + f, :], psG[:, FT + f, :],
                                                 cols[:, 1, ds(e, 1), f:f + 1].rearrange("p a b -> p (a b)"),
                                                 act_g[:, f, :], ALU.add, ALU.mult).then_inc(h_ready, 1)

                    def add_weighted(part):
                        e, i = e2 * 2 + part // NG, part % NG
                        for j in range(GT):
                            n = (e * NG + i) * GT + j
                            dve.wait_ge(down, n + 2)
                            dve.tensor_tensor(tmp[:, j % 2, :], psO[:, j % 2, :], bd[:, ds(e, 1), :].rearrange("p a n -> p (a n)"),
                                              ALU.add).then_inc(taken, 1)
                            dve.wait_ge(taken, n + 2)
                            x_tile = g.x[:, i * GT + j, :]
                            dve.scalar_tensor_tensor(x_tile, tmp[:, j % 2, :], g.weight_of[:, i * GT + j, ds(e, 1)],
                                                     x_tile, ALU.mult, ALU.add).then_inc(own_dve, 1)

                    for part in range(2 * NG):
                        gate(part, 0)
                        if part:
                            add_weighted(part - 1)
                            nf4.quantize(dve, own_nf4, e2, part - 1)
                        gate(part, 1)
                    add_weighted(2 * NG - 1)
                    nf4.quantize(dve, own_nf4, e2, 2 * NG - 1)
                own_nf4.turns_over(N // 2)

            @block.gpsimd
            def _(pool):
                nf4.move(pool)



def feature_attention(nc, g, name, zT, wqT, bq, wkT, bk):
    MT = L // P
    with Stage(nc, name) as st:
        ctxT = st.sb("ctxT", [P, KC, T])
        wq = st.sb("wq", [P, KC, P])
        wk = st.sb("wk", [P, KC, P])
        bias = st.sb("bias", [P, 2])
        qkT = st.sb("qkT", [P, 2, L])
        att = st.sb("att", [P, MT, L])
        attT = st.sb("attT", [P, MT, L])
        zs = st.sb("zs", [P, KD, L])
        top = st.sb("top", [P, MT])
        den = st.sb("den", [P, MT])
        psQ = st.ps("psQ", [P, 2, L])
        psE = st.ps("psE", [P, 2, L])
        psT = st.ps("psT", [P, 2, L])
        psO = st.ps("psO", [P, 2, L])
        w_in = st.sem("w_in")
        projected = st.sem("projected")
        qk_ready = st.sem("qk_ready")
        scored = st.sem("scored")
        maxed = st.sem("maxed")
        exps = st.sem("exps")
        inverse = st.sem("inverse")
        att_ready = st.sem("att_ready")
        turned = st.sem("turned")
        attT_ready = st.sem("attT_ready")
        z_copied = st.sem("z_copied")
        mixed = st.sem("mixed")
        added = st.sem("added")

        def sequences(eng, front, turn, back):
            front(0)
            with eng.Fori(0, B - 1) as b:
                turn(b)
                front(b + 1)
                back(b)
            turn(B - 1)
            back(B - 1)

        with st.block() as block:

            @block.sync
            def _(sp):
                for dst, src in ((ctxT[:], g.ctxT), (wq[:], wqT), (wk[:], wkT), (bias[:, 0:1], bq.rearrange("(n a) -> n a", a=1)),
                                 (bias[:, 1:2], bk.rearrange("(n a) -> n a", a=1))):
                    sp.dma_start(dst, src).then_inc(w_in, 16)

            @block.tensor
            def _(pe):
                pe.wait_ge(w_in, 81)

                def front(b):
                    pe.wait_ge(qk_ready, b * 2 + 1)
                    for half, w in enumerate((wq, wk)):
                        for k in range(KC):
                            last = pe.matmul(psQ[:, half, :], w[:, k, :], ctxT[:, k, ds(b * L, L)], start=(k == 0), stop=(k == KC - 1))
                        last.then_inc(projected, 1)
                    pe.wait_ge(qk_ready, b * 2 + 2 + 1)
                    for j in range(MT):
                        pe.wait_ge(exps, (b * MT + j - 1 if j else b * MT) + 1)
                        pe.matmul(psE[:, j % 2, :], qkT[:, 0, j * P:(j + 1) * P], qkT[:, 1, :], start=True, stop=True).then_inc(scored, 1)

                def turn(b):
                    pe.wait_ge(att_ready, (b + 1) * MT + 1)
                    for k in range(MT):
                        pe.wait_ge(attT_ready, (b * MT + k - 1 if k else b * MT) + 1)
                        for j in range(MT):
                            last = pe.transpose(psT[:, k % 2, j * P:(j + 1) * P], att[:, j, k * P:(k + 1) * P], g.ident[:])
                        last.then_inc(turned, 1)

                def back(b):
                    pe.wait_ge(attT_ready, (b + 1) * MT + 1)
                    pe.wait_ge(z_copied, b + 2)
                    for j in range(LT):
                        pe.wait_ge(added, (b * LT + j - 1 if j else b * LT) + 1)
                        for k in range(MT):
                            last = pe.matmul(psO[:, j % 2, :], zs[:, k, j * P:(j + 1) * P], attT[:, k, :], start=(k == 0), stop=(k == MT - 1))
                        last.then_inc(mixed, 1)

                sequences(pe, front, turn, back)

            @block.scalar
            def _(act):
                act.wait_ge(w_in, 81)

                def front(b):
                    for half in range(2):
                        act.wait_ge(projected, b * 2 + half + 2)
                        act.wait_ge(scored, b * MT + 1)
                        act.activation(qkT[:, half, :], psQ[:, half, :], ACT.Identity, bias=bias[:, half:half + 1]).then_inc(qk_ready, 1)
                    for j in range(MT):
                        act.wait_ge(maxed, b * MT + j + 2)
                        act.wait_ge(turned, b * MT + 1)
                        act.activation(att[:, j, :], psE[:, j % 2, :], ACT.Exp, bias=top[:, j:j + 1], accum_out=den[:, j:j + 1]).then_inc(exps, 1)

                def turn(b):
                    for k in range(MT):
                        act.wait_ge(turned, b * MT + k + 2)
                        act.wait_ge(mixed, b * LT + 1)
                        act.activation(attT[:, k, :], psT[:, k % 2, :], ACT.Copy).then_inc(attT_ready, 1)

                sequences(act, front, turn, lambda b: None)

            @block.vector
            def _(dve):
                def front(b):
                    for j in range(MT):
                        dve.wait_ge(scored, b * MT + j + 2)
                        dve.wait_ge(exps, b * MT + 1)
                        dve.wait_ge(inverse, b * MT + 1)
                        dve.tensor_reduce(top[:, j:j + 1], psE[:, j % 2, :], AX.X, ALU.max, negate=True).then_inc(maxed, 1)
                    for j in range(MT):
                        dve.wait_ge(exps, b * MT + j + 2)
                        dve.reciprocal(den[:, j:j + 1], den[:, j:j + 1]).then_inc(inverse, 1)
                        dve.wait_ge(inverse, b * MT + j + 2)
                        dve.tensor_scalar(att[:, j, :], att[:, j, :], den[:, j:j + 1], None, ALU.mult).then_inc(att_ready, 1)

                def back(b):
                    for j in range(LT):
                        dve.wait_ge(mixed, b * LT + j + 2)
                        x_tile = g.x[:, ds(b * LT + j, 1), :].rearrange("p a n -> p (a n)")
                        dve.tensor_tensor(x_tile, x_tile, psO[:, j % 2, :], ALU.add).then_inc(added, 1)

                sequences(dve, front, lambda b: None, back)

            @block.gpsimd
            def _(pool):
                with pool.Fori(0, B) as b:
                    pool.wait_ge(mixed, b * LT + 1)
                    pool.tensor_copy(zs[:], zT[:, :, ds(b * L, L)]).then_inc(z_copied, 1)



def cross_attention(nc, g, name, zT, wq, wk, wv, wo, gq, gk):
    H, J = 16, L // P
    SCALE = P ** -0.5
    with Stage(nc, name) as st:
        ctxT = st.sb("ctxT", [P, KC, T])
        wo_sb = st.sb("wo", [P, H, D])
        w_head = st.sb("w_head", [P, 2, 8, P])
        gains = st.sb("gains", [P, 2])
        gain = st.sb("gain", [P, 1])
        eps = st.sb("eps", [P, 1])
        cs = st.sb("cs", [P, KC, L])
        qT = st.sb("qT", [P, 2, L])
        kT = st.sb("kT", [P, 2, L])
        v = st.sb("v", [P, 2, J, P])
        sq = st.sb("sq", [P, 2, L])
        rk = st.sb("rk", [P, L])
        rq = st.sb("rq", [P, 2, J])
        top = st.sb("top", [P, J])
        den = st.sb("den", [P, J])
        prob = st.sb("prob", [P, J, L])
        probT = st.sb("probT", [P, J, L])
        oT = st.sb("oT", [P, H, L])
        psP = st.ps("psP", [P, 2, L])
        psV = st.ps("psV", [P, J, P])
        psK = st.ps("psK", [P, L])
        psS = st.ps("psS", [P, 2, L])
        psT = st.ps("psT", [P, 2, L])
        w_in = st.sem("w_in")
        wo_in = g.pool_sem(f"{name}_wo_in")
        own_dve = st.sem("own_dve")
        own_act = st.sem("own_act")
        head_in = st.sems_of("head_in", 2)
        projected = st.sem("projected")
        squared = st.sem("squared")
        copied = st.sem("copied")
        summed = st.sem("summed")
        rk_ready = st.sem("rk_ready")
        front_done = st.sem("front_done")
        scored = st.sem("scored")
        maxed = st.sem("maxed")
        exps = st.sem("exps")
        inverse = st.sem("inverse")
        prob_ready = st.sem("prob_ready")
        turned = st.sem("turned")
        probT_ready = st.sem("probT_ready")
        mixed = st.sem("mixed")
        out_copied = st.sem("out_copied")
        ctx_copied = st.sem("ctx_copied")
        y_done = st.sem("y_done")
        added = st.sem("added")
        q_taken = st.sem("q_taken")
        kT_ready = st.sem("kT_ready")
        reduced = st.sem("reduced")

        with st.block() as block:

            @block.sync
            def _(sp):
                for dst, src in ((ctxT[:], g.ctxT), (gains[:, 0:1], gq.rearrange("(n a) -> n a", a=1)),
                                 (gains[:, 1:2], gk.rearrange("(n a) -> n a", a=1))):
                    sp.dma_start(dst, src).then_inc(w_in, 16)
                with sp.Fori(0, B) as b:
                    with sp.Fori(0, H // 2) as i:
                        for s in range(2):
                            sp.wait_ge(projected, (b * H + i * 2) * 3 + 1)
                            for k0, k1, w in ((0, 4, wq), (4, 6, wk), (6, 8, wv)):
                                sp.dma_start(w_head[:, s, k0:k1, :], w[:, :, ds(i * (2 * P) + s * P, P)]).then_inc(head_in[s], 16)

            def turns(eng, front, back, end):
                with eng.Fori(0, B) as b:
                    front(b, b * H, 0)
                    with eng.Fori(0, H // 2 - 1) as i:
                        for s in range(2):
                            back(b, i * 2 + s, b * H + i * 2 + s, s, True)
                    back(b, H - 2, b * H + H - 2, 0, True)
                    back(b, H - 1, b * H + H - 1, 1, False)
                    end(b)

            @block.tensor
            def _(pe):
                pe.wait_ge(w_in, 49)

                def project_q(b, m, s):
                    pe.wait_ge(head_in[s], (m + 2) * 24 + 1 if s == 0 else (m + 1) * 24 + 1)
                    for k in range(KD):
                        last = pe.matmul(psP[:, 0, :], w_head[:, s, k, :], zT[:, k, ds(b * L, L)], start=(k == 0), stop=(k == KD - 1))
                    last.then_inc(projected, 1)

                def project_kv(b, m, s):
                    pe.wait_ge(kT_ready, m + 1)
                    for k in range(KC):
                        last = pe.matmul(psP[:, 1, :], w_head[:, s, 4 + k, :], ctxT[:, k, ds(b * L, L)], start=(k == 0), stop=(k == KC - 1))
                    last.then_inc(projected, 1)
                    pe.wait_ge(ctx_copied, b + 2)
                    pe.wait_ge(rk_ready, m * 2 + 1)
                    for j in range(J):
                        for k in range(KC):
                            last = pe.matmul(psV[:, j, :], cs[:, k, j * P:(j + 1) * P], w_head[:, s, 6 + k, :], start=(k == 0), stop=(k == KC - 1))
                    last.then_inc(projected, 1)
                    pe.wait_ge(squared, m * 2 + 3)
                    pe.matmul(psK[:], g.ones[:], sq[:, 1, :], start=True, stop=True).then_inc(summed, 1)

                def sum_q(m):
                    pe.wait_ge(copied, m + 2)
                    for j in range(J):
                        last = pe.matmul(psV[:, 0, j:j + 1], sq[:, 0, j * P:(j + 1) * P], g.ones[:, 0:1], start=True, stop=True)
                    last.then_inc(summed, 1)

                def front(b, m, s):
                    project_q(b, m, s)
                    project_kv(b, m, s)
                    sum_q(m)

                def scores(m, s, tiles):
                    for j in tiles:
                        pe.wait_ge(exps, m * J + j if j else m * J + 1)
                        pe.matmul(psS[:, j % 2, :], qT[:, s, j * P:(j + 1) * P], kT[:, s, :], start=True, stop=True).then_inc(scored, 1)

                def back(b, h, m, s, more):
                    pe.wait_ge(q_taken, m + 2)
                    pe.wait_ge(kT_ready, m + 2)
                    scores(m, s, (0, 1))
                    if more:
                        pe.wait_ge(out_copied, m + 1)
                        project_q(b, m + 1, 1 - s)
                    scores(m, s, (2, 3))
                    if more:
                        project_kv(b, m + 1, 1 - s)
                    pe.wait_ge(prob_ready, (m + 1) * J + 1)
                    for k in range(J):
                        pe.wait_ge(probT_ready, m * J + k if k else m * J + 1)
                        for j in range(J):
                            last = pe.transpose(psT[:, k % 2, j * P:(j + 1) * P], prob[:, j, k * P:(k + 1) * P], g.ident[:])
                        last.then_inc(turned, 1)
                    if more:
                        sum_q(m + 1)
                        pe.wait_ge(q_taken, m + 3)
                    for k in range(J):
                        pe.wait_ge(probT_ready, m * J + k + 2)
                        last = pe.matmul(psP[:, 0, :], v[:, s, k, :], probT[:, k, :], start=(k == 0), stop=(k == J - 1))
                    last.then_inc(mixed, 1)

                def end(b):
                    pe.wait_ge(wo_in, 16)
                    pe.wait_ge(out_copied, (b + 1) * H + 1)
                    for j in range(J):
                        pe.wait_ge(added, b * J + j if j else b * J + 1)
                        for h in range(H):
                            last = pe.matmul(psS[:, j % 2, :], oT[:, h, j * P:(j + 1) * P], wo_sb[:, h, :], start=(h == 0), stop=(h == H - 1))
                        last.then_inc(y_done, 1)
                    pe.wait_ge(added, (b + 1) * J + 1)

                turns(pe, front, back, end)

            @block.scalar
            def _(act):
                act.wait_ge(own_dve, 3)
                act.preload_act_table_set("natural_log_exp_and_others")

                def take_q(m, s):
                    act.wait_ge(projected, m * 3 + 2)
                    act.wait_ge(summed, m * 2 + 1)
                    act.activation(sq[:, 0, :], psP[:, 0, :], ACT.Square).then_inc(squared, 1)
                    act.activation(qT[:, s, :], psP[:, 0, :], ACT.Copy, scale=gain[:]).then_inc(q_taken, 1)

                def take_kv(m, s):
                    act.wait_ge(projected, m * 3 + 3)
                    act.activation(sq[:, 1, :], psP[:, 1, :], ACT.Square).then_inc(squared, 1)
                    act.wait_ge(projected, m * 3 + 4)
                    act.activation(v[:, s, :, :], psV[:], ACT.Copy).then_inc(copied, 1)
                    act.wait_ge(summed, m * 2 + 2)
                    act.wait_ge(kT_ready, m + 1)
                    act.activation(rk[:], psK[:], ACT.Ln, bias=eps[:], scale=1.0 / P).then_inc(own_act, 1)
                    act.wait_ge(own_act, m * 2 + 2)
                    act.activation(rk[:], rk[:], ACT.Exp, scale=-0.5).then_inc(rk_ready, 1)

                def norm_q(m, s):
                    act.wait_ge(summed, m * 2 + 3)
                    act.activation(rq[:, s, :], psV[:, 0, 0:J], ACT.Ln, bias=eps[:], scale=1.0 / P).then_inc(own_act, 1)
                    act.wait_ge(own_act, m * 2 + 3)
                    act.activation(rq[:, s, :], rq[:, s, :], ACT.Exp, scale=-0.5).then_inc(rk_ready, 1)

                def front(b, m, s):
                    take_q(m, s)
                    take_kv(m, s)
                    norm_q(m, s)

                def exponentials(m, s, tiles):
                    for j in tiles:
                        act.wait_ge(maxed, m * J + j + 2)
                        act.wait_ge(turned, m * J + 1)
                        act.activation(prob[:, j, :], psS[:, j % 2, :], ACT.Exp, bias=top[:, j:j + 1], scale=rq[:, s, j:j + 1],
                                       accum_out=den[:, j:j + 1]).then_inc(exps, 1)

                def back(b, h, m, s, more):
                    exponentials(m, s, (0, 1))
                    if more:
                        take_q(m + 1, 1 - s)
                    exponentials(m, s, (2, 3))
                    if more:
                        take_kv(m + 1, 1 - s)
                        norm_q(m + 1, 1 - s)
                    act.wait_ge(mixed, m + 2)
                    act.activation(oT[:, ds(h, 1), :], psP[:, 0:1, :], ACT.Copy).then_inc(out_copied, 1)

                turns(act, front, back, lambda b: act.wait_ge(y_done, (b + 1) * J + 1))

            @block.vector
            def _(dve):
                dve.wait_ge(w_in, 49)
                dve.memset(eps[:], 1e-5).then_inc(own_dve, 1)
                dve.tensor_tensor(gain[:], gains[:, 0:1], gains[:, 1:2], ALU.mult).then_inc(own_dve, 1)

                def norm_k(m, s):
                    dve.wait_ge(rk_ready, m * 2 + 2)
                    dve.tensor_tensor(kT[:, s, :], psP[:, 1, :], rk[:], ALU.mult).then_inc(kT_ready, 1)

                def scale_q(m, s):
                    dve.wait_ge(rk_ready, m * 2 + 3)
                    dve.tensor_scalar(rq[:, s, :], rq[:, s, :], SCALE, None, ALU.mult).then_inc(front_done, 1)

                def front(b, m, s):
                    norm_k(m, s)
                    scale_q(m, s)

                def back(b, h, m, s, more):
                    dve.wait_ge(front_done, m + 2)
                    for j in range(J):
                        n = m * J + j
                        dve.wait_ge(scored, n + 2)
                        dve.wait_ge(exps, m * J + 1)
                        dve.tensor_reduce(top[:, j:j + 1], psS[:, j % 2, :], AX.X, ALU.max, negate=True).then_inc(reduced, 1)
                        dve.wait_ge(reduced, n + 2)
                        dve.tensor_tensor(top[:, j:j + 1], top[:, j:j + 1], rq[:, s, j:j + 1], ALU.mult).then_inc(maxed, 1)
                    for j in range(J):
                        n = m * J + j
                        dve.wait_ge(exps, n + 2)
                        dve.reciprocal(den[:, j:j + 1], den[:, j:j + 1]).then_inc(inverse, 1)
                        dve.wait_ge(inverse, n + 2)
                        dve.tensor_scalar(prob[:, j, :], prob[:, j, :], den[:, j:j + 1], None, ALU.mult).then_inc(prob_ready, 1)
                    for k in range(J):
                        dve.wait_ge(turned, m * J + k + 2)
                        dve.wait_ge(mixed, m + 1)
                        dve.tensor_copy(probT[:, k, :], psT[:, k % 2, :]).then_inc(probT_ready, 1)
                    if more:
                        norm_k(m + 1, 1 - s)
                        scale_q(m + 1, 1 - s)

                def end(b):
                    for j in range(J):
                        dve.wait_ge(y_done, b * J + j + 2)
                        x_tile = g.x[:, ds(b * J + j, 1), :].rearrange("p a n -> p (a n)")
                        dve.tensor_tensor(x_tile, x_tile, psS[:, j % 2, :], ALU.add).then_inc(added, 1)

                turns(dve, front, back, end)

            @block.gpsimd
            def _(pool):
                pool.wait_ge(w_in, 49)
                pool.tensor_copy(cs[:], ctxT[:, :, 0:L]).then_inc(ctx_copied, 1)
                pool.wait_ge(projected, 2)
                pool.dma_start(wo_sb[:], channels_first(wo)).then_inc(wo_in, 16)
                with pool.Fori(1, B) as b:
                    pool.wait_ge(projected, b * H * 3 + 1)
                    pool.tensor_copy(cs[:], ctxT[:, :, ds(b * L, L)]).then_inc(ctx_copied, 1)



NF4 = [-1.0, -0.6962, -0.5251, -0.3949, -0.2844, -0.1848, -0.0911, 0.0, 0.0796, 0.1609, 0.2461, 0.3379, 0.4407, 0.5626, 0.723, 1.0]


def bf16_round(v):
    import struct
    n = struct.unpack("<I", struct.pack("<f", v))[0]
    n = (n + 0x7FFF + ((n >> 16) & 1)) & 0xFFFF0000
    return struct.unpack("<f", struct.pack("<I", n))[0]


CODES = [bf16_round(v) for v in NF4]
FIRST_OF = [-0.84375, -0.60546875, -0.45703125, -0.337890625, -0.234375, -0.1376953125, -0.04541015625, 0.0400390625,
            0.12060546875, 0.2041015625, 0.29296875, 0.390625, 0.50390625, 0.64453125, 0.86328125]
ROUND = 12582912.0


class Nf4:
    N, BL = 5632, 64

    def __init__(self, nc, g, weights, values):
        self.g, self.weights, self.values = g, weights, values
        self.NW = weights.shape[0]
        self.NB = self.N // self.BL
        self.GP = P * self.NB // (2 * self.BL)
        self.rows = nc.dram_tensor("nf4_rows", (2, P * self.NB), BF16).ap()

    def allocate(self, st):
        N, BL, NB, GP = self.N, self.BL, self.NB, self.GP
        self.w = st.sb("nf4_w", [P, N], BF16)
        self.step = st.sb("nf4_step", [P, N // 2], BF16)
        self.above = st.sb("nf4_above", [P, N // 2], BF16)
        self.value = st.sb("nf4_value", [P, N], BF16)
        self.s1 = st.sb("nf4_s1", [P, NB], BF16)
        self.inv = st.sb("nf4_inv", [P, NB])
        self.part = st.sb("nf4_part", [P, 2])
        self.mean = st.sb("nf4_mean", [P, 1], BF16)
        self.sb_ = st.sb("nf4_sb", [GP, 2, BL], BF16)
        self.top = st.sb("nf4_top", [GP, 2], BF16)
        self.qf = st.sb("nf4_qf", [GP, 2], BF16)
        self.qi = st.sb("nf4_qi", [GP, 2])
        self.q = st.sb("nf4_q", [GP, 2, BL], BF16)
        self.qr = st.sb("nf4_qr", [GP, 2, BL])
        self.deq = st.sb("nf4_deq", [GP, 2, BL], BF16)
        self.deqs = st.sb("nf4_deqs", [P, NB], BF16)
        self.psM = st.ps("nf4_psM", [P, 512])
        self.own_nf4 = st.sem("own_nf4")
        self.s1_ready = st.sem("s1_ready")
        self.part_ready = st.sem("part_ready")
        self.mean_done = st.sem("mean_done")
        self.w_used = st.sem("w_used")
        self.deq_ready = st.sem("deq_ready")
        self.value_ready = st.sem("value_ready")
        self.value_free = st.sem("value_free")
        self.nf4_tick = st.sem("nf4_tick")
        self.w_loaded, self.s1_out, self.groups_in, self.deq_out, self.deqs_in, self.value_stored = (
            self.g.pool_sem(f"nf4_{n}") for n in ("w_loaded", "s1_out", "groups_in", "deq_out", "deqs_in", "value_stored"))

    def blocks(self, ap):
        return ap.rearrange("p (b c) -> p b c", c=self.BL)

    def spread(self, ap):
        return ap.unsqueeze(2).broadcast_to([P, self.NB, self.BL])

    def move(self, pool):
        GP, rows = self.GP, self.rows

        def after(sem, value):
            pool.wait_ge(sem, value)
            take_wait(pool, self.nf4_tick)

        def load(n):
            pool.dma_start(self.w[:], self.weights[ds(n, 1), :, :].rearrange("a p n -> p (a n)")).then_inc(self.w_loaded, 16)

        def weight(n, more):
            after(self.s1_ready, n + 2)
            pool.dma_start(rows[0].rearrange("(p n) -> p n", p=P), self.s1[:]).then_inc(self.s1_out, 16)
            after(self.s1_out, n * 16 + 16)
            pool.dma_start(self.sb_[:].rearrange("p a n -> p (a n)"), rows[0].rearrange("(p n) -> p n", p=GP)).then_inc(self.groups_in, 16)
            after(self.deq_ready, n + 2)
            pool.dma_start(rows[1].rearrange("(p n) -> p n", p=GP), self.deq[:].rearrange("p a n -> p (a n)")).then_inc(self.deq_out, 16)
            after(self.deq_out, n * 16 + 16)
            pool.dma_start(self.deqs[:], rows[1].rearrange("(p n) -> p n", p=P)).then_inc(self.deqs_in, 16)
            if more:
                after(self.w_used, n + 2)
                load(n + 1)
            after(self.value_ready, n + 2)
            pool.dma_start(self.values[ds(n, 1), :, :].rearrange("a p n -> p (a n)"), self.value[:]).then_inc(self.value_stored, 16)
            pool.wait_ge(self.value_stored, n * 16 + 16)
            pool.sem_inc(self.value_free, 1)

        load(0)
        with pool.Fori(0, self.NW - 1) as n:
            weight(n, True)
        weight(self.NW - 1, False)

    def sum_scalers(self, pe, n):
        pe.wait_ge(self.part_ready, n + 2)
        pe.matmul(self.psM[:, 0:1], self.g.ones[:], self.part[:, 0:1], start=True, stop=True).then_inc(self.mean_done, 1)

    STEPS = 2 + 11 + 2 * (15 + 13 + 1) - 1

    def quantize(self, dve, own, n, part):
        if part == 0:
            self.scale(dve, own, n)
        elif part < 7:
            if part == 5:
                self.quantize_scalers(dve, own, n)
            self.find_codes(dve, own, n, (part - 1) // 3, (part - 1) % 3 * 5)
        else:
            dve.wait_ge(self.deqs_in, n * 16 + 16)
            dve.tensor_tensor(self.blocks(self.value[:]), self.blocks(self.value[:]), self.spread(self.deqs[:]), ALU.mult).then_inc(self.value_ready, 1)

    def scale(self, dve, own, n):
        w, s1 = self.w, self.s1
        dve.wait_ge(self.w_loaded, n * 16 + 16)
        dve.tensor_reduce(s1[:], self.blocks(w[:]), AX.X, ALU.max, apply_absolute_value=True).then_inc(self.s1_ready, 1)
        dve.wait_ge(self.s1_ready, n + 2)
        own.step(dve.reciprocal(self.inv[:], s1[:]))
        dve.tensor_reduce(self.part[:, 0:1], s1[:], AX.X, ALU.add).then_inc(self.part_ready, 1)
        own.settle()
        own.link(dve.tensor_tensor(self.blocks(w[:]), self.blocks(w[:]), self.spread(self.inv[:]), ALU.mult))

    def quantize_scalers(self, dve, own, n):
        GP, BL, sb_, top, qf, qi, q, qr, deq, mean = (self.GP, self.BL, self.sb_, self.top, self.qf, self.qi, self.q,
                                                       self.qr, self.deq, self.mean)
        dve.wait_ge(self.mean_done, n + 2)
        own.link(dve.tensor_scalar(mean[:], self.psM[:, 0:1], 1.0 / (P * self.NB), None, ALU.mult))
        dve.wait_ge(self.groups_in, n * 16 + 16)
        own.link(dve.tensor_scalar(sb_[:], sb_[:], mean[0:GP, :], None, ALU.subtract))
        own.link(dve.tensor_reduce(top[:], sb_[:], AX.X, ALU.max, apply_absolute_value=True))
        own.link(dve.tensor_scalar(top[:], top[:], 2.0, None, ALU.mult))
        own.link(dve.reciprocal(qi[:], top[:]))
        own.link(dve.tensor_scalar(qf[:], qi[:], 256.0, None, ALU.mult))
        own.link(dve.tensor_tensor(q[:], sb_[:], qf[:].unsqueeze(2).broadcast_to([GP, 2, BL]), ALU.mult))
        own.link(dve.tensor_scalar(qr[:], q[:], ROUND, -ROUND, ALU.add, ALU.add))
        own.link(dve.tensor_scalar(qr[:], qr[:], -128.0, 127.0, ALU.max, ALU.min))
        own.link(dve.reciprocal(qi[:], qf[:]))
        own.link(dve.tensor_tensor(deq[:], qr[:], qi[:].unsqueeze(2).broadcast_to([GP, 2, BL]), ALU.mult))
        dve.tensor_scalar(deq[:], deq[:], mean[0:GP, :], None, ALU.add).then_inc(self.deq_ready, 1)

    def find_codes(self, dve, own, n, half, first):
        cut = slice(half * self.N // 2, (half + 1) * self.N // 2)
        scaled, value, above, step = self.w[:, cut], self.value[:, cut], self.above[:], self.step[:]
        if half == first == 0:
            dve.wait_ge(self.value_free, n + 1)
        for c in range(first, first + 5):
            code = c if c < 7 else c + 1
            compare = (FIRST_OF[c], CODES[code], ALU.is_lt if c < 7 else ALU.is_ge, ALU.mult)
            into = value if c < 7 else above
            if c in (0, 7):
                own.link(dve.tensor_scalar(into, scaled, *compare))
            else:
                own.link(dve.tensor_scalar(step, scaled, *compare))
                own.link(dve.tensor_tensor(into, into, step, ALU.min if c < 7 else ALU.max))
            if c == 14:
                out = dve.tensor_tensor(value, value, above, ALU.add)
                if half == 0:
                    own.link(out)
                else:
                    out.then_inc(self.w_used, 1)
                    dve.wait_ge(self.w_used, n + 2)


def turn_weights(nc, g, name, values, groups):
    NW, _, N = values.shape
    R = N // (4 * P)
    with Stage(nc, name) as st:
        v = st.sb("v", [P, NW, N], BF16)
        psT = st.ps("psT", [P, 4, 1024], BF16)
        v_in = st.sems_of("v_in", NW)
        turned = st.sem("turned")
        copied = [st.sem("copied_even"), st.sem("copied_odd")]
        with st.block() as block:

            @block.sync
            def _(sp):
                for n in range(NW):
                    sp.dma_start(v[:, n, :], values[n]).then_inc(v_in[n], 16)

            @block.tensor
            def _(pe):
                for n in range(NW):
                    pe.wait_ge(v_in[n], 17)
                    for r in range(R):
                        i = n * R + r
                        if i >= 4:
                            pe.wait_ge(copied[i % 2], (i - 4) // 2 + 2)
                        for q, src in enumerate(groups[n](v[:, n, :], r)[0]):
                            last = pe.transpose(psT[:, i % 4, q * P:(q + 1) * P], src, g.ident16[:])
                        last.then_inc(turned, 1)

            def copy_out(eng, parity, copy):
                for i in range(parity, NW * R, 2):
                    eng.wait_ge(turned, i + 2)
                    dst = groups[i // R](v[:, i // R, :], i % R)[1]
                    copy(dst, psT[:, i % 4, 0:4 * P].rearrange("p (q n) -> p q n", q=4)).then_inc(copied[parity], 1)

            @block.scalar
            def _(act):
                copy_out(act, 0, lambda dst, src: act.activation(dst, src, ACT.Copy))

            @block.vector
            def _(dve):
                copy_out(dve, 1, lambda dst, src: dve.tensor_copy(dst, src))


def nf4_feed_forward(nc, g, name, zT, w1T, w2T, w3T, F):
    FT, G = F // P, 512
    GT = G // P
    with Stage(nc, name) as st:
        z_high = st.sb("z_high", [P, 2, KD, G], F32R)
        z_low = st.sb("z_low", [P, 2, KD, G], F32R)
        act_g = st.sb("act_g", [P, 2, G])
        hidden = st.sb("hidden", [P, 2, G])
        h_high = st.sb("h_high", [P, 2, G], F32R)
        h_low = st.sb("h_low", [P, 2, G], F32R)
        psG = st.ps("psG", [P, 2, 2, G])
        psO = st.ps("psO", [P, GT, D])
        z_high_ready = st.sem("z_high_ready")
        z_split = st.sem("z_split")
        gated = st.sem("gated")
        silu_done = st.sem("silu_done")
        h_ready = st.sem("h_ready")
        h_high_ready = st.sem("h_high_ready")
        h_split = st.sem("h_split")
        down = st.sem("down")
        added = st.sem("added")
        slot = lambda s, f: (s * FT + f) % 2
        of_tokens = lambda r: zT[:, :, ds(r * G, G)]

        with st.block() as block:

            @block.tensor
            def _(pe):
                def gate_up(r, s, f):
                    p = slot(s, f)
                    if f >= 2:
                        pe.wait_ge(h_ready, r * FT + f)
                    for half, w in enumerate((w1T, w2T)):
                        for k in range(KD):
                            for part in (z_high, z_low):
                                last = pe.matmul(psG[:, p, half, :], w[:, k, f * P:(f + 1) * P], part[:, s, k, :],
                                                 start=(k == 0 and part is z_high), stop=(k == KD - 1 and part is z_low))
                        last.then_inc(gated, 1)

                def multiply_down(r, s, f):
                    p = slot(s, f)
                    pe.wait_ge(h_split, r * FT + f + 2)
                    if f == 0:
                        pe.wait_ge(added, r * GT + 1)
                    for j in range(GT):
                        for part in (h_high, h_low):
                            last = pe.matmul(psO[:, j, :], part[:, p, j * P:(j + 1) * P], w3T[:, f, :],
                                             start=(f == 0 and part is h_high), stop=(f == FT - 1 and part is h_low))
                    last.then_inc(down, 1)

                with pe.Fori(0, T // G // 2) as i:
                    for s in range(2):
                        r = i * 2 + s
                        pe.wait_ge(z_split, r + 2)
                        for f in range(FT):
                            gate_up(r, s, f)
                            if f:
                                multiply_down(r, s, f - 1)
                        multiply_down(r, s, FT - 1)

            @block.scalar
            def _(act):
                def split(r, s):
                    act.activation(z_high[:, s, :, :], of_tokens(r), ACT.Copy).then_inc(z_high_ready, 1)

                with act.Fori(0, T // G // 2) as i:
                    act.wait_ge(gated, i * 4 * FT + 1)
                    split(i * 2, 0)
                    for s in range(2):
                        for f in range(FT):
                            p, n = slot(s, f), (i * 2 + s) * FT + f
                            act.wait_ge(gated, 2 * n + 2)
                            if f >= 2:
                                act.wait_ge(h_ready, n)
                            act.activation(act_g[:, p, :], psG[:, p, 0, :], ACT.Silu).then_inc(silu_done, 1)
                            act.wait_ge(h_ready, n + 2)
                            if f >= 2:
                                act.wait_ge(down, n)
                            act.activation(h_high[:, p, :], hidden[:, p, :], ACT.Copy).then_inc(h_high_ready, 1)
                            if s == 0 and f == 4:
                                split(i * 2 + 1, 1)

            @block.vector
            def _(dve):
                def split(r, s):
                    dve.wait_ge(z_high_ready, r + 2)
                    dve.tensor_tensor(z_low[:, s, :, :], of_tokens(r), z_high[:, s, :, :].bitcast(F32), ALU.subtract).then_inc(z_split, 1)

                with dve.Fori(0, T // G // 2) as i:
                    split(i * 2, 0)
                    for s in range(2):
                        r = i * 2 + s
                        for f in range(FT):
                            p, n = slot(s, f), r * FT + f
                            dve.wait_ge(gated, 2 * n + 3)
                            dve.wait_ge(silu_done, n + 2)
                            dve.tensor_tensor(hidden[:, p, :], act_g[:, p, :], psG[:, p, 1, :], ALU.mult).then_inc(h_ready, 1)
                            dve.wait_ge(h_high_ready, n + 2)
                            if f >= 2:
                                dve.wait_ge(down, n)
                            dve.tensor_tensor(h_low[:, p, :], hidden[:, p, :], h_high[:, p, :].bitcast(F32), ALU.subtract).then_inc(h_split, 1)
                            if s == 0 and f == 5:
                                split(r + 1, 1)
                        dve.wait_ge(down, (r + 1) * FT + 1)
                        for j in range(GT):
                            x_tile = g.x[:, ds(r * GT + j, 1), :].rearrange("p a n -> p (a n)")
                            dve.tensor_tensor(x_tile, x_tile, psO[:, j, :], ALU.add).then_inc(added, 1)



class Globals:
    pass


def program(nc, a, out, stages=None):
    g = Globals()
    with ExitStack() as ctx:
        def sb(name, shape, dt=F32):
            return ctx.enter_context(nc.sbuf_tensor(name, shape, dt))

        g.x = sb("x_sb", [P, NT, D])
        g.mean, g.rstd, g.shift, g.ln_rstd = (sb(n, [P, NT]) for n in ("mean", "rstd", "shift", "ln_rstd"))
        g.weight_of = sb("weight_of", [P, NT, 8])
        g.slot_of = sb("slot_of", [P, NT, 8])
        g.ident, g.ones, g.earlier = (sb(n, [P, P]) for n in ("ident", "ones", "earlier"))
        g.ident16 = sb("ident16", [P, P], BF16)
        g.zeros_i = sb("zeros_i", [P, 144], I32)
        g.z_rows = nc.dram_tensor("z_rows", (T, D), F32).ap()
        g.slot_token = nc.dram_tensor("slot_token", (32 * 512 + 16 * P, 1), I32).ap()
        g.slot_rows = nc.dram_tensor("slot_rows", (32 * 512, D), F32).ap()
        g.nf4_values = nc.dram_tensor("nf4_values", a["L3_ffn"]["weights"].shape, BF16).ap()
        g.pool_sem = lambda name: ctx.enter_context(nc.semaphore(name))
        g.ctxT = a["ctxT"]
        x_rows = a["x"].rearrange("(t p) n -> p t n", p=P)
        out_rows = out.rearrange("(t p) n -> p t n", p=P)

        with Stage(nc, "start") as st:
            x_in = st.sem("x_in")
            made = st.sem("made")
            with st.block() as block:

                @block.sync
                def _(sp):
                    sp.dma_start(g.x[:], x_rows).then_inc(x_in, 16)
                    sp.wait_ge(x_in, 17)

                @block.gpsimd
                def _(pool):
                    pool.memset(g.ident[:], 0.0).then_inc(made, 1)
                    pool.memset(g.ones[:], 1.0).then_inc(made, 1)
                    pool.memset(g.zeros_i[:], 0).then_inc(made, 1)
                    pool.wait_ge(made, 4)
                    pool.affine_select(out=g.ident[:], in_=g.ident[:], compare_op=ALU.not_equal, fill=1.0, base=0,
                                       pattern=[[-1, P]], channel_multiplier=1).then_inc(made, 1)
                    pool.affine_select(out=g.earlier[:], in_=g.ones[:], compare_op=ALU.is_gt, fill=0.0, base=0,
                                       pattern=[[1, P]], channel_multiplier=-1).then_inc(made, 1)
                    pool.wait_ge(made, 5)
                    pool.tensor_copy(g.ident16[:], g.ident[:])

        run = stages or range(8)
        if 0 in run:
            mixer(nc, g, "m0", a["L0_xattn"])
        if 1 in run:
            w = a["L0_ffn"]
            with nc.sbuf_tensor("zT1", [P, KD, T], F32) as zT:
                layer_norm(nc, g, "n1", zT=zT, rms_weight=w["norm_w"], z_dram=g.z_rows,
                           router=Router(nc, g, 32, 4, 512, w["gateT"], True, 0.0))
                experts_wide(nc, g, "e1", 32, 512, 256, w["w13"], w["w2"])
                combine_and_shared_expert(nc, g, "s1", 32 * 512, 4, zT, 256, w["shared_gate_w"], w["shared_up_w"], w["shared_down_w"])
        if 2 in run:
            mixer(nc, g, "m2", a["L1_xattn"])
        if 3 in run:
            w = a["L1_ffn"]
            with nc.sbuf_tensor("zT3", [P, KD, T], F32) as zT:
                layer_norm(nc, g, "n3", zT=zT, router=SoftRouter(g, 8, 6, w["gate"], w["bg"]))
                soft_experts(nc, g, "e3", zT, 6, 256, w["Wgate"], w["bgate"], w["Wup"], w["bup"], w["Wdown"], w["bdown"],
                             w["Ws_up"], w["bs_up"], w["Ws_down"], w["bs_down"],
                             Nf4(nc, g, a["L3_ffn"]["weights"], g.nf4_values))
        if 4 in run:
            w = a["L2_xattn"]
            with nc.sbuf_tensor("zT4", [P, KD, T], F32) as zT:
                layer_norm(nc, g, "n4", zT=zT)
                feature_attention(nc, g, "a4", zT, w["WqT"], w["bq"], w["WkT"], w["bk"])
        if 5 in run:
            w = a["L2_ffn"]
            with nc.sbuf_tensor("zT5", [P, KD, T], F32) as zT:
                layer_norm(nc, g, "n5", zT=zT, z_dram=g.z_rows, router=Router(nc, g, 64, 8, 128, w["gateT"], False, 1e-20))
            experts_narrow(nc, g, "e5", 64, 128, 192, w["w_gate"], w["w_up"], w["w_down"])
            combine(nc, g, "c5", 64 * 128, 8)
        if 6 in run:
            w = a["L3_xattn"]
            with nc.sbuf_tensor("zT6", [P, KD, T], F32) as zT:
                layer_norm(nc, g, "n6", zT=zT)
                cross_attention(nc, g, "a6", zT, channels_first(w["Wq"]), channels_first(w["Wk"]), channels_first(w["Wv"]),
                                w["Wo"], w["gq"], w["gk"])
        if 7 in run:
            w = a["L3_ffn"]
            F = 1408
            RF = F // P
            with (nc.sbuf_tensor("w1T", [P, KD, F], F32R) as w1T, nc.sbuf_tensor("w2T", [P, KD, F], F32R) as w2T,
                  nc.sbuf_tensor("w3T", [P, RF, D], F32R) as w3T):
                def rows_of_hidden(wT):
                    return lambda v, r: ([v[:, r * D + k * P:r * D + (k + 1) * P] for k in range(KD)], wT[:, :, r * P:(r + 1) * P])

                def rows_of_channels(v, r):
                    return ([v[:, c * F:(c + 1) * F].rearrange("p (n r) -> p r n", r=RF)[:, r, :] for c in range(4)],
                            w3T[:, r, :].rearrange("p (n c) -> p c n", c=4))

                turn_weights(nc, g, "q7", g.nf4_values, [rows_of_hidden(w1T), rows_of_hidden(w2T), rows_of_channels])
                with nc.sbuf_tensor("zT7", [P, KD, T], F32) as zT:
                    layer_norm(nc, g, "n7", zT=zT)
                    nf4_feed_forward(nc, g, "f7", zT, w1T, w2T, w3T, F)

        with Stage(nc, "end") as st:
            x_out = st.sem("x_out")
            with st.block() as block:

                @block.sync
                def _(sp):
                    sp.dma_start(out_rows, g.x[:]).then_inc(x_out, 16)
                    sp.wait_ge(x_out, 17)



def laid_out(inputs):
    import numpy as np
    a = {k: np.asarray(v) for k, v in inputs.items()}

    def tiles(w, rows):
        return w.reshape(-1, rows, w.shape[-1]).transpose(1, 0, 2)

    out = {"x": a["x"].reshape(T, D), "ctxT": tiles(a["ctx_1024"].reshape(T, DC).T, P)}
    for n in ("L0_xattn", "L1_xattn"):
        cols = [a[f"{n}_conv_w"].reshape(D, 4), a[f"{n}_conv_b"][:, None], a[f"{n}_dt_proj_b"][:, None],
                a[f"{n}_D"][:, None], a[f"{n}_A_log"]]
        out[f"{n}/in_projT"] = tiles(a[f"{n}_in_proj_w"].T, P)
        out[f"{n}/x_projT"] = tiles(a[f"{n}_x_proj_w"].T, P)
        out[f"{n}/dt_projT"] = a[f"{n}_dt_proj_w"].T
        out[f"{n}/cols"] = tiles(np.concatenate(cols, axis=1), P)
    for n in ("norm_w", "w13", "w2", "shared_gate_w", "shared_up_w", "shared_down_w"):
        out[f"L0_ffn/{n}"] = a[f"L0_ffn_{n}"]
    out["L0_ffn/gateT"] = tiles(a["L0_ffn_gate_w"].T, P)
    for n in ("bg", "Wgate", "Wup", "Wdown", "bdown", "Ws_up", "Ws_down", "bs_down"):
        out[f"L1_ffn/{n}"] = a[f"L1_ffn_{n}"]
    out["L1_ffn/gate"] = tiles(a["L1_ffn_Wg"], P)
    for n in ("bgate", "bup"):
        out[f"L1_ffn/{n}"] = a[f"L1_ffn_{n}"].reshape(6, 2, P).transpose(2, 0, 1)
    out["L1_ffn/bs_up"] = a["L1_ffn_bs_up"].reshape(4, P).T
    for n in ("Wq", "Wk"):
        out[f"L2_xattn/{n}T"] = tiles(a[f"L2_xattn_{n}"].T, P)
    for n in ("bq", "bk"):
        out[f"L2_xattn/{n}"] = a[f"L2_xattn_{n}"]
    out["L2_ffn/gateT"] = tiles(a["L2_ffn_router_w"].T, P)
    for n in ("w_gate", "w_up", "w_down"):
        out[f"L2_ffn/{n}"] = a[f"L2_ffn_{n}"]
    for n in ("Wq", "Wk", "Wv", "Wo", "gq", "gk"):
        out[f"L3_xattn/{n}"] = a[f"L3_xattn_{n}"]
    out["L3_ffn/weights"] = np.stack([a[f"L3_ffn_weight{n}"].reshape(P, -1) for n in (1, 2, 3)])
    return {k: np.ascontiguousarray(v) for k, v in out.items()}


def kernel(**inputs):
    import concourse.bacc as _bacc
    from concourse.bass_utils import run_bass_kernel_spmd as _run

    nc = _bacc.Bacc("TRN2", target_bir_lowering=False, num_devices=1)
    arrays, args = {}, {}
    for key, v in laid_out(inputs).items():
        dram = "in_" + key.replace("/", "_")
        arrays[dram] = v
        ap = nc.dram_tensor(dram, v.shape, mybir.dt.from_np(v.dtype), kind="ExternalInput").ap()
        group, _, leaf = key.partition("/")
        if leaf:
            args.setdefault(group, {})[leaf] = ap
        else:
            args[group] = ap
    out = nc.dram_tensor("out", (T, D), F32, kind="ExternalOutput").ap()
    program(nc, args, out)
    r = _run(nc, [arrays], core_ids=[0])
    return r.results[0]["out"].reshape(B, L, D)
```
